# Optimizing a Trainium2 kernel written in Bass

```python
import numpy as np
import jax
import jax.numpy as jnp

def _softmax(x, axis=-1):
    return jax.nn.softmax(x, axis=axis)
def _gelu(x):
    return jax.nn.gelu(x, approximate=True)
def _silu(x):
    return jax.nn.silu(x)
def _sigmoid(x):
    return jax.nn.sigmoid(x)
def _layernorm(x, axis=-1, eps=1e-5):
    m = jnp.mean(x, axis=axis, keepdims=True)
    v = jnp.var(x, axis=axis, keepdims=True)
    return (x - m) / jnp.sqrt(v + eps)
def _scatter_add(tgt, idx, src, axis=0):
    return tgt.at[idx].add(src)
def _segment_sum(src, seg, n):
    return jax.ops.segment_sum(src, seg, n)

kernel_name = 'mk_adj_resnorm_d4_adj_64_f8b590'

def setup_inputs(seed: int = 0):
    np.random.seed(seed)
    _w = jnp.asarray
    def _rec_inputs():
        import jax
        import jax.numpy as jnp
        _gk = jax.random.key(seed)
        x = -0.000929 + 1 * jax.random.normal(jax.random.fold_in(_gk, 1), (4096, 64), jnp.float32)
        _w = (1.0 + jnp.arange(4096, dtype=jnp.float32)) ** -0.5
        _w = _w / _w.mean()
        _pij = jnp.clip(0.000976562 * _w[:, None] * _w[None, :], 0.0, 1.0)
        _a = jax.random.uniform(jax.random.fold_in(_gk, 2), (4096, 4096)) < _pij
        _af = _a.astype(jnp.float32)
        adj = _af
        return x, adj
    x, adj = _rec_inputs()
    def _L0_gnn_setup():
        import jax, jax.numpy as jnp
        import numpy as np
        N = 16384
        D_IN = 64
        D_OUT = 64
        EDGE_P = 0.002
        key = jax.random.key(seed)
        kx, ka, kw = jax.random.split(key, 3)
        X = jax.random.normal(kx, (N, D_IN), dtype=jnp.float32)
        adj = (jax.random.uniform(ka, (N, N)) < EDGE_P).astype(jnp.float32)
        W = jax.random.normal(kw, (D_OUT, 2 * D_IN), dtype=jnp.float32) * (1.0 / np.sqrt(2 * D_IN))
        return {'X': X, 'adj': adj, 'W': W}
    _L0_gnn_all = _L0_gnn_setup()
    _L0_gnn_in = {k: v for k, v in _L0_gnn_all.items() if k in ('W', )}
    del _L0_gnn_all

    def _L1_gnn_setup():
        import jax, jax.numpy as jnp
        import numpy as np
        N = 4096
        D = 64
        NUM_LAYERS = 2
        THETA0 = 0.000244
        THETA_MAX = 0.0003
        LAM = 0.1
        TAU = 1.0
        EPS = 1e-06
        H_DENSITY = 0.005

        def _safe_norm(x, axis):
            return jnp.sqrt(jnp.maximum(jnp.sum(x * x, axis=axis), 1e-16))

        def _layer(x, H, W, Theta, Wq, bq, Wv, bv, iteration):
            scale = D ** (-0.5)
            theta_base = THETA0 + (1.0 - np.exp(-LAM * iteration)) * (THETA_MAX - THETA0)
            th_comp = theta_base
            th_edge = min(theta_base, 0.8)
            th_node = min(theta_base, 0.7)
            structural = _safe_norm(x @ W, axis=1)
            Q = x @ Wq + bq
            V = x @ Wv + bv
            edge_feat = H.T @ V
            att = Q @ edge_feat.T * scale * H
            att = jax.nn.softmax(att, axis=1)
            att_scores = att.mean(axis=0)
            importance = 0.5 * structural + 0.5 * att_scores
            comp_scores = jax.nn.softmax(importance / TAU)
            comp_mask = comp_scores >= th_comp
            x_comp = x * comp_mask[:, None]
            nrm = jnp.maximum(_safe_norm(x_comp, axis=1), 1e-08)
            xn = x_comp / nrm[:, None]
            cos = xn @ xn.T
            edge_scores = jax.nn.softmax(cos * H / TAU, axis=1)
            edge_mask = (edge_scores >= th_edge) & comp_mask[:, None]
            H_pruned = H * edge_mask
            connectivity = H_pruned.sum(axis=1)
            feat_mag = _safe_norm(x_comp, axis=1)
            node_scores = jax.nn.softmax(connectivity * feat_mag / TAU)
            connected = (H_pruned * edge_mask).sum(axis=1) > 0
            node_mask = (node_scores >= th_node) & connected
            x_final = x_comp * node_mask[:, None]
            vdeg = jnp.maximum(H_pruned.sum(axis=1), EPS)
            edeg = jnp.maximum(H_pruned.sum(axis=0), EPS)
            dv_isqrt = 1.0 / jnp.sqrt(vdeg)
            de_inv = 1.0 / edeg
            transformed = x_final @ W
            agg = H_pruned.T * dv_isqrt[None, :] @ transformed
            agg = agg * de_inv[:, None]
            msg = dv_isqrt[:, None] * (H_pruned @ agg)
            msg = msg @ Theta
            return jax.nn.relu(msg)
        key = jax.random.key(seed)
        ks = jax.random.split(key, 8)
        xav = 0.125
        X = jax.random.normal(ks[0], (N, D), jnp.float32) * 0.05
        W = jax.random.normal(ks[1], (D, D), jnp.float32) * xav
        Theta = jax.random.normal(ks[2], (D, D), jnp.float32) * xav
        Wq = jax.random.normal(ks[3], (D, D), jnp.float32) * xav
        bq = jnp.zeros((D,), jnp.float32)
        Wv = jax.random.normal(ks[4], (D, D), jnp.float32) * xav
        bv = jnp.zeros((D,), jnp.float32)
        H = (jax.random.uniform(ks[7], (N, N)) < H_DENSITY).astype(jnp.float32)
        return {'X': X, 'W': W, 'Theta': Theta, 'Wq': Wq, 'bq': bq, 'Wv': Wv, 'bv': bv, 'H': H}
    _L1_gnn_all = _L1_gnn_setup()
    _L1_gnn_in = {k: v for k, v in _L1_gnn_all.items() if k in ('W', 'Theta', 'Wq', 'bq', 'Wv', 'bv', )}
    del _L1_gnn_all

    def _L2_gnn_setup():
        import jax, jax.numpy as jnp
        import numpy as np
        N = 16384
        NFEAT = 64
        NHID = 64
        key = jax.random.key(seed)
        k1, k2, k3, k4 = jax.random.split(key, 4)
        x = jax.random.normal(k1, (N, NFEAT), dtype=jnp.float32)
        adj_matrix = jax.random.uniform(k2, (N, N), dtype=jnp.float32)
        degree_norm = jax.random.uniform(k3, (N, 1), dtype=jnp.float32)
        W = jax.random.normal(k4, (NFEAT, NHID), dtype=jnp.float32) / np.sqrt(NFEAT)
        b = jnp.zeros((NHID,), dtype=jnp.float32)
        return {'x': x, 'adj_matrix': adj_matrix, 'degree_norm': degree_norm, 'W': W, 'b': b}
    _L2_gnn_all = _L2_gnn_setup()
    _L2_gnn_in = {k: v for k, v in _L2_gnn_all.items() if k in ('W', 'b', )}
    del _L2_gnn_all

    def _L3_gnn_setup():
        import jax, jax.numpy as jnp
        import numpy as np
        N, D_IN, D_OUT = (8192, 64, 64)
        MAX_NEIGH = 100
        DECAY = 0.5
        key = jax.random.key(seed)
        k1, k2, k3, k4 = jax.random.split(key, 4)
        stdv = 1.0 / np.sqrt(D_OUT)
        inputs = {'input': jax.random.normal(k1, (N, D_IN), dtype=jnp.float32), 'adj': jax.random.randint(k2, (N, N), 0, 2).astype(jnp.float32), 'weight': jax.random.uniform(k3, (D_IN, D_OUT), minval=-stdv, maxval=stdv, dtype=jnp.float32), 'bias': jax.random.uniform(k4, (D_OUT,), minval=-stdv, maxval=stdv, dtype=jnp.float32)}
        return inputs
    _L3_gnn_all = _L3_gnn_setup()
    _L3_gnn_in = {k: v for k, v in _L3_gnn_all.items() if k in ('weight', 'bias', )}
    del _L3_gnn_all

    return {
        "x": x,
        "adj": adj,
        "L0_gnn_W": _L0_gnn_in["W"],
        "L1_gnn_W": _L1_gnn_in["W"],
        "L1_gnn_Theta": _L1_gnn_in["Theta"],
        "L1_gnn_Wq": _L1_gnn_in["Wq"],
        "L1_gnn_bq": _L1_gnn_in["bq"],
        "L1_gnn_Wv": _L1_gnn_in["Wv"],
        "L1_gnn_bv": _L1_gnn_in["bv"],
        "L2_gnn_W": _L2_gnn_in["W"],
        "L2_gnn_b": _L2_gnn_in["b"],
        "L3_gnn_weight": _L3_gnn_in["weight"],
        "L3_gnn_bias": _L3_gnn_in["bias"],
    }

def reference(x, adj, L0_gnn_W, L1_gnn_W, L1_gnn_Theta, L1_gnn_Wq, L1_gnn_bq, L1_gnn_Wv, L1_gnn_bv, L2_gnn_W, L2_gnn_b, L3_gnn_weight, L3_gnn_bias):
    import jax
    import jax.numpy as jnp
    def _L0_gnn_ref(X, adj, W):
        import jax, jax.numpy as jnp
        import numpy as np
        N = 16384
        D_IN = 64
        D_OUT = 64
        EDGE_P = 0.002
        deg = jnp.sum(adj, axis=1, keepdims=True)
        nb_agg = adj @ X / jnp.maximum(deg, 1.0)
        X_cat = jnp.concatenate([X, nb_agg], axis=1)
        out = X_cat @ W.T
        return jax.nn.relu(out)

    def _L1_gnn_ref(X, W, Theta, Wq, bq, Wv, bv, H):
        import jax, jax.numpy as jnp
        import numpy as np
        N = 4096
        D = 64
        NUM_LAYERS = 2
        THETA0 = 0.000244
        THETA_MAX = 0.0003
        LAM = 0.1
        TAU = 1.0
        EPS = 1e-06
        H_DENSITY = 0.005

        def _safe_norm(x, axis):
            return jnp.sqrt(jnp.maximum(jnp.sum(x * x, axis=axis), 1e-16))

        def _layer(x, H, W, Theta, Wq, bq, Wv, bv, iteration):
            scale = D ** (-0.5)
            theta_base = THETA0 + (1.0 - np.exp(-LAM * iteration)) * (THETA_MAX - THETA0)
            th_comp = theta_base
            th_edge = min(theta_base, 0.8)
            th_node = min(theta_base, 0.7)
            structural = _safe_norm(x @ W, axis=1)
            Q = x @ Wq + bq
            V = x @ Wv + bv
            edge_feat = H.T @ V
            att = Q @ edge_feat.T * scale * H
            att = jax.nn.softmax(att, axis=1)
            att_scores = att.mean(axis=0)
            importance = 0.5 * structural + 0.5 * att_scores
            comp_scores = jax.nn.softmax(importance / TAU)
            comp_mask = comp_scores >= th_comp
            x_comp = x * comp_mask[:, None]
            nrm = jnp.maximum(_safe_norm(x_comp, axis=1), 1e-08)
            xn = x_comp / nrm[:, None]
            cos = xn @ xn.T
            edge_scores = jax.nn.softmax(cos * H / TAU, axis=1)
            edge_mask = (edge_scores >= th_edge) & comp_mask[:, None]
            H_pruned = H * edge_mask
            connectivity = H_pruned.sum(axis=1)
            feat_mag = _safe_norm(x_comp, axis=1)
            node_scores = jax.nn.softmax(connectivity * feat_mag / TAU)
            connected = (H_pruned * edge_mask).sum(axis=1) > 0
            node_mask = (node_scores >= th_node) & connected
            x_final = x_comp * node_mask[:, None]
            vdeg = jnp.maximum(H_pruned.sum(axis=1), EPS)
            edeg = jnp.maximum(H_pruned.sum(axis=0), EPS)
            dv_isqrt = 1.0 / jnp.sqrt(vdeg)
            de_inv = 1.0 / edeg
            transformed = x_final @ W
            agg = H_pruned.T * dv_isqrt[None, :] @ transformed
            agg = agg * de_inv[:, None]
            msg = dv_isqrt[:, None] * (H_pruned @ agg)
            msg = msg @ Theta
            return jax.nn.relu(msg)
        x = X
        for it in range(NUM_LAYERS):
            x = _layer(x, H, W, Theta, Wq, bq, Wv, bv, it)
        return x

    def _L2_gnn_ref(x, adj_matrix, degree_norm, W, b):
        import jax, jax.numpy as jnp
        import numpy as np
        N = 16384
        NFEAT = 64
        NHID = 64
        neighbor_sum = adj_matrix @ x
        sub = x - degree_norm * neighbor_sum
        h = sub @ W + b
        return jax.nn.relu(h)

    def _L3_gnn_ref(input, adj, weight, bias):
        import jax, jax.numpy as jnp
        import numpy as np
        N, D_IN, D_OUT = (8192, 64, 64)
        MAX_NEIGH = 100
        DECAY = 0.5
        support = input @ weight
        mask = (adj != 0).astype(support.dtype)
        rank = jnp.cumsum(mask, axis=1)
        deg = rank[:, -1:]
        k = jnp.minimum(deg, float(MAX_NEIGH))
        pos = rank - (deg - k)
        w = mask * jnp.where(pos > 0, DECAY ** (k - pos), 0.0)
        out = w @ support + bias
        return out

    deg = jnp.maximum((adj != 0).astype(jnp.float32).sum(-1), 1.0)
    deg = deg ** -0.5
    x = _layernorm(x + _L0_gnn_ref(x, adj, L0_gnn_W), axis=-1)
    x = _layernorm(x + _L1_gnn_ref(x, L1_gnn_W, L1_gnn_Theta, L1_gnn_Wq, L1_gnn_bq, L1_gnn_Wv, L1_gnn_bv, adj), axis=-1)
    x = _layernorm(x + _L2_gnn_ref(x, adj, deg[..., None], L2_gnn_W, L2_gnn_b), axis=-1)
    x = _layernorm(x + _L3_gnn_ref(x, adj, L3_gnn_weight, L3_gnn_bias), axis=-1)
    return x


_drawn_inputs = setup_inputs


def setup_inputs(seed=0):
    import zlib

    import numpy as np

    out = dict(_drawn_inputs(seed))
    spreads = {'L1_gnn_bq': (0.0, 0.1), 'L1_gnn_bv': (0.0, 0.1), 'L2_gnn_b': (0.0, 0.1)}
    factors = {'L1_gnn_W': 8.0, 'L1_gnn_Theta': 8.0}
    for name, (base, spread) in spreads.items():
        noise = np.random.default_rng([zlib.crc32(name.encode()), seed]).standard_normal(out[name].shape)
        drawn = base * np.exp(spread * noise) if base else spread * noise
        out[name] = jnp.asarray(drawn.astype(out[name].dtype))
    for name, factor in factors.items():
        out[name] = (out[name] * factor).astype(out[name].dtype)
    return out
```

```python
import numpy as np
from contextlib import ExitStack

import concourse.bass as bass
from concourse import mybir

DT = mybir.dt
F32, BF16, F16, U8, U16, I16, FP8 = (DT.float32, DT.bfloat16, DT.float16, DT.uint8, DT.uint16,
                                     DT.int16, DT.float8e4)
ALU = mybir.AluOpType
ACT = mybir.ActivationFunctionType
AX = mybir.AxisListType
RED = bass.bass_isa.ReduceOp

P = 128
N = 4096
D = 64
T = N // P
NB = T // 2
HALF = N // 2
BYTE = 64.0
FP8_ONE = 2.0
INV = 1.0 / FP8_ONE
VC = 200
PANEL = 512
PT = PANEL // P
NPANEL = N // PANEL
LN_EPS = 1e-5
SAFE = 1e-16
EDGE_EPS = 1e-6
COS_SCALE = 64.0
X_SCALE = 256.0
MASK_OFF = float(2 ** 19)
BF16_STEP = 128.0
W_UP = float(2 ** 27)
KEEP = 128.0
MAX_NEIGH = 100
THETA0, THETA_MAX, LAM = 0.000244, 0.0003, 0.1


def psum(nc, ctx, name, shape, dt):
    return ctx.enter_context(nc.psum_tensor(name, shape, dt))


def sbuf(nc, ctx, name, shape, dt):
    return ctx.enter_context(nc.sbuf_tensor(name, shape, dt))


class Chain:

    def __init__(self, eng, g):
        self.eng, self.g = eng, g

    def __call__(self, instruction):
        instruction.then_inc(self.g.vector_step, 1)
        self.g.vector_steps += 1
        self.eng.wait_ge(self.g.vector_step, self.g.vector_steps)


def per_node(a, width=D):
    return a.unsqueeze(2).broadcast_to([P, T, width])


def split3(v, step, dst, slots, src, rest):
    hi, mid, lo = (dst[:, :, s * D:(s + 1) * D] for s in slots)
    step(v.tensor_copy(hi, src))
    step(v.tensor_tensor(rest, src, hi, ALU.subtract))
    step(v.tensor_copy(mid, rest))
    step(v.tensor_tensor(lo, rest, mid, ALU.subtract))


def split2(v, step, dst, src, scaled, scale):
    hi, lo = dst[:, :, 0:D], dst[:, :, D:2 * D]
    step(v.tensor_scalar(scaled, src, scale, None, ALU.mult))
    step(v.tensor_copy(hi, scaled))
    step(v.tensor_tensor(lo, scaled, hi, ALU.subtract))


def layernorm(nc, g, name, add):
    with ExitStack() as ctx:
        row = sbuf(nc, ctx, f"{name}_row", [P, T], F32)
        mean = sbuf(nc, ctx, f"{name}_mean", [P, T], F32)
        var = sbuf(nc, ctx, f"{name}_var", [P, T], F32)
        std = sbuf(nc, ctx, f"{name}_std", [P, T], F32)
        square = sbuf(nc, ctx, f"{name}_square", [P, T, D], F32)
        var_ready, std_ready = (g.sem(f"{name}_{s}") for s in ("var_ready", "std_ready"))
        with nc.Block() as block:
            @block.vector
            def _(dve):
                v = nc.vector
                step = Chain(dve, g)
                if add is not None:
                    step(v.tensor_tensor(g.x[:], g.x[:], add, ALU.add))
                step(v.tensor_reduce(row[:], g.x[:], AX.X, ALU.add))
                step(v.tensor_scalar(mean[:], row[:], 1.0 / D, None, ALU.mult))
                step(v.tensor_tensor(g.x[:], g.x[:], per_node(mean[:]), ALU.subtract))
                step(v.tensor_tensor(square[:], g.x[:], g.x[:], ALU.mult))
                step(v.tensor_reduce(row[:], square[:], AX.X, ALU.add))
                v.tensor_scalar(var[:], row[:], 1.0 / D, LN_EPS, ALU.mult, ALU.add).then_inc(var_ready, 1)
                dve.wait_ge(std_ready, 1)
                step(v.reciprocal(var[:], std[:]))
                step(v.tensor_tensor(g.x[:], g.x[:], per_node(var[:]), ALU.mult))

            @block.scalar
            def _(act):
                act.wait_ge(var_ready, 1)
                nc.scalar.activation(std[:], var[:], ACT.Sqrt).then_inc(std_ready, 1)


def linear(nc, g, name, src, k, weights, n, dst, relu=False, ones_row=False):
    kk = k + 1 if ones_row else k
    G = 4
    NG = T // G
    with ExitStack() as ctx:
        turned = sbuf(nc, ctx, f"{name}_turned", [kk, 2, G * P], F32)
        flipped = [psum(nc, ctx, f"{name}_flipped{i}", [P, G * P], F32) for i in range(2)]
        out = [psum(nc, ctx, f"{name}_out{i}", [P, G, 256], F32) for i in range(2)]
        flip_ready, turned_ready, out_ready, out_read, ones_ready = (
            g.sem(f"{name}_{s}") for s in ("flip_ready", "turned_ready", "out_ready", "out_read", "ones_ready"))
        with nc.Block() as block:
            @block.tensor
            def _(pe):
                def flips(i):
                    if i >= 2:
                        pe.wait_ge(turned_ready, i - 1)
                    for q in range(G):
                        last = nc.tensor.transpose(flipped[i % 2][0:k, q * P:(q + 1) * P],
                                                   src[:, i * G + q, 0:k], g.ident_f[:])
                    last.then_inc(flip_ready, 1)

                def products(i):
                    pe.wait_ge(turned_ready, i + 1)
                    if i == 0 and ones_row:
                        pe.wait_ge(ones_ready, 1)
                    if i >= 2:
                        pe.wait_ge(out_read, i - 1)
                    for q in range(G):
                        last = nc.tensor.matmul(out[i % 2][:, q, 0:n], turned[0:kk, i % 2, q * P:(q + 1) * P],
                                                weights, start=True, stop=True)
                    last.then_inc(out_ready, 1)

                flips(0)
                for i in range(NG):
                    if i + 1 < NG:
                        flips(i + 1)
                    products(i)

            @block.scalar
            def _(act):
                for i in range(NG):
                    act.wait_ge(flip_ready, i + 1)
                    if i >= 2:
                        act.wait_ge(out_ready, i - 1)
                    nc.scalar.copy(turned[0:k, i % 2, :], flipped[i % 2][0:k, :]).then_inc(turned_ready, 1)

            @block.vector
            def _(dve):
                if ones_row:
                    nc.vector.memset(turned[k:kk, :, :], 1.0).then_inc(ones_ready, 1)
                for i in range(NG):
                    dve.wait_ge(out_ready, i + 1)
                    to, frm = dst[:, i * G:(i + 1) * G, 0:n], out[i % 2][:, :, 0:n]
                    if relu:
                        nc.vector.tensor_scalar(to, frm, 0.0, None, ALU.max).then_inc(out_read, 1)
                    else:
                        nc.vector.tensor_copy(to, frm).then_inc(out_read, 1)


def build_stacks(nc, g, name, jobs, dt, ident):
    G = 8
    groups = [(src, dst, natural, t0) for src, dst, natural in jobs for t0 in range(0, T, G)]
    with ExitStack() as ctx:
        bank = [psum(nc, ctx, f"{name}_bank{i}", [P, G, P], dt) for i in range(8)]
        flipped, by_dve, by_act = (g.sem(f"{name}_{s}") for s in ("flipped", "by_dve", "by_act"))

        def place(i):
            _, dst, natural, t0 = groups[i]
            to = dst[:, t0 * P:(t0 + G) * P]
            if natural:
                return to.rearrange("k (b p e) -> k b e p", p=P, e=2), \
                    bank[i % 8][:].rearrange("k (b e) p -> k b e p", e=2)
            return to.rearrange("k (t p) -> k t p", p=P), bank[i % 8][:]

        with nc.Block() as block:
            @block.tensor
            def _(pe):
                for i, (src, _, _, t0) in enumerate(groups):
                    if i >= 8:
                        pe.wait_ge(by_act if i % 2 else by_dve, (i - 8) // 2 + 1)
                    for q in range(G):
                        last = nc.tensor.transpose(bank[i % 8][:, q, :], src(t0 + q), ident)
                    last.then_inc(flipped, 1)

            @block.vector
            def _(dve):
                for i in range(0, len(groups), 2):
                    dve.wait_ge(flipped, i + 1)
                    nc.vector.tensor_copy(*place(i)).then_inc(by_dve, 1)

            @block.scalar
            def _(act):
                for i in range(1, len(groups), 2):
                    act.wait_ge(flipped, i + 1)
                    nc.scalar.copy(*place(i)).then_inc(by_act, 1)


def softmax_keep(nc, g, name, logits, theta, keep):
    with ExitStack() as ctx:
        part = sbuf(nc, ctx, f"{name}_part", [P, 4], F32)
        whole = sbuf(nc, ctx, f"{name}_whole", [P, 4], F32)
        e = sbuf(nc, ctx, f"{name}_e", [P, T], F32)
        part_ready, whole_ready, neg_ready, e_ready = (
            g.sem(f"{name}_{s}") for s in ("part_ready", "whole_ready", "neg_ready", "e_ready"))
        with nc.Block() as block:
            @block.vector
            def _(dve):
                v, step = nc.vector, Chain(dve, g)
                v.tensor_reduce(part[:, 0:1], logits, AX.X, ALU.max).then_inc(part_ready, 1)
                dve.wait_ge(whole_ready, 1)
                v.tensor_scalar(whole[:, 1:2], whole[:, 0:1], -1.0, None, ALU.mult).then_inc(neg_ready, 1)
                dve.wait_ge(whole_ready, 2)
                step(v.reciprocal(part[:, 2:3], whole[:, 2:3]))
                step(v.tensor_scalar(keep, e[:], part[:, 2:3], theta, ALU.mult, ALU.is_ge))

            @block.scalar
            def _(act):
                act.wait_ge(neg_ready, 1)
                nc.scalar.activation(e[:], logits, ACT.Exp, bias=whole[:, 1:2],
                                     accum_out=part[:, 1:2]).then_inc(e_ready, 1)

            @block.gpsimd
            def _(pool):
                pool.wait_ge(part_ready, 1)
                nc.gpsimd.partition_all_reduce(whole[:, 0:1], part[:, 0:1], P, RED.max).then_inc(whole_ready, 1)
                pool.wait_ge(e_ready, 1)
                nc.gpsimd.partition_all_reduce(whole[:, 2:3], part[:, 1:2], P, RED.add).then_inc(whole_ready, 1)


def row_product(nc, g, name, rows, cols, parts, out, sums=None):
    HT = T // 2
    with ExitStack() as ctx:
        panel = [sbuf(nc, ctx, f"{name}_panel{i}", [P, HT, PANEL], U8) for i in range(4)]
        acc = [psum(nc, ctx, f"{name}_acc{i}", [P, PT, 512], F32) for i in range(2)]
        loaded = [g.sem(f"{name}_loaded{i}") for i in range(4)]
        half_used, acc_read = (g.sem(f"{name}_{s}") for s in ("half_used", "acc_read"))
        by_panel = rows.rearrange("t p (n j) -> n p t j", j=PANEL)
        rounds = NPANEL // 2
        with nc.Block() as block:
            @block.sync
            def _(sp):
                def load(r, i):
                    half = i % 2
                    nc.sync.dma_start(panel[i][:], by_panel[bass.ds(r * 2 + i // 2, 1), :,
                                                            half * HT:(half + 1) * HT, :]
                                      .rearrange("n p t j -> (n p) t j")).then_inc(loaded[i], 16)
                for i in range(4):
                    load(0, i)
                with sp.Fori(1, rounds) as r:
                    for i in range(4):
                        sp.wait_ge(half_used, r * 4 + (i - 3))
                        g.carry(sp)
                        load(r, i)

            @block.tensor
            def _(pe):
                def round_(r, first):
                    for i in range(4):
                        a, half = acc[i // 2], i % 2
                        pe.wait_ge(loaded[i], (r + 1) * 16)
                        if half == 0 and not first:
                            pe.wait_ge(acc_read, r * 2 + (i // 2 - 1))
                        g.carry(pe)
                        for t in range(HT):
                            tt = half * HT + t
                            for q in range(PT):
                                b, e = divmod(q, 2)
                                lhs = panel[i][:, t, 256 * b + e:256 * b + 256:2].bitcast(FP8)
                                last = nc.tensor.matmul(a[:, q, 0:cols], lhs, g.vs[:, tt, 0:cols],
                                                        start=(tt == 0), stop=(tt == T - 1))
                        last.then_inc(half_used, 1)
                round_(0, True)
                with pe.Fori(1, rounds) as r:
                    round_(r, False)

            @block.vector
            def _(dve):
                with dve.Fori(0, rounds) as r:
                    for k in range(2):
                        dve.wait_ge(half_used, r * 4 + (2 * k + 2))
                        tiles = bass.ds((r * 2 + k) * PT, PT)
                        if sums is not None:
                            nc.vector.tensor_scalar(sums[:, tiles], acc[k][:, :, parts * D], INV, None, ALU.mult)
                        nc.vector.tensor_reduce(out[:, tiles, :], acc[k][:, :, 0:parts * D]
                                                .rearrange("p q (s d) -> p q d s", s=parts),
                                                AX.X, ALU.add).then_inc(acc_read, 1)


def image_product(nc, g, name, images, parts, out, operand):
    cols = parts * D
    with ExitStack() as ctx:
        img = [sbuf(nc, ctx, f"{name}_img{i}", [P, N], U8) for i in range(4)]
        acc = [psum(nc, ctx, f"{name}_acc{i}", [P, 512], F32) for i in range(4)]
        loaded = [g.sem(f"{name}_loaded{i}") for i in range(4)]
        acc_ready, acc_read = (g.sem(f"{name}_{s}") for s in ("acc_ready", "acc_read"))
        rounds = T // 4
        with nc.Block() as block:
            @block.sync
            def _(sp):
                def load(r, i):
                    nc.sync.dma_start(img[i][:], images[bass.ds(r * 4 + i, 1), :, :]
                                      .rearrange("t p j -> (t p) j")).then_inc(loaded[i], 16)
                for i in range(4):
                    load(0, i)
                with sp.Fori(1, rounds) as r:
                    for i in range(4):
                        sp.wait_ge(acc_ready, r * 4 + (i - 3))
                        g.carry(sp)
                        load(r, i)

            @block.tensor
            def _(pe):
                def round_(r, first):
                    for i in range(4):
                        pe.wait_ge(loaded[i], (r + 1) * 16)
                        if not first:
                            pe.wait_ge(acc_read, r * 4 + (i - 3))
                        g.carry(pe)
                        image_matmuls(nc, img[i], acc[i][:, 0:cols], operand, cols).then_inc(acc_ready, 1)
                round_(0, True)
                with pe.Fori(1, rounds) as r:
                    round_(r, False)

            @block.vector
            def _(dve):
                with dve.Fori(0, rounds) as r:
                    for i in range(4):
                        dve.wait_ge(acc_ready, r * 4 + (i + 1))
                        reduce_parts(nc, out, r * 4 + i, acc[i][:, 0:cols], parts).then_inc(acc_read, 1)


def image_matmuls(nc, img, acc, operand, cols):
    view = img[:].rearrange("c (b i e) -> c b i e", i=P, e=2)
    for t in range(T):
        last = nc.tensor.matmul(acc, view[:, t // 2, :, t % 2].bitcast(FP8), operand[:, t, 0:cols],
                                start=(t == 0), stop=(t == T - 1))
    return last


def reduce_parts(nc, out, t, acc, parts):
    return nc.vector.tensor_reduce(out[:, bass.ds(t, 1), :].rearrange("p t d -> p (t d)"),
                                   acc.rearrange("p (s d) -> p d s", s=parts), AX.X, ALU.add)


def flip_pairs(nc, g, rows, bank):
    pairs = rows.bitcast(BF16)
    for b in range(NB):
        last = nc.tensor.transpose(bank[:, b * P:(b + 1) * P], pairs[:, b * P:(b + 1) * P], g.ident_b[:])
    return last


def constants(nc, g, ins):
    with ExitStack() as ctx:
        work = sbuf(nc, ctx, "const_work", [P, 2, P], F32)
        loaded, zeroed, shaped = (g.sem(f"const_{s}") for s in ("loaded", "zeroed", "shaped"))
        x_tiles = ins["x"].rearrange("(b p e) d -> p b e d", p=P, e=2)
        x_to = g.x[:].rearrange("p (b e) d -> p b e d", e=2)
        w0 = ins["L0_gnn_W"]
        loads = [(x_to[:, :, e, :], x_tiles[:, :, e, :]) for e in range(2)]
        loads += [
            (g.w0_rows[:], w0),
            (g.w_prep[0:D, 0:D], ins["L1_gnn_W"]), (g.w_prep[0:D, D:2 * D], ins["L1_gnn_Wq"]),
            (g.w_prep[0:D, 2 * D:3 * D], ins["L1_gnn_Wv"]),
            (g.w_prep[D:D + 1, D:2 * D], ins["L1_gnn_bq"].unsqueeze(0)),
            (g.w_prep[D:D + 1, 2 * D:3 * D], ins["L1_gnn_bv"].unsqueeze(0)),
            (g.theta[:], ins["L1_gnn_Theta"]),
            (g.w2[0:D, :], ins["L2_gnn_W"]), (g.w2[D:D + 1, :], ins["L2_gnn_b"].unsqueeze(0)),
            (g.w3[0:D, :], ins["L3_gnn_weight"]), (g.w3[D:D + 1, :], ins["L3_gnn_bias"].unsqueeze(0)),
        ]
        flipped = psum(nc, ctx, "const_flipped", [P, D], F32)
        w0_flipped = g.sem("const_w0_flipped")
        ident_ready = g.sem("const_ident_ready")
        with nc.Block() as block:
            @block.sync
            def _(sp):
                for to, frm in loads:
                    nc.sync.dma_start(to, frm).then_inc(loaded, 16)

            @block.gpsimd
            def _(pool):
                nc.gpsimd.memset(work[:], 0.0).then_inc(zeroed, 1)
                pool.wait_ge(zeroed, 1)
                nc.gpsimd.affine_select(out=work[:, 0, :], in_=work[:, 0, :], compare_op=ALU.not_equal, fill=1.0,
                                        base=0, pattern=[[-1, P]], channel_multiplier=1).then_inc(shaped, 1)
                nc.gpsimd.affine_select(out=work[:, 1, :], in_=work[:, 1, :], compare_op=ALU.is_ge, fill=1.0,
                                        base=0, pattern=[[1, P]], channel_multiplier=-1).then_inc(shaped, 1)

            @block.tensor
            def _(pe):
                pe.wait_ge(loaded, 16 * len(loads))
                pe.wait_ge(ident_ready, 1)
                nc.tensor.transpose(flipped[:], g.w0_rows[:], g.ident_f[0:D, 0:D]).then_inc(w0_flipped, 1)

            @block.vector
            def _(dve):
                v, step = nc.vector, Chain(dve, g)
                step(v.memset(g.w_prep[D:D + 1, 0:D], 0.0))
                dve.wait_ge(shaped, 2)
                eye, low = work[:, 0, :], work[:, 1, :]
                v.tensor_copy(g.ident_f[:], eye).then_inc(ident_ready, 1)
                step(v.tensor_copy(g.ident_b[:], eye))
                step(v.tensor_copy(g.ident_h[:], eye))
                step(v.tensor_scalar(g.mask_off[:], eye, -MASK_OFF, None, ALU.mult))
                step(v.memset(g.half[:], INV))
                count, unit = g.count, -BF16_STEP * INV
                step(v.tensor_scalar(count[:, 0, :], low, unit, None, ALU.mult))
                step(v.tensor_scalar(count[:, 2, :], eye, unit * (KEEP + 1.0), None, ALU.mult))
                step(v.tensor_scalar(count[:, 3, :], eye, -unit * KEEP, None, ALU.mult))
                step(v.tensor_tensor(count[:, 1, :], count[:, 0, :], count[:, 3, :], ALU.add))
                step(v.tensor_scalar(count[:, 5, :], count[:, 1, :], -1.0, unit, ALU.mult, ALU.add))
                step(v.tensor_tensor(work[:, 1, :], low, eye, ALU.add))
                step(v.tensor_scalar(count[:, 4, :], work[:, 1, :], -unit, unit, ALU.mult, ALU.add))
                dve.wait_ge(w0_flipped, 1)
                step(v.tensor_copy(g.w0[:], flipped[:]))
                dve.wait_ge(loaded, 16 * len(loads))


def neighbour_layer(nc, g, adj):
    cols = 3 * D + 1
    with ExitStack() as ctx:
        wide = sbuf(nc, ctx, "nb_wide", [P, T, 2 * D], F32)
        rest = sbuf(nc, ctx, "nb_rest", [P, T, D], F32)
        inv = sbuf(nc, ctx, "nb_inv", [P, T], F32)
        with nc.Block() as block:
            @block.vector
            def _(dve):
                step = Chain(dve, g)
                split3(nc.vector, step, g.vs, (1, 2, 0), g.x[:], rest[:])
                step(nc.vector.memset(g.vs[:, :, 3 * D:cols], 1.0))

        with ExitStack() as inner:
            raw = [sbuf(nc, inner, f"nb_raw{i}", [P, N], F32) for i in range(4)]
            byte = [sbuf(nc, inner, f"nb_byte{i}", [P, N], U8) for i in range(4)]
            img = [sbuf(nc, inner, f"nb_img{i}", [P, N], U8) for i in range(4)]
            bank = [psum(nc, inner, f"nb_bank{i}", [P, HALF], BF16) for i in range(2)]
            acc = [psum(nc, inner, f"nb_acc{i}", [P, 512], F32) for i in range(4)]
            loaded = [g.sem(f"nb_loaded{i}") for i in range(4)]
            rows_kept = [g.sem(f"nb_rows_kept{i}") for i in range(4)]
            imgs_kept = [g.sem(f"nb_imgs_kept{i}") for i in range(4)]
            byte_ready, flipped, img_ready, acc_ready, acc_read = (
                g.sem(f"nb_{s}") for s in ("byte_ready", "flipped", "img_ready", "acc_ready", "acc_read"))
            tiles = adj.rearrange("(r h p e) j -> r h e p j", h=2, p=P, e=2)
            rounds = T // 4
            with nc.Block() as block:
                @block.sync
                def _(sp):
                    def load(r, i):
                        nc.sync.dma_start(raw[i][:], tiles[bass.ds(r, 1), i // 2, i % 2, :, :]
                                          .rearrange("r p j -> (r p) j")).then_inc(loaded[i], 16)
                    for i in range(4):
                        load(0, i)
                    with sp.Fori(1, rounds) as r:
                        for i in range(4):
                            sp.wait_ge(byte_ready, r * 4 + (i - 3))
                            load(r, i)

                def reduce(nc, g, t, a):
                    tile = bass.ds(t, 1)
                    nc.vector.tensor_scalar(g.deg[:, tile], a[:, 3 * D:cols], INV, None, ALU.mult)
                    return reduce_parts(nc, g.prod, t, a[:, 0:3 * D], 3)

                @block.vector
                def _(dve):
                    def to_bytes(r, i, first=False):
                        dve.wait_ge(loaded[i], (r + 1) * 16)
                        if not first:
                            dve.wait_ge(flipped, r * 4 + (i - 3))
                            dve.wait_ge(rows_kept[i], r * 16)
                        nc.vector.tensor_scalar(byte[i][:], raw[i][:], BYTE, None, ALU.mult).then_inc(byte_ready, 1)
                    for i in range(4):
                        to_bytes(0, i, True)
                    with dve.Fori(1, rounds) as r:
                        for i in range(4):
                            to_bytes(r, i)
                            dve.wait_ge(acc_ready, r * 4 + (i - 3))
                            reduce(nc, g, r * 4 + (i - 4), acc[i]).then_inc(acc_read, 1)
                    for i in range(4):
                        dve.wait_ge(acc_ready, T - 3 + i)
                        reduce(nc, g, T - 4 + i, acc[i]).then_inc(acc_read, 1)

                def last_of_round(pe, r):
                    pe.wait_ge(img_ready, r * 4)
                    if not (isinstance(r, int) and r == 1):
                        pe.wait_ge(acc_read, r * 4 - 4)
                    g.carry(pe)
                    image_matmuls(nc, img[3], acc[3][:, 0:cols], g.vs, cols).then_inc(acc_ready, 1)

                @block.tensor
                def _(pe):
                    def flip(r, i, first=False):
                        pe.wait_ge(byte_ready, r * 4 + (i + 1))
                        if not (first and i < 2):
                            pe.wait_ge(img_ready, r * 4 + (i - 1))
                        flip_pairs(nc, g, byte[i][:], bank[i % 2][:]).then_inc(flipped, 1)

                    def product(r, i, first=False):
                        pe.wait_ge(img_ready, r * 4 + (i + 1))
                        if not first:
                            pe.wait_ge(acc_read, r * 4 + (i - 3))
                        g.carry(pe)
                        image_matmuls(nc, img[i], acc[i][:, 0:cols], g.vs, cols).then_inc(acc_ready, 1)

                    flip(0, 0, True)
                    for i in range(1, 4):
                        flip(0, i, True)
                        product(0, i - 1, True)

                    def round_(r):
                        flip(r, 0)
                        last_of_round(pe, r)
                        for i in range(1, 4):
                            flip(r, i)
                            product(r, i - 1)
                    round_(1)
                    with pe.Fori(2, rounds) as r:
                        round_(r)
                    last_of_round(pe, rounds)

                @block.scalar
                def _(act):
                    def to_image(r, i, first=False):
                        act.wait_ge(flipped, r * 4 + (i + 1))
                        if not first:
                            act.wait_ge(acc_ready, r * 4 + (i - 3))
                            act.wait_ge(imgs_kept[i], r * 16)
                        nc.scalar.copy(img[i][:].bitcast(U16), bank[i % 2][:].bitcast(U16)).then_inc(img_ready, 1)
                    for i in range(4):
                        to_image(0, i, True)
                    with act.Fori(1, rounds) as r:
                        for i in range(4):
                            to_image(r, i)

                @block.gpsimd
                def _(pool):
                    with pool.Fori(0, rounds) as r:
                        for i in range(4):
                            to = bass.ds(r * 4 + i, 1)
                            pool.wait_ge(byte_ready, r * 4 + (i + 1))
                            g.carry(pool)
                            nc.gpsimd.dma_start(g.rows[to, :, :].rearrange("t p j -> (t p) j"),
                                                byte[i][:]).then_inc(rows_kept[i], 16)
                            pool.wait_ge(img_ready, r * 4 + (i + 1))
                            g.carry(pool)
                            nc.gpsimd.dma_start(g.images[to, :, :].rearrange("t p j -> (t p) j"),
                                                img[i][:]).then_inc(imgs_kept[i], 16)
                    for i in range(4):
                        pool.wait_ge(rows_kept[i], rounds * 16)
                        pool.wait_ge(imgs_kept[i], rounds * 16)

        with nc.Block() as block:
            @block.vector
            def _(dve):
                v, step = nc.vector, Chain(dve, g)
                step(v.tensor_scalar(g.deg_floor[:], g.deg[:], 1.0, None, ALU.max))
                step(v.reciprocal(inv[:], g.deg_floor[:]))
                step(v.tensor_copy(wide[:, :, 0:D], g.x[:]))
                step(v.tensor_scalar(g.prod[:], g.prod[:], INV, None, ALU.mult))
                step(v.tensor_tensor(wide[:, :, D:2 * D], g.prod[:], per_node(inv[:]), ALU.mult))
        linear(nc, g, "nb_out", wide, 2 * D, g.w0[:], D, g.prod, relu=True)
    layernorm(nc, g, "ln0", g.prod[:])


def attention_scores(nc, g, name):
    with ExitStack() as ctx:
        q_hm = sbuf(nc, ctx, f"{name}_q_hm", [P, N], BF16)
        q_lh = sbuf(nc, ctx, f"{name}_q_lh", [P, N], BF16)
        f_hh = sbuf(nc, ctx, f"{name}_f_hh", [P, N], BF16)
        f_mm = sbuf(nc, ctx, f"{name}_f_mm", [P, N], BF16)
        f_hl = sbuf(nc, ctx, f"{name}_f_hl", [P, N], BF16)
        with ExitStack() as inner:
            qs = sbuf(nc, inner, f"{name}_qs", [P, T, 3 * D], BF16)
            fs = sbuf(nc, inner, f"{name}_fs", [P, T, 6 * D], BF16)
            rest = sbuf(nc, inner, f"{name}_rest", [P, T, D], F32)
            with nc.Block() as block:
                @block.vector
                def _(dve):
                    v, step = nc.vector, Chain(dve, g)
                    split3(v, step, qs, (1, 2, 0), g.xqv[:, :, D:2 * D], rest[:])
                    step(v.tensor_scalar(g.prod[:], g.prod[:], INV, None, ALU.mult))
                    split3(v, step, fs, (0, 2, 5), g.prod[:], rest[:])
                    step(v.tensor_copy(fs[:, :, D:2 * D], fs[:, :, 0:D]))
                    step(v.tensor_copy(fs[:, :, 3 * D:4 * D], fs[:, :, 2 * D:3 * D]))
                    step(v.tensor_copy(fs[:, :, 4 * D:5 * D], fs[:, :, 0:D]))
            build_stacks(nc, g, f"{name}_stacks", [
                (lambda t: qs[:, t, D:3 * D], q_hm, False),
                (lambda t: qs[:, t, 0:2 * D], q_lh, False),
                (lambda t: fs[:, t, 0:2 * D], f_hh, True),
                (lambda t: fs[:, t, 2 * D:4 * D], f_mm, True),
                (lambda t: fs[:, t, 4 * D:6 * D], f_hl, True)], BF16, g.ident_b[:])

        weighted = sbuf(nc, ctx, f"{name}_weighted", [P, N], F32)
        score = [sbuf(nc, ctx, f"{name}_score{i}", [P, N], F32) for i in range(2)]
        row = [sbuf(nc, ctx, f"{name}_row{i}", [P, N], U8) for i in range(2)]
        top = sbuf(nc, ctx, f"{name}_top", [P, 2, 4], F32)
        total = sbuf(nc, ctx, f"{name}_total", [P, 2, 2], F32)
        loaded = [g.sem(f"{name}_loaded{i}") for i in range(2)]
        raw_ready, masked, shift_ready, exp_ready, top_step, weight_step, weighted_step = (
            g.sem(f"{name}_{s}") for s in ("raw_ready", "masked", "shift_ready", "exp_ready", "top_step",
                                           "weight_step", "weighted_step"))
        with ExitStack() as inner:
            raw = [psum(nc, inner, f"{name}_raw{i}", [P, HALF], F32) for i in range(2)]
            rounds = T // 2
            with nc.Block() as block:
                @block.sync
                def _(sp):
                    def load(r, e):
                        nc.sync.dma_start(row[e][:], g.rows[bass.ds(r * 2 + e, 1), :, :]
                                          .rearrange("t p j -> (t p) j")).then_inc(loaded[e], 16)
                    load(0, 0)
                    load(0, 1)
                    with sp.Fori(1, rounds) as r:
                        for e in range(2):
                            sp.wait_ge(masked, r * 4 + (2 * e - 2))
                            load(r, e)

                @block.tensor
                def _(pe):
                    def products(r, e, first=False):
                        cols = bass.ds((r * 2 + e) * P, P)
                        for half in range(2):
                            if not (first and e == 0):
                                pe.wait_ge(masked, r * 4 + (2 * e + half - 1))
                            for lhs, rhs, kind in ((q_hm, f_hh, 0), (q_hm, f_mm, 1), (q_lh, f_hl, 2)):
                                for c in range(4):
                                    j = half * HALF + c * 512
                                    last = nc.tensor.matmul(raw[half][:, c * 512:(c + 1) * 512],
                                                            lhs[:, cols], rhs[:, j:j + 512],
                                                            start=(kind == 0), stop=(kind == 2))
                            last.then_inc(raw_ready, 1)
                    products(0, 0, True)
                    products(0, 1, True)
                    with pe.Fori(1, rounds) as r:
                        products(r, 0)
                        products(r, 1)

                @block.vector
                def _(dve):
                    v = nc.vector

                    def mask(r, e):
                        for half in range(2):
                            dve.wait_ge(raw_ready, r * 4 + (2 * e + half + 1))
                            if half == 0:
                                dve.wait_ge(loaded[e], (r + 1) * 16)
                                if not (isinstance(r, int) and r == 0):
                                    dve.wait_ge(weighted_step, r * 2 + e)
                            j = half * HALF
                            g.carry(dve)
                            v.tensor_tensor_reduce(score[e][:, j:j + HALF], raw[half][:], row[e][:, j:j + HALF],
                                                   D ** -0.5 / BYTE, -3.0e38, ALU.mult, ALU.max,
                                                   top[:, e, half:half + 1]).then_inc(masked, 1)
                        dve.wait_ge(masked, r * 4 + (2 * e + 2))
                        v.tensor_tensor(top[:, e, 2:3], top[:, e, 0:1], top[:, e, 1:2], ALU.max).then_inc(top_step, 1)
                        dve.wait_ge(top_step, r * 2 + (e + 1))
                        v.tensor_scalar(top[:, e, 3:4], top[:, e, 2:3], -1.0, None,
                                        ALU.mult).then_inc(shift_ready, 1)

                    def weigh(r, e, back=0):
                        dve.wait_ge(exp_ready, r * 2 + (e + 1 - back))
                        par = (e - back) % 2
                        v.reciprocal(total[:, par, 1:2], total[:, par, 0:1]).then_inc(weight_step, 1)
                        dve.wait_ge(weight_step, r * 2 + (e + 1 - back))
                        dve.wait_ge(weighted_step, r * 2 + (e + 1 - back))
                        v.scalar_tensor_tensor(out=weighted[:], in0=score[par][:], scalar=total[:, par, 1:2],
                                               in1=weighted[:], op0=ALU.mult, op1=ALU.add).then_inc(weighted_step, 1)

                    v.memset(weighted[:], 0.0).then_inc(weighted_step, 1)
                    dve.wait_ge(weighted_step, 1)
                    mask(0, 0)
                    mask(0, 1)
                    weigh(0, 0)
                    with dve.Fori(1, rounds) as r:
                        mask(r, 0)
                        weigh(r, 0, 1)
                        mask(r, 1)
                        weigh(r, 1, 1)
                    weigh(rounds - 1, 1)

                @block.scalar
                def _(act):
                    with act.Fori(0, rounds) as r:
                        for e in range(2):
                            act.wait_ge(shift_ready, r * 2 + (e + 1))
                            nc.scalar.activation(score[e][:], score[e][:], ACT.Exp, bias=top[:, e, 3:4],
                                                 accum_out=total[:, e, 0:1]).then_inc(exp_ready, 1)

        bank = psum(nc, ctx, f"{name}_colsum", [P, 512], F32)
        ones = sbuf(nc, ctx, f"{name}_ones", [P, 1], F32)
        ones_ready, summed = (g.sem(f"{name}_{s}") for s in ("ones_ready", "summed"))
        with nc.Block() as block:
            @block.tensor
            def _(pe):
                pe.wait_ge(ones_ready, 1)
                for t in range(T):
                    b, e = divmod(t, 2)
                    last = nc.tensor.matmul(bank[:, t:t + 1], weighted[:, 256 * b + e:256 * b + 256:2], ones[:],
                                            start=True, stop=True)
                last.then_inc(summed, 1)

            @block.vector
            def _(dve):
                nc.vector.memset(ones[:], 1.0).then_inc(ones_ready, 1)
                dve.wait_ge(summed, 1)
                Chain(dve, g)(nc.vector.tensor_copy(g.att[:], bank[:, 0:T]))


def root_of_squares(nc, g, name, src, dst):
    with ExitStack() as ctx:
        square = sbuf(nc, ctx, f"{name}_square", [P, T, D], F32)
        total = sbuf(nc, ctx, f"{name}_total", [P, T], F32)
        ready, rooted = (g.sem(f"{name}_{s}") for s in ("ready", "rooted"))
        with nc.Block() as block:
            @block.vector
            def _(dve):
                step = Chain(dve, g)
                step(nc.vector.tensor_tensor(square[:], src, src, ALU.mult))
                step(nc.vector.tensor_reduce(total[:], square[:], AX.X, ALU.add))
                nc.vector.tensor_scalar(total[:], total[:], SAFE, None, ALU.max).then_inc(ready, 1)

            @block.scalar
            def _(act):
                act.wait_ge(ready, 1)
                nc.scalar.activation(dst, total[:], ACT.Sqrt).then_inc(rooted, 1)
                act.wait_ge(rooted, 1)


def prune_edges(nc, g, name, theta):
    with ExitStack() as ctx:
        u_hl = sbuf(nc, ctx, f"{name}_u_hl", [P, N], F16)
        u_hh = sbuf(nc, ctx, f"{name}_u_hh", [P, N], F16)
        u_ll = sbuf(nc, ctx, f"{name}_u_ll", [P, N], F16)
        never = sbuf(nc, ctx, f"{name}_never", [P, T], F32)
        others = sbuf(nc, ctx, f"{name}_others", [P, T], F32)
        with ExitStack() as inner:
            us = sbuf(nc, inner, f"{name}_us", [P, T, 4 * D], F16)
            ul = sbuf(nc, inner, f"{name}_ul", [P, T, 2 * D], F16)
            unit = sbuf(nc, inner, f"{name}_unit", [P, T, D], F32)
            inv = sbuf(nc, inner, f"{name}_inv", [P, T], F32)
            with nc.Block() as block:
                @block.vector
                def _(dve):
                    v, step = nc.vector, Chain(dve, g)
                    step(v.tensor_scalar(inv[:], g.norm[:], 1e-8, None, ALU.max))
                    step(v.reciprocal(inv[:], inv[:]))
                    step(v.tensor_tensor(unit[:], g.kept_x[:], per_node(inv[:]), ALU.mult))
                    split2(v, step, ul, unit[:], unit[:], COS_SCALE)
                    for k, half in enumerate((0, 0, 1, 1)):
                        step(v.tensor_copy(us[:, :, k * D:(k + 1) * D], ul[:, :, half * D:(half + 1) * D]))
                    step(v.tensor_scalar(never[:], g.keep[:], -1.0e30, 1.0e30, ALU.mult, ALU.add))
                    step(v.tensor_scalar(others[:], g.deg[:], -1.0, float(N), ALU.mult, ALU.add))
            build_stacks(nc, g, f"{name}_stacks", [
                (lambda t: ul[:, t, :], u_hl, False),
                (lambda t: us[:, t, 0:2 * D], u_hh, True),
                (lambda t: us[:, t, 2 * D:4 * D], u_ll, True)], F16, g.ident_h[:])

        row = [sbuf(nc, ctx, f"{name}_row{i}", [P, N], U8) for i in range(2)]
        away = [sbuf(nc, ctx, f"{name}_away{i}", [P, N], U8) for i in range(2)]
        e_cos = [sbuf(nc, ctx, f"{name}_e_cos{i}", [P, N], F32) for i in range(2)]
        kept = [sbuf(nc, ctx, f"{name}_kept{i}", [P, N], U8) for i in range(2)]
        img = [sbuf(nc, ctx, f"{name}_img{i}", [P, N], U8) for i in range(2)]
        weight = sbuf(nc, ctx, f"{name}_weight", [P, 2, 8], F32)
        cos = [psum(nc, ctx, f"{name}_cos{i}", [P, 1024], F32) for i in range(2)]
        bank = psum(nc, ctx, f"{name}_bank", [P, HALF], BF16)
        count = psum(nc, ctx, f"{name}_count", [P, 2, 512], F32)
        loaded, rows_kept, imgs_kept = ([g.sem(f"{name}_{s}{i}") for i in range(2)]
                                        for s in ("loaded", "rows_kept", "imgs_kept"))
        away_ready, cos_ready, exp_ready, thr_step, kept_ready, flipped, img_ready, count_ready, count_read = (
            g.sem(f"{name}_{s}") for s in ("away_ready", "cos_ready", "exp_ready", "thr_step", "kept_ready",
                                           "flipped", "img_ready", "count_ready", "count_read"))
        rounds = T // 2
        with nc.Block() as block:
            @block.sync
            def _(sp):
                def load(r, e):
                    nc.sync.dma_start(row[e][:], g.rows[bass.ds(r * 2 + e, 1), :, :]
                                      .rearrange("t p j -> (t p) j")).then_inc(loaded[e], 16)

                def keep_rows(t, e, n):
                    sp.wait_ge(kept_ready, n)
                    g.carry(sp)
                    nc.sync.dma_start(g.kept_rows[bass.ds(t, 1), :, :].rearrange("t p j -> (t p) j"),
                                      kept[e][:]).then_inc(rows_kept[e], 16)

                def keep_image(t, e, n):
                    sp.wait_ge(img_ready, n)
                    g.carry(sp)
                    nc.sync.dma_start(g.kept_images[bass.ds(t, 1), :, :].rearrange("t p j -> (t p) j"),
                                      img[e][:]).then_inc(imgs_kept[e], 16)
                load(0, 0)
                load(0, 1)
                with sp.Fori(1, rounds) as r:
                    for e in range(2):
                        sp.wait_ge(away_ready, r * 2 + (e - 1))
                        g.carry(sp)
                        load(r, e)
                        keep_rows(r * 2 + (e - 2), e, r * 2 + (e - 1))
                        keep_image(r * 2 + (e - 2), e, r * 2 + (e - 1))
                for e in range(2):
                    keep_rows(T - 2 + e, e, T - 1 + e)
                    keep_image(T - 2 + e, e, T - 1 + e)
                for e in range(2):
                    sp.wait_ge(rows_kept[e], rounds * 16)
                    sp.wait_ge(imgs_kept[e], rounds * 16)

            @block.gpsimd
            def _(pool):
                def turn(r, e, first=False):
                    pool.wait_ge(loaded[e], (r + 1) * 16)
                    if not first:
                        pool.wait_ge(cos_ready, r * 8 + (4 * e - 4))
                    g.carry(pool)
                    nc.gpsimd.tensor_scalar(away[e][:].bitcast(U16), row[e][:].bitcast(U16), -1.0,
                                            BYTE * 257.0, ALU.mult, ALU.add).then_inc(away_ready, 1)
                turn(0, 0, True)
                turn(0, 1, True)
                with pool.Fori(1, rounds) as r:
                    turn(r, 0)
                    turn(r, 1)

            @block.tensor
            def _(pe):
                def cosines(r, e, first=False):
                    cols = bass.ds((r * 2 + e) * P, P)
                    pe.wait_ge(away_ready, r * 2 + (e + 1))
                    for k in range(4):
                        if not (first and e == 0 and k < 2):
                            pe.wait_ge(exp_ready, r * 8 + (4 * e + k - 1))
                        g.carry(pe)
                        for lhs, rhs, kind in ((g.mask_off, None, 0), (u_hl, u_hh, 1), (u_hl, u_ll, 2)):
                            for c in range(2):
                                j = k * 1024 + c * 512
                                mov = rhs[:, j:j + 512] if kind else away[e][:, j:j + 512].bitcast(FP8)
                                last = nc.tensor.matmul(cos[k % 2][:, c * 512:(c + 1) * 512],
                                                        lhs[:, cols] if kind else lhs[:], mov,
                                                        start=(kind == 0), stop=(kind == 2))
                        last.then_inc(cos_ready, 1)

                def flip(par, n):
                    pe.wait_ge(kept_ready, n)
                    if not (isinstance(n, int) and n == 1):
                        pe.wait_ge(img_ready, n - 1)
                    flip_pairs(nc, g, kept[par][:], bank[:]).then_inc(flipped, 1)

                def degrees(par, n):
                    pe.wait_ge(img_ready, n)
                    if not (isinstance(n, int) and n <= 2):
                        pe.wait_ge(count_read, n - 2)
                    g.carry(pe)
                    image_matmuls(nc, img[par], count[:, par, 0:1], g.half, 1).then_inc(count_ready, 1)

                cosines(0, 0, True)
                cosines(0, 1, True)
                flip(0, 1)
                for e in range(2):
                    cosines(1, e)
                    degrees(e, 1 + e)
                    flip(1 - e, 2 + e)
                with pe.Fori(2, rounds) as r:
                    for e in range(2):
                        cosines(r, e)
                        degrees(e, r * 2 + (e - 1))
                        flip(1 - e, r * 2 + e)
                flip(1, T)
                degrees(0, T - 1)
                degrees(1, T)

            @block.scalar
            def _(act):
                def exps(r, e, first=False):
                    for k in range(4):
                        act.wait_ge(cos_ready, r * 8 + (4 * e + k + 1))
                        if k == 0 and not first:
                            act.wait_ge(kept_ready, r * 2 + (e - 1))
                        nc.scalar.activation(e_cos[e][:, k * 1024:(k + 1) * 1024], cos[k % 2][:], ACT.Exp,
                                             scale=COS_SCALE ** -2,
                                             accum_out=weight[:, e, k:k + 1]).then_inc(exp_ready, 1)
                exps(0, 0, True)
                exps(0, 1, True)
                with act.Fori(1, rounds) as r:
                    exps(r, 0)
                    exps(r, 1)

            @block.vector
            def _(dve):
                v = nc.vector

                def compare(r, e, first=False):
                    tile = bass.ds(r * 2 + e, 1)
                    dve.wait_ge(exp_ready, r * 8 + (4 * e + 4))
                    v.tensor_reduce(weight[:, e, 4:5], weight[:, e, 0:4], AX.X, ALU.add).then_inc(thr_step, 1)
                    dve.wait_ge(thr_step, r * 6 + (3 * e + 1))
                    v.tensor_tensor(weight[:, e, 5:6], weight[:, e, 4:5], others[:, tile], ALU.add).then_inc(thr_step, 1)
                    dve.wait_ge(thr_step, r * 6 + (3 * e + 2))
                    v.scalar_tensor_tensor(out=weight[:, e, 6:7], in0=weight[:, e, 5:6], scalar=theta,
                                           in1=never[:, tile], op0=ALU.mult, op1=ALU.add).then_inc(thr_step, 1)
                    dve.wait_ge(thr_step, r * 6 + (3 * e + 3))
                    if not first:
                        dve.wait_ge(flipped, r * 2 + (e - 1))
                        dve.wait_ge(rows_kept[e], r * 16)
                    v.tensor_scalar(kept[e][:], e_cos[e][:], weight[:, e, 6:7], BYTE,
                                    ALU.is_ge, ALU.mult).then_inc(kept_ready, 1)

                def image(par, n, first=False):
                    dve.wait_ge(flipped, n)
                    if not first:
                        dve.wait_ge(count_ready, n - 2)
                        dve.wait_ge(imgs_kept[par], (n - 1 - par) * 8)
                        v.tensor_copy(g.conn[:, bass.ds(n - 3, 1)], count[:, par, 0:1]).then_inc(count_read, 1)
                    v.tensor_copy(img[par][:].bitcast(U16), bank[:].bitcast(U16)).then_inc(img_ready, 1)

                compare(0, 0, True)
                compare(0, 1, True)
                image(0, 1, True)
                compare(1, 0)
                image(1, 2, True)
                compare(1, 1)
                image(0, 3)
                with dve.Fori(2, rounds) as r:
                    compare(r, 0)
                    image(1, r * 2)
                    compare(r, 1)
                    image(0, r * 2 + 1)
                image(1, T)
                for par in range(2):
                    dve.wait_ge(count_ready, T - 1 + par)
                    v.tensor_copy(g.conn[:, T - 2 + par:T - 1 + par], count[:, par, 0:1]).then_inc(count_read, 1)
                dve.wait_ge(count_read, T)


def pruned_layer(nc, g, name, src, theta):
    linear(nc, g, f"{name}_xqv", src, D, g.w_prep[:], 3 * D, g.xqv, ones_row=True)
    with ExitStack() as ctx:
        rest = sbuf(nc, ctx, f"{name}_rest", [P, T, D], F32)
        with nc.Block() as block:
            @block.vector
            def _(dve):
                step = Chain(dve, g)
                split3(nc.vector, step, g.vs, (1, 2, 0), g.xqv[:, :, 2 * D:3 * D], rest[:])
    row_product(nc, g, f"{name}_ef", g.rows, 3 * D, 3, g.prod)
    attention_scores(nc, g, f"{name}_att")
    root_of_squares(nc, g, f"{name}_structural", g.xqv[:, :, 0:D], g.norm[:])
    with nc.Block() as block:
        @block.vector
        def _(dve):
            step = Chain(dve, g)
            step(nc.vector.tensor_scalar(g.norm[:], g.norm[:], 0.5, None, ALU.mult))
            step(nc.vector.scalar_tensor_tensor(out=g.logit[:], in0=g.att[:], scalar=0.5 / N, in1=g.norm[:],
                                                op0=ALU.mult, op1=ALU.add))
    softmax_keep(nc, g, f"{name}_comp", g.logit[:], theta, g.keep[:])
    with nc.Block() as block:
        @block.vector
        def _(dve):
            step = Chain(dve, g)
            step(nc.vector.tensor_tensor(g.kept_x[:], src[:], per_node(g.keep[:]), ALU.mult))
    root_of_squares(nc, g, f"{name}_magnitude", g.kept_x[:], g.norm[:])
    g.end_stage()
    prune_edges(nc, g, f"{name}_prune", theta)

    with nc.Block() as block:
        @block.vector
        def _(dve):
            step = Chain(dve, g)
            step(nc.vector.tensor_tensor(g.logit[:], g.conn[:], g.norm[:], ALU.mult))
    softmax_keep(nc, g, f"{name}_node", g.logit[:], theta, g.node[:])

    with ExitStack() as ctx:
        rest = sbuf(nc, ctx, f"{name}_rest2", [P, T, D], F32)
        inv = sbuf(nc, ctx, f"{name}_inv", [P, T], F32)
        root = sbuf(nc, ctx, f"{name}_root", [P, T], F32)
        floor_ready, root_ready = (g.sem(f"{name}_{s}") for s in ("floor_ready", "root_ready"))
        with nc.Block() as block:
            @block.vector
            def _(dve):
                v, step = nc.vector, Chain(dve, g)
                v.tensor_scalar(inv[:], g.conn[:], EDGE_EPS, None, ALU.max).then_inc(floor_ready, 1)
                step(v.tensor_scalar(g.logit[:], g.conn[:], 0.0, None, ALU.is_gt))
                step(v.tensor_tensor(g.node[:], g.node[:], g.logit[:], ALU.mult))
                step(v.tensor_tensor(g.node[:], g.node[:], g.keep[:], ALU.mult))
                dve.wait_ge(root_ready, 1)
                step(v.reciprocal(g.rsqrt[:], root[:]))
                step(v.tensor_tensor(g.node[:], g.node[:], g.rsqrt[:], ALU.mult))
                step(v.tensor_tensor(g.prod[:], g.xqv[:, :, 0:D], per_node(g.node[:]), ALU.mult))
                split3(v, step, g.vs, (1, 2, 0), g.prod[:], rest[:])

            @block.scalar
            def _(act):
                act.wait_ge(floor_ready, 1)
                nc.scalar.activation(root[:], inv[:], ACT.Sqrt).then_inc(root_ready, 1)
    row_product(nc, g, f"{name}_agg", g.kept_rows, 3 * D + 1, 3, g.prod, sums=g.logit)
    with ExitStack() as ctx:
        rest = sbuf(nc, ctx, f"{name}_rest3", [P, T, D], F32)
        inv = sbuf(nc, ctx, f"{name}_inv2", [P, T], F32)
        with nc.Block() as block:
            @block.vector
            def _(dve):
                v, step = nc.vector, Chain(dve, g)
                step(v.tensor_scalar(inv[:], g.logit[:], EDGE_EPS, None, ALU.max))
                step(v.reciprocal(inv[:], inv[:]))
                step(v.tensor_scalar(inv[:], inv[:], INV, None, ALU.mult))
                step(v.tensor_tensor(g.prod[:], g.prod[:], per_node(inv[:]), ALU.mult))
                split3(v, step, g.vs, (1, 2, 0), g.prod[:], rest[:])
    image_product(nc, g, f"{name}_msg", g.kept_images, 3, g.prod, g.vs)
    with nc.Block() as block:
        @block.vector
        def _(dve):
            v, step = nc.vector, Chain(dve, g)
            step(v.tensor_scalar(g.rsqrt[:], g.rsqrt[:], INV, None, ALU.mult))
            step(v.tensor_tensor(g.prod[:], g.prod[:], per_node(g.rsqrt[:]), ALU.mult))
    linear(nc, g, f"{name}_theta", g.prod, D, g.theta[:], D, g.y, relu=True)


def difference_layer(nc, g):
    with ExitStack() as ctx:
        xs = sbuf(nc, ctx, "df_xs", [P, T, 2 * D], F16)
        scaled = sbuf(nc, ctx, "df_scaled", [P, T, D], F32)
        inv = sbuf(nc, ctx, "df_inv", [P, T], F32)
        root = sbuf(nc, ctx, "df_root", [P, T], F32)
        with nc.Block() as block:
            @block.vector
            def _(dve):
                split2(nc.vector, Chain(dve, g), xs, g.x[:], scaled[:], X_SCALE)
        image_product(nc, g, "df_sum", g.images, 2, g.prod, xs)
        root_ready = g.sem("df_root_ready")
        with nc.Block() as block:
            @block.scalar
            def _(act):
                nc.scalar.activation(root[:], g.deg_floor[:], ACT.Sqrt).then_inc(root_ready, 1)

            @block.vector
            def _(dve):
                v, step = nc.vector, Chain(dve, g)
                dve.wait_ge(root_ready, 1)
                step(v.reciprocal(inv[:], root[:]))
                step(v.tensor_scalar(inv[:], inv[:], INV / X_SCALE, None, ALU.mult))
                step(v.tensor_tensor(g.prod[:], g.prod[:], per_node(inv[:]), ALU.mult))
                step(v.tensor_tensor(g.prod[:], g.x[:], g.prod[:], ALU.subtract))
        linear(nc, g, "df_out", g.prod, D, g.w2[:], D, g.y, relu=True, ones_row=True)
    layernorm(nc, g, "ln2", g.y[:])


def suffix_layer(nc, g):
    QUARTER = 8
    QT = 2 * QUARTER
    PAIRS = 2
    LOADS = NB // PAIRS
    BUF = 2
    R = LOADS // BUF
    S = 2 * PAIRS * BUF
    CLIP = BF16_STEP * (MAX_NEIGH - KEEP)
    with ExitStack() as ctx:
        xs = sbuf(nc, ctx, "sf_xs", [P, T, 2 * D], F16)
        scaled = sbuf(nc, ctx, "sf_scaled", [P, T, D], F32)
        clip = sbuf(nc, ctx, "sf_clip", [P, 1], F32)
        with nc.Block() as block:
            @block.vector
            def _(dve):
                step = Chain(dve, g)
                split2(nc.vector, step, xs, g.x[:], scaled[:], X_SCALE)
                step(nc.vector.memset(clip[:], CLIP))
        with ExitStack() as inner:
            blk = [sbuf(nc, inner, f"sf_blk{i}", [P, QT, PAIRS * 256], U8) for i in range(BUF)]
            w = [sbuf(nc, inner, f"sf_w{i}", [P, QT * P], I16) for i in range(2)]
            cnt = [psum(nc, inner, f"sf_cnt{i}", [P, 1024], F32) for i in range(2)]
            out = psum(nc, inner, "sf_out", [P, QT, 2 * D], F32)
            loaded = [g.sem(f"sf_loaded{i}") for i in range(BUF)]
            cnt_ready, w_act, w_dve, blk_used, w_used, out_read = (
                g.sem(f"sf_{s}") for s in ("cnt_ready", "w_act", "w_dve", "blk_used", "w_used", "out_read"))
            view = g.images.rearrange("t c (l m) -> l c t m", m=PAIRS * 256)
            passes = T // QT
            with nc.Block() as block:
                @block.sync
                def _(sp):
                    for q in range(passes):
                        def load(r, i):
                            nc.sync.dma_start(blk[i][:], view[bass.ds(r * (-BUF) + (LOADS - 1 - i), 1), :,
                                                              q * QT:(q + 1) * QT, :]
                                              .rearrange("l c t m -> (l c) t m")).then_inc(loaded[i], 16)
                        if q == 0:
                            for i in range(BUF):
                                load(0, i)
                        with sp.Fori(1 if q == 0 else 0, R) as r:
                            for i in range(BUF):
                                sp.wait_ge(blk_used, r * BUF + (q * LOADS + i + 1 - BUF))
                                load(r, i)

                @block.tensor
                def _(pe):
                    def add(i, pair, half, terms, fresh=False):
                        for ch in range(2):
                            tt = half * QUARTER + ch * 4
                            for k, (mat, e) in enumerate(terms):
                                cols = blk[i][:, tt:tt + 4, pair * 256 + e:pair * 256 + 256:2].bitcast(FP8)
                                last = nc.tensor.matmul(cnt[half][:, ch * 512:(ch + 1) * 512], g.count[:, mat, :],
                                                        cols, start=(fresh and k == 0),
                                                        stop=(k == len(terms) - 1), skip_group_check=True)
                        return last

                    def product(s, tile, n, opening=False):
                        pe.wait_ge(w_act, n)
                        pe.wait_ge(w_dve, n)
                        rhs = xs[:, tile, :].rearrange("p t d -> p (t d)")
                        for i in range(QT):
                            last = nc.tensor.matmul(out[:, i, :], w[s % 2][:, i * P:(i + 1) * P].bitcast(BF16), rhs,
                                                    start=(opening and i % 4 == 0), stop=True,
                                                    skip_group_check=True)
                        last.then_inc(w_used, 1)

                    def round_(q, r, first):
                        n0 = r * S + q * T
                        for s in range(S):
                            i, pair, e = s // (2 * PAIRS), PAIRS - 1 - s // 2 % PAIRS, 1 - s % 2
                            if s % (2 * PAIRS) == 0:
                                pe.wait_ge(loaded[i], (r + (q * R + 1)) * 16)
                            for half in range(2):
                                if not (first and s == 0 and q == 0):
                                    pe.wait_ge(w_dve if half else w_act, n0 + s)
                                g.carry(pe)
                                add(i, pair, half, ((1, 1), (0, 0)) if e else ((2, 1), (3, 0)),
                                    fresh=first and s == 0).then_inc(cnt_ready, 1)
                            if not (first and s == 0):
                                if first and s == 1 and q:
                                    pe.wait_ge(out_read, q)
                                product(s - 1, bass.ds(r * (-S) + (T - s), 1), n0 + s, first and s == 1)
                            if e == 0:
                                for half in range(2):
                                    pe.wait_ge(w_dve if half else w_act, n0 + (s + 1))
                                    g.carry(pe)
                                    last = add(i, pair, half, ((4, 1), (5, 0)))
                                if pair == 0:
                                    last.then_inc(blk_used, 1)

                    for q in range(passes):
                        round_(q, 0, True)
                        with pe.Fori(1, R) as r:
                            round_(q, r, False)
                        product(S - 1, slice(0, 1), (q + 1) * T)

                @block.scalar
                def _(act):
                    def weights(r, first=False):
                        for s in range(S):
                            act.wait_ge(cnt_ready, r * (2 * S) + (2 * s + 1))
                            if not (first and s < 2):
                                act.wait_ge(w_used, r * S + (s - 1))
                            nc.scalar.activation(w[s % 2][:, 0:QUARTER * P], cnt[0][:], ACT.Relu,
                                                 bias=clip[:]).then_inc(w_act, 1)
                    weights(0, True)
                    with act.Fori(1, passes * R) as r:
                        weights(r)

                @block.vector
                def _(dve):
                    def weights(n0, s, wait_used=True):
                        dve.wait_ge(cnt_ready, n0 * 2 + (2 * s + 2))
                        if wait_used:
                            dve.wait_ge(w_used, n0 + (s - 1))
                        nc.vector.tensor_scalar(w[s % 2][:, QUARTER * P:], cnt[1][:], CLIP, 0.0,
                                                ALU.add, ALU.max).then_inc(w_dve, 1)

                    for q in range(passes):
                        for s in range(S):
                            weights(q * T, s, wait_used=(q > 0 or s >= 2))
                        with dve.Fori(1, R) as r:
                            for s in range(S):
                                weights(r * S + q * T, s)
                        dve.wait_ge(w_used, (q + 1) * T)
                        nc.vector.tensor_reduce(g.prod[:, q * QT:(q + 1) * QT, :],
                                                out[:].rearrange("p t (s d) -> p t d s", s=2),
                                                AX.X, ALU.add).then_inc(out_read, 1)
        with nc.Block() as block:
            @block.vector
            def _(dve):
                step = Chain(dve, g)
                step(nc.vector.tensor_scalar(g.prod[:], g.prod[:], W_UP / X_SCALE, None, ALU.mult))
        linear(nc, g, "sf_out_w", g.prod, D, g.w3[:], D, g.y, ones_row=True)
    layernorm(nc, g, "ln3", g.y[:])


class State:

    def __init__(self, nc, ctx):
        self.nc, self.held = nc, []
        self.carried = ctx.enter_context(nc.semaphore("carried"))
        self.vector_step, self.vector_steps = ctx.enter_context(nc.semaphore("vector_step")), 0

        def keep(name, shape, dt=F32):
            return sbuf(nc, ctx, name, shape, dt)
        self.x, self.prod, self.y = (keep(n, [P, T, D]) for n in ("x", "prod", "y"))
        self.kept_x = keep("kept_x", [P, T, D])
        self.xqv = keep("xqv", [P, T, 3 * D])
        self.vs = keep("vs", [P, T, VC], BF16)
        (self.deg, self.deg_floor, self.att, self.norm, self.logit, self.keep, self.node, self.conn,
         self.rsqrt) = (keep(n, [P, T]) for n in ("deg", "deg_floor", "att", "norm", "logit", "keep",
                                                  "node", "conn", "rsqrt"))
        self.half = keep("half", [P, T, 1], BF16)
        self.ident_f = keep("ident_f", [P, P])
        self.ident_b = keep("ident_b", [P, P], BF16)
        self.ident_h = keep("ident_h", [P, P], F16)
        self.mask_off = keep("mask_off", [P, P], BF16)
        self.count = keep("count", [P, 6, P], BF16)
        self.w0_rows, self.w0 = keep("w0_rows", [D, 2 * D]), keep("w0", [2 * D, D])
        self.w_prep = keep("w_prep", [D + 1, 3 * D])
        self.theta = keep("theta", [D, D])
        self.w2, self.w3 = keep("w2", [D + 1, D]), keep("w3", [D + 1, D])
        self.rows, self.images, self.kept_rows, self.kept_images = (
            nc.dram_tensor(n, (T, P, N), U8, kind="Internal").ap()
            for n in ("rows", "images", "kept_rows", "kept_images"))


    def sem(self, name):
        self.held.append(self.nc.alloc_semaphore(name=name))
        return self.held[-1]

    def carry(self, eng):
        eng.sem_inc(self.carried, 1)

    def end_stage(self):
        with self.nc.Block() as block:
            @block.gpsimd
            def _(pool):
                self.nc.clear_and_free_semaphores(self.held)
        self.held = []


def store(nc, g, out):
    with ExitStack() as ctx:
        stored = g.sem("stored")
        to = out.rearrange("(b p e) d -> p b e d", p=P, e=2)
        frm = g.x[:].rearrange("p (b e) d -> p b e d", e=2)
        with nc.Block() as block:
            @block.sync
            def _(sp):
                for e in range(2):
                    nc.sync.dma_start(to[:, :, e, :], frm[:, :, e, :]).then_inc(stored, 16)
                sp.wait_ge(stored, 32)


def program(nc, ins, out):
    with ExitStack() as ctx:
        g = State(nc, ctx)
        constants(nc, g, ins)
        neighbour_layer(nc, g, ins["adj"])
        g.end_stage()
        src = g.x
        for it in range(2):
            theta = THETA0 + (1.0 - float(np.exp(-LAM * it))) * (THETA_MAX - THETA0)
            pruned_layer(nc, g, f"l{it}", src, theta)
            src = g.y
            g.end_stage()
        layernorm(nc, g, "ln1", g.y[:])
        difference_layer(nc, g)
        g.end_stage()
        suffix_layer(nc, g)
        store(nc, g, out)


INPUTS = ["x", "adj", "L0_gnn_W", "L1_gnn_W", "L1_gnn_Theta", "L1_gnn_Wq", "L1_gnn_bq", "L1_gnn_Wv",
          "L1_gnn_bv", "L2_gnn_W", "L2_gnn_b", "L3_gnn_weight", "L3_gnn_bias"]


def kernel(**inputs):
    import concourse.bacc as bacc
    from concourse.bass_utils import run_bass_kernel_spmd

    nc = bacc.Bacc("TRN2", target_bir_lowering=False, num_devices=1)
    arrays, args = {}, {}
    for name in INPUTS:
        a = np.ascontiguousarray(inputs[name])
        arrays[f"in_{name}"] = a
        args[name] = nc.dram_tensor(f"in_{name}", a.shape, mybir.dt.from_np(a.dtype), kind="ExternalInput").ap()
    out = nc.dram_tensor("out", (N, D), F32, kind="ExternalOutput").ap()
    program(nc, args, out)
    return run_bass_kernel_spmd(nc, [arrays], core_ids=[0]).results[0]["out"]
```

```python
import numpy as np
from contextlib import ExitStack

import concourse.bass as bass
from concourse import mybir

DT = mybir.dt
F32, BF16, F16, U8, U16, I16, I32, FP8 = (DT.float32, DT.bfloat16, DT.float16, DT.uint8, DT.uint16,
                                          DT.int16, DT.int32, DT.float8e4)
ALU = mybir.AluOpType
ACT = mybir.ActivationFunctionType
AX = mybir.AxisListType
RED = bass.bass_isa.ReduceOp

P = 128
N = 4096
D = 64
T = N // P
NB = T // 2
HALF = N // 2
BYTE = 64.0
FP8_ONE = 2.0
INV = 1.0 / FP8_ONE
SCALE_BITS = 14
SMALLEST_MAX = 1e-30
EXPONENT = 0x7F800000
PANEL = 512
PT = PANEL // P
NPANEL = N // PANEL
LN_EPS = 1e-5
SAFE = 1e-16
EDGE_EPS = 1e-6
COS_SCALE = 64.0
X_SCALE = 256.0
MASK_OFF = float(2 ** 19)
BF16_STEP = 128.0
W_UP = float(2 ** 27)
KEEP = 128.0
MAX_NEIGH = 100
DVE_COLS = 1536
THETA0, THETA_MAX, LAM = 0.000244, 0.0003, 0.1


def psum(nc, ctx, name, shape, dt):
    return ctx.enter_context(nc.psum_tensor(name, shape, dt))


def sbuf(nc, ctx, name, shape, dt):
    return ctx.enter_context(nc.sbuf_tensor(name, shape, dt))


class Chain:

    def __init__(self, eng, g):
        self.eng, self.g = eng, g

    def __call__(self, instruction):
        instruction.then_inc(self.g.vector_step, 1)
        self.g.vector_steps += 1
        self.eng.wait_ge(self.g.vector_step, self.g.vector_steps)


class LoopChain:

    def __init__(self, eng, sem, before):
        self.eng, self.sem, self.before, self.n = eng, sem, before, 0

    def __call__(self, instruction):
        instruction.then_inc(self.sem, 1)
        self.n += 1
        self.eng.wait_ge(self.sem, self.before + self.n)


def per_node(a, width=D):
    return a.unsqueeze(2).broadcast_to([P, a.shape[1], width])


def split3(v, step, dst, slots, src, rest, ready=None):
    hi, mid, lo = (dst[:, :, s * D:(s + 1) * D] for s in slots)
    step(v.tensor_copy(hi, src))
    step(v.tensor_tensor(rest, src, hi, ALU.subtract))
    step(v.tensor_copy(mid, rest))
    low = v.tensor_tensor(lo, rest, mid, ALU.subtract)
    low.then_inc(ready, 1) if ready is not None else step(low)


def split2(v, step, dst, src, scaled=None, scale=None, ready=None):
    hi, lo = dst[:, :, 0:D], dst[:, :, D:2 * D]
    if scale is not None:
        step(v.tensor_scalar(scaled, src, scale, None, ALU.mult))
        src = scaled
    step(v.tensor_copy(hi, src))
    low = v.tensor_tensor(lo, src, hi, ALU.subtract)
    low.then_inc(ready, 1) if ready is not None else step(low)


def layernorm(nc, g, name):
    with ExitStack() as ctx:
        norm = Layernorm(nc, g, ctx, name, T)
        with nc.Block() as block:
            @block.vector
            def _(dve):
                step = Chain(dve, g)
                step(nc.vector.tensor_tensor(g.x[:], g.x[:], g.y[:], ALU.add))
                norm.center(step, 0)
                norm.scale(dve, step, 0)

            @block.scalar
            def _(act):
                norm.roots(act)


class Layernorm:

    def __init__(self, nc, g, ctx, name, G):
        self.nc, self.g, self.G = nc, g, G
        self.row, self.mean, self.var, self.std = (sbuf(nc, ctx, f"{name}_{n}", [P, T], F32)
                                                   for n in ("row", "mean", "var", "std"))
        self.square = sbuf(nc, ctx, f"{name}_square", [P, G, D], F32)
        self.var_ready, self.std_ready = g.sem(f"{name}_var_ready"), g.sem(f"{name}_std_ready")

    def center(self, step, i):
        v, t = self.nc.vector, slice(i * self.G, (i + 1) * self.G)
        x, row, mean = self.g.x[:, t, :], self.row[:, t], self.mean[:, t]
        step(v.tensor_reduce(row, x, AX.X, ALU.add))
        step(v.tensor_scalar(mean, row, 1.0 / D, None, ALU.mult))
        step(v.tensor_tensor(x, x, per_node(mean), ALU.subtract))
        step(v.tensor_tensor(self.square[:], x, x, ALU.mult))
        step(v.tensor_reduce(row, self.square[:], AX.X, ALU.add))
        v.tensor_scalar(self.var[:, t], row, 1.0 / D, LN_EPS, ALU.mult, ALU.add).then_inc(self.var_ready, 1)

    def roots(self, act):
        for i in range(T // self.G):
            t = slice(i * self.G, (i + 1) * self.G)
            act.wait_ge(self.var_ready, i + 1)
            self.nc.scalar.activation(self.std[:, t], self.var[:, t], ACT.Sqrt).then_inc(self.std_ready, 1)

    def scale(self, dve, step, i):
        v, t = self.nc.vector, slice(i * self.G, (i + 1) * self.G)
        dve.wait_ge(self.std_ready, i + 1)
        step(v.reciprocal(self.var[:, t], self.std[:, t]))
        step(v.tensor_tensor(self.g.x[:, t, :], self.g.x[:, t, :], per_node(self.var[:, t]), ALU.mult))


def linear(nc, g, name, src, k, weights, n, dst, relu=False, ones_row=False, post=None, norm=False):
    kk = k + 1 if ones_row else k
    G = 4 if n > D else 8
    NG = T // G
    with ExitStack() as ctx:
        turned = sbuf(nc, ctx, f"{name}_turned", [kk, 2, G * P], F32)
        flipped = [psum(nc, ctx, f"{name}_flipped{i}", [P, G * P], F32) for i in range(2)]
        out = [psum(nc, ctx, f"{name}_out{i}", [P, G, 256 if n > D else D], F32) for i in range(2)]
        ln = Layernorm(nc, g, ctx, name, G) if norm else None
        flip_ready, turned_ready, out_ready, out_read, ones_ready = (
            g.sem(f"{name}_{s}") for s in ("flip_ready", "turned_ready", "out_ready", "out_read", "ones_ready"))
        with nc.Block() as block:
            @block.tensor
            def _(pe):
                def flips(i):
                    if i >= 2:
                        pe.wait_ge(turned_ready, i - 1)
                    for q in range(G):
                        last = nc.tensor.transpose(flipped[i % 2][0:k, q * P:(q + 1) * P],
                                                   src[:, i * G + q, 0:k], g.ident_f[:])
                    last.then_inc(flip_ready, 1)

                def products(i):
                    pe.wait_ge(turned_ready, i + 1)
                    if i == 0 and ones_row:
                        pe.wait_ge(ones_ready, 1)
                    if i >= 2:
                        pe.wait_ge(out_read, i - 1)
                    for q in range(G):
                        last = nc.tensor.matmul(out[i % 2][:, q, 0:n], turned[0:kk, i % 2, q * P:(q + 1) * P],
                                                weights, start=True, stop=True)
                    last.then_inc(out_ready, 1)

                flips(0)
                for i in range(NG):
                    if i + 1 < NG:
                        flips(i + 1)
                    products(i)

            @block.scalar
            def _(act):
                for i in range(NG):
                    act.wait_ge(flip_ready, i + 1)
                    if i >= 2:
                        act.wait_ge(out_ready, i - 1)
                    nc.scalar.copy(turned[0:k, i % 2, :], flipped[i % 2][0:k, :]).then_inc(turned_ready, 1)
                if norm:
                    ln.roots(act)

            @block.vector
            def _(dve):
                v, step = nc.vector, Chain(dve, g)
                if ones_row:
                    v.memset(turned[k:kk, :, :], 1.0).then_inc(ones_ready, 1)
                for i in range(NG):
                    dve.wait_ge(out_ready, i + 1)
                    tiles, frm = slice(i * G, (i + 1) * G), out[i % 2][:, :, 0:n]
                    if norm:
                        x = g.x[:, tiles, :]
                        if relu:
                            last = v.scalar_tensor_tensor(out=x, in0=frm, scalar=0.0, in1=x, op0=ALU.max, op1=ALU.add)
                        else:
                            last = v.tensor_tensor(x, frm, x, ALU.add)
                    elif relu:
                        last = v.tensor_scalar(dst[:, tiles, 0:n], frm, 0.0, None, ALU.max)
                    else:
                        last = v.tensor_copy(dst[:, tiles, 0:n], frm)
                    last.then_inc(out_read, 1)
                    if norm or post:
                        dve.wait_ge(out_read, i + 1)
                    if norm:
                        ln.center(step, i)
                        if i:
                            ln.scale(dve, step, i - 1)
                    if post:
                        post(step, tiles)
                if norm:
                    ln.scale(dve, step, NG - 1)


def build_stacks(nc, g, name, jobs, dt, ident):
    G = 8
    groups = [(src, dst, interleaved, t0) for src, dst, interleaved in jobs for t0 in range(0, T, G)]
    with ExitStack() as ctx:
        bank = [psum(nc, ctx, f"{name}_bank{i}", [P, G, P], dt) for i in range(8)]
        flipped, by_dve, by_act = (g.sem(f"{name}_{s}") for s in ("flipped", "by_dve", "by_act"))

        def place(i):
            _, dst, interleaved, t0 = groups[i]
            to = dst[:, t0 * P:(t0 + G) * P]
            if interleaved:
                return to.rearrange("k (b p e) -> k b e p", p=P, e=2), \
                    bank[i % 8][:].rearrange("k (b e) p -> k b e p", e=2)
            return to.rearrange("k (t p) -> k t p", p=P), bank[i % 8][:]

        with nc.Block() as block:
            @block.tensor
            def _(pe):
                for i, (src, _, _, t0) in enumerate(groups):
                    if i >= 8:
                        pe.wait_ge(by_act if i % 2 else by_dve, (i - 8) // 2 + 1)
                    for q in range(G):
                        last = nc.tensor.transpose(bank[i % 8][:, q, :], src(t0 + q), ident)
                    last.then_inc(flipped, 1)

            @block.vector
            def _(dve):
                for i in range(0, len(groups), 2):
                    dve.wait_ge(flipped, i + 1)
                    nc.vector.tensor_copy(*place(i)).then_inc(by_dve, 1)

            @block.scalar
            def _(act):
                for i in range(1, len(groups), 2):
                    act.wait_ge(flipped, i + 1)
                    nc.scalar.copy(*place(i)).then_inc(by_act, 1)


class SoftmaxKeep:

    def __init__(self, nc, g, ctx, name, logits, theta, keep):
        self.nc, self.g, self.logits, self.theta, self.keep = nc, g, logits, theta, keep
        self.one = sbuf(nc, ctx, f"{name}_one", [P, 4], F32)
        self.top = sbuf(nc, ctx, f"{name}_top", [1, 1], F32)
        self.e = sbuf(nc, ctx, f"{name}_e", [P, T], F32)
        self.bank = [psum(nc, ctx, f"{name}_bank{i}", [P, 512], F32) for i in range(2)]
        (self.top_ready, self.turned, self.neg_ready, self.spread, self.shift_ready, self.sum_ready,
         self.total_ready) = (g.sem(f"{name}_{s}") for s in ("top_ready", "turned", "neg_ready", "spread",
                                                             "shift_ready", "sum_ready", "total_ready"))

    def vector(self, dve, step):
        v, one = self.nc.vector, self.one
        v.tensor_reduce(one[:, 0:1], self.logits, AX.X, ALU.max).then_inc(self.top_ready, 1)
        dve.wait_ge(self.turned, 1)
        step(v.tensor_reduce(self.top[:], self.bank[0][0:1, 0:P], AX.X, ALU.max))
        v.tensor_scalar(self.top[:], self.top[:], -1.0, None, ALU.mult).then_inc(self.neg_ready, 1)
        dve.wait_ge(self.spread, 1)
        v.tensor_copy(one[:, 1:2], self.bank[1][:, 0:1]).then_inc(self.shift_ready, 1)
        dve.wait_ge(self.total_ready, 1)
        step(v.reciprocal(one[:, 3:4], self.bank[0][:, 0:1]))
        step(v.tensor_scalar(self.keep, self.e[:], one[:, 3:4], self.theta, ALU.mult, ALU.is_ge))

    def tensor(self, pe):
        t, g, one = self.nc.tensor, self.g, self.one
        pe.wait_ge(self.top_ready, 1)
        t.transpose(self.bank[0][0:1, 0:P], one[:, 0:1], g.ident_f[:]).then_inc(self.turned, 1)
        pe.wait_ge(self.neg_ready, 1)
        t.matmul(self.bank[1][:, 0:1], g.ones[0:1, :], self.top[:], start=True, stop=True).then_inc(self.spread, 1)
        pe.wait_ge(self.sum_ready, 1)
        t.matmul(self.bank[0][:, 0:1], g.ones[:], one[:, 2:3], start=True, stop=True).then_inc(self.total_ready, 1)

    def scalar(self, act):
        act.wait_ge(self.shift_ready, 1)
        self.nc.scalar.activation(self.e[:], self.logits, ACT.Exp, bias=self.one[:, 1:2],
                                  accum_out=self.one[:, 2:3]).then_inc(self.sum_ready, 1)


class Scales:

    def __init__(self, nc, g, ctx, name, maxima):
        self.nc, self.g, self.maxima = nc, g, maxima
        self.own = sbuf(nc, ctx, f"{name}_own", [P, 2], F32)
        self.top = sbuf(nc, ctx, f"{name}_top", [1, 2], F32)
        self.all = sbuf(nc, ctx, f"{name}_all", [P, 2], F32)
        self.bank = [psum(nc, ctx, f"{name}_bank{i}", [P, 512], F32) for i in range(2)]
        self.own_ready, self.turned, self.top_ready, self.spread = (
            g.sem(f"{name}_{s}") for s in ("own_ready", "turned", "top_ready", "spread"))

    def vector(self, dve, step):
        v, scales = self.nc.vector, self.g.scales
        v.tensor_reduce(self.own[:], self.maxima.rearrange("p g s -> p s g"), AX.X, ALU.max).then_inc(self.own_ready, 1)
        dve.wait_ge(self.turned, 1)
        step(v.tensor_reduce(self.top[:], self.bank[0][0:1, 0:2 * P].rearrange("o (s p) -> o s p", s=2),
                             AX.X, ALU.max))
        v.tensor_scalar(self.top[:], self.top[:], SMALLEST_MAX, None, ALU.max).then_inc(self.top_ready, 1)
        dve.wait_ge(self.spread, 1)
        step(v.tensor_copy(self.all[:], self.bank[1][:, 0:2]))
        bits = self.all[:].bitcast(I32)
        step(v.tensor_scalar(bits, bits, EXPONENT, None, ALU.bitwise_and))
        step(v.tensor_scalar(scales[:, 0:2].bitcast(I32), bits, -1.0, float((254 + SCALE_BITS) << 23),
                             ALU.mult, ALU.add))
        step(v.tensor_scalar(scales[:, 2:4].bitcast(I32), bits, float(-(SCALE_BITS << 23)), None, ALU.add))

    def tensor(self, pe):
        t, g = self.nc.tensor, self.g
        pe.wait_ge(self.own_ready, 1)
        for k in range(2):
            last = t.transpose(self.bank[0][0:1, k * P:(k + 1) * P], self.own[:, k:k + 1], g.ident_f[:])
        last.then_inc(self.turned, 1)
        pe.wait_ge(self.top_ready, 1)
        t.matmul(self.bank[1][:, 0:2], g.ones[0:1, :], self.top[:], start=True, stop=True).then_inc(self.spread, 1)


def row_product(nc, g, name, rows, operand, out, prelude, post, post_steps, sums=None, opening=None,
                squares=None, roots=None):
    cols = 2 * D + (1 if sums is not None else 0)
    HT = T // 2
    with ExitStack() as ctx:
        panel = [sbuf(nc, ctx, f"{name}_panel{i}", [P, HT, PANEL], U8) for i in range(4)]
        acc = [psum(nc, ctx, f"{name}_acc{i}", [P, PT, 256], F32) for i in range(2)]
        loaded = [g.sem(f"{name}_loaded{i}") for i in range(4)]
        half_used, acc_read, summed, operand_ready = (
            g.sem(f"{name}_{s}") for s in ("half_used", "acc_read", "summed", "operand_ready"))
        by_panel = rows.rearrange("t p (n j) -> n p t j", j=PANEL)
        rounds = NPANEL // 2
        with nc.Block() as block:
            @block.sync
            def _(sp):
                def load(r, i):
                    half = i % 2
                    nc.sync.dma_start(panel[i][:], by_panel[bass.ds(r * 2 + i // 2, 1), :,
                                                            half * HT:(half + 1) * HT, :]
                                      .rearrange("n p t j -> (n p) t j")).then_inc(loaded[i], 16)
                for i in range(4):
                    load(0, i)
                with sp.Fori(1, rounds) as r:
                    for i in range(4):
                        sp.wait_ge(half_used, r * 4 + (i - 3))
                        g.carry(sp)
                        load(r, i)

            @block.tensor
            def _(pe):
                def round_(r, first):
                    for i in range(4):
                        a, half = acc[i // 2], i % 2
                        pe.wait_ge(loaded[i], (r + 1) * 16)
                        if half == 0 and not first:
                            pe.wait_ge(acc_read, r * 2 + (i // 2 - 1))
                        g.carry(pe)
                        for t in range(HT):
                            tt = half * HT + t
                            if first and i < 2 and tt % (T // 4) == 0:
                                pe.wait_ge(operand_ready, tt // (T // 4) + 1)
                            for q in range(PT):
                                b, e = divmod(q, 2)
                                lhs = panel[i][:, t, 256 * b + e:256 * b + 256:2].bitcast(FP8)
                                last = nc.tensor.matmul(a[:, q, 0:cols], lhs, operand[:, tt, 0:cols],
                                                        start=(tt == 0 and e == 0), stop=(tt == T - 1),
                                                        skip_group_check=True)
                        last.then_inc(half_used, 1)
                if opening:
                    opening(pe)
                round_(0, True)
                with pe.Fori(1, rounds) as r:
                    round_(r, False)

            @block.vector
            def _(dve):
                prelude(dve, operand_ready)
                with dve.Fori(0, rounds) as r:
                    for k in range(2):
                        per_panel = post_steps + (1 if sums is not None else 0)
                        step = LoopChain(dve, summed, r * (2 * per_panel) + k * per_panel)
                        dve.wait_ge(half_used, r * 4 + (2 * k + 2))
                        tiles = bass.ds((r * 2 + k) * PT, PT)
                        if sums is not None:
                            step(nc.vector.tensor_scalar(sums[:, tiles], acc[k][:, :, 2 * D], INV, None, ALU.mult))
                        nc.vector.tensor_reduce(out[:, tiles, :], acc[k][:, :, 0:2 * D]
                                                .rearrange("p q (s d) -> p q d s", s=2),
                                                AX.X, ALU.add).then_inc(acc_read, 1)
                        dve.wait_ge(acc_read, r * 2 + (k + 1))
                        post(step, tiles)
                        assert step.n == per_panel

            if roots:
                @block.scalar
                def _(act):
                    roots(act)

            if squares:
                @block.gpsimd
                def _(pool):
                    squares(pool)


def image_product(nc, g, name, images, out, operand, scale, prelude=None):
    cols = 2 * D
    with ExitStack() as ctx:
        img = [sbuf(nc, ctx, f"{name}_img{i}", [P, N], U8) for i in range(4)]
        acc = [psum(nc, ctx, f"{name}_acc{i}", [P, 512], F32) for i in range(4)]
        raw = sbuf(nc, ctx, f"{name}_raw", [P, 4, D], F32)
        loaded = [g.sem(f"{name}_loaded{i}") for i in range(4)]
        acc_ready, acc_read, scaled, operand_ready = (
            g.sem(f"{name}_{s}") for s in ("acc_ready", "acc_read", "scaled", "operand_ready"))
        rounds = T // 4
        with nc.Block() as block:
            @block.sync
            def _(sp):
                def load(r, i):
                    nc.sync.dma_start(img[i][:], images[bass.ds(r * 4 + i, 1), :, :]
                                      .rearrange("t p j -> (t p) j")).then_inc(loaded[i], 16)
                for i in range(4):
                    load(0, i)
                with sp.Fori(1, rounds) as r:
                    for i in range(4):
                        sp.wait_ge(acc_ready, r * 4 + (i - 3))
                        g.carry(sp)
                        load(r, i)

            @block.tensor
            def _(pe):
                def round_(r, first):
                    for i in range(4):
                        pe.wait_ge(loaded[i], (r + 1) * 16)
                        if not first:
                            pe.wait_ge(acc_read, r * 4 + (i - 3))
                        g.carry(pe)
                        if first and i == 0 and prelude:
                            last = image_matmuls(nc, img[i], acc[i][:, 0:cols], operand, cols,
                                                 lambda quarter: pe.wait_ge(operand_ready, quarter + 1))
                        else:
                            last = image_matmuls(nc, img[i], acc[i][:, 0:cols], operand, cols)
                        last.then_inc(acc_ready, 1)
                round_(0, True)
                with pe.Fori(1, rounds) as r:
                    round_(r, False)

            @block.vector
            def _(dve):
                if prelude:
                    prelude(dve, operand_ready)

                def round_(r, first=False):
                    for i in range(4):
                        dve.wait_ge(acc_ready, r * 4 + (i + 1))
                        if not first:
                            dve.wait_ge(scaled, r * 4 + (i - 3))
                        nc.vector.tensor_reduce(raw[:, i, :], acc[i][:, 0:cols].rearrange("p (s d) -> p d s", s=2),
                                                AX.X, ALU.add).then_inc(acc_read, 1)
                        dve.wait_ge(acc_read, r * 4 + (i + 1))
                        tile = bass.ds(r * 4 + i, 1)
                        nc.vector.tensor_scalar(out[:, tile, :].rearrange("p t d -> p (t d)"), raw[:, i, :],
                                                scale if isinstance(scale, float) else scale[:, tile], None,
                                                ALU.mult).then_inc(scaled, 1)
                round_(0, True)
                with dve.Fori(1, rounds) as r:
                    round_(r)


def image_matmuls(nc, img, acc, operand, cols, await_quarter=None):
    view = img[:].rearrange("c (b i e) -> c b i e", i=P, e=2)
    for t in range(T):
        if await_quarter and t % (T // 4) == 0:
            await_quarter(t // (T // 4))
        last = nc.tensor.matmul(acc, view[:, t // 2, :, t % 2].bitcast(FP8), operand[:, t, 0:cols],
                                start=(t == 0), stop=(t == T - 1))
    return last


def flip_pairs(nc, g, rows, bank):
    pairs = rows.bitcast(BF16)
    for b in range(NB):
        last = nc.tensor.transpose(bank[:, b * P:(b + 1) * P], pairs[:, b * P:(b + 1) * P], g.ident_b[:])
    return last


def constants(nc, g, ins):
    with ExitStack() as ctx:
        work = sbuf(nc, ctx, "const_work", [P, 3, P], F32)
        loaded, zeroed, shaped = (g.sem(f"const_{s}") for s in ("loaded", "zeroed", "shaped"))
        w0 = ins["L0_gnn_W"]
        x_tiles = ins["x"].rearrange("(t p) d -> p t d", p=P)
        loads = [(g.x[:, h:h + T // 2, :], x_tiles[:, h:h + T // 2, :]) for h in (0, T // 2)]
        loads += [
            (g.w0_rows[:], w0),
            (g.w_prep[0:D, 0:D], ins["L1_gnn_W"]), (g.w_prep[0:D, D:2 * D], ins["L1_gnn_Wv"]),
            (g.w_prep[0:D, 2 * D:3 * D], ins["L1_gnn_Wq"]),
            (g.w_prep[D:D + 1, D:2 * D], ins["L1_gnn_bv"].unsqueeze(0)),
            (g.w_prep[D:D + 1, 2 * D:3 * D], ins["L1_gnn_bq"].unsqueeze(0)),
            (g.theta[:], ins["L1_gnn_Theta"]),
            (g.w2[0:D, :], ins["L2_gnn_W"]), (g.w2[D:D + 1, :], ins["L2_gnn_b"].unsqueeze(0)),
            (g.w3[0:D, :], ins["L3_gnn_weight"]), (g.w3[D:D + 1, :], ins["L3_gnn_bias"].unsqueeze(0)),
        ]
        flipped = psum(nc, ctx, "const_flipped", [P, D], F32)
        w0_flipped = g.sem("const_w0_flipped")
        ident_ready = g.sem("const_ident_ready")
        with nc.Block() as block:
            @block.sync
            def _(sp):
                for to, frm in loads:
                    nc.sync.dma_start(to, frm).then_inc(loaded, 16)

            @block.gpsimd
            def _(pool):
                nc.gpsimd.memset(work[:], 0.0).then_inc(zeroed, 1)
                pool.wait_ge(zeroed, 1)
                nc.gpsimd.affine_select(out=work[:, 0, :], in_=work[:, 0, :], compare_op=ALU.not_equal, fill=1.0,
                                        base=0, pattern=[[-1, P]], channel_multiplier=1).then_inc(shaped, 1)
                nc.gpsimd.affine_select(out=work[:, 1, :], in_=work[:, 1, :], compare_op=ALU.is_ge, fill=1.0,
                                        base=0, pattern=[[1, P]], channel_multiplier=-1).then_inc(shaped, 1)

            @block.tensor
            def _(pe):
                pe.wait_ge(loaded, 16 * len(loads))
                pe.wait_ge(ident_ready, 1)
                nc.tensor.transpose(flipped[:], g.w0_rows[:], g.ident_f[0:D, 0:D]).then_inc(w0_flipped, 1)

            @block.vector
            def _(dve):
                v, step = nc.vector, Chain(dve, g)
                step(v.memset(g.w_prep[D:D + 1, 0:D], 0.0))
                dve.wait_ge(shaped, 2)
                eye, low = work[:, 0, :], work[:, 1, :]
                v.tensor_copy(g.ident_f[:], eye).then_inc(ident_ready, 1)
                step(v.tensor_copy(g.ident_b[:], eye))
                step(v.tensor_copy(g.ident_h[:], eye))
                step(v.tensor_scalar(g.mask_off[:], eye, -MASK_OFF, None, ALU.mult))
                step(v.memset(g.half[:], INV))
                step(v.memset(g.ones[:], 1.0))
                step(v.memset(g.operand[:, :, 2 * D:2 * D + 1], 1.0))
                count, unit = g.count, -BF16_STEP * INV
                step(v.tensor_scalar(work[:, 2, :], eye, -KEEP, None, ALU.mult))
                step(v.tensor_tensor(work[:, 2, :], low, work[:, 2, :], ALU.add))
                step(v.tensor_scalar(count[:, 0, :], work[:, 2, :], unit, None, ALU.mult))
                step(v.tensor_scalar(count[:, 1, :], work[:, 2, :], -unit, unit, ALU.mult, ALU.add))
                dve.wait_ge(w0_flipped, 1)
                step(v.tensor_copy(g.w0[:], flipped[:]))
                dve.wait_ge(loaded, 16 * len(loads))


def neighbour_layer(nc, g, adj):
    cols = 3 * D + 1
    with ExitStack() as ctx:
        parts = sbuf(nc, ctx, "nb_parts", [P, T, cols + 7], BF16)
        wide = sbuf(nc, ctx, "nb_wide", [P, T, 2 * D], F32)
        rest = sbuf(nc, ctx, "nb_rest", [P, T, D], F32)
        inv = sbuf(nc, ctx, "nb_inv", [P, T], F32)
        with nc.Block() as block:
            @block.vector
            def _(dve):
                step = Chain(dve, g)
                split3(nc.vector, step, parts, (1, 2, 0), g.x[:], rest[:])
                step(nc.vector.memset(parts[:, :, 3 * D:cols], 1.0))

        with ExitStack() as inner:
            raw = [sbuf(nc, inner, f"nb_raw{i}", [P, N], F32) for i in range(4)]
            byte = [sbuf(nc, inner, f"nb_byte{i}", [P, N], U8) for i in range(4)]
            img = [sbuf(nc, inner, f"nb_img{i}", [P, N], U8) for i in range(4)]
            bank = [psum(nc, inner, f"nb_bank{i}", [P, HALF], BF16) for i in range(2)]
            acc = [psum(nc, inner, f"nb_acc{i}", [P, 512], F32) for i in range(4)]
            loaded = [g.sem(f"nb_loaded{i}") for i in range(4)]
            rows_kept = [g.sem(f"nb_rows_kept{i}") for i in range(4)]
            imgs_kept = [g.sem(f"nb_imgs_kept{i}") for i in range(4)]
            byte_ready, flipped, img_ready, acc_ready, acc_read = (
                g.sem(f"nb_{s}") for s in ("byte_ready", "flipped", "img_ready", "acc_ready", "acc_read"))
            tiles = adj.rearrange("(t p) j -> t p j", p=P)
            rounds = T // 4
            with nc.Block() as block:
                @block.sync
                def _(sp):
                    def load(r, i):
                        nc.sync.dma_start(raw[i][:], tiles[bass.ds(r * 4 + i, 1), :, :]
                                          .rearrange("t p j -> (t p) j")).then_inc(loaded[i], 16)
                    for i in range(4):
                        load(0, i)
                    with sp.Fori(1, rounds) as r:
                        for i in range(4):
                            sp.wait_ge(byte_ready, r * 4 + (i - 3))
                            load(r, i)

                def reduce(nc, g, t, a):
                    tile = bass.ds(t, 1)
                    nc.vector.tensor_scalar(g.deg[:, tile], a[:, 3 * D:cols], INV, None, ALU.mult)
                    return nc.vector.tensor_reduce(g.prod[:, tile, :].rearrange("p t d -> p (t d)"),
                                                   a[:, 0:3 * D].rearrange("p (s d) -> p d s", s=3), AX.X, ALU.add)

                @block.vector
                def _(dve):
                    def to_bytes(r, i, first=False):
                        dve.wait_ge(loaded[i], (r + 1) * 16)
                        if not first:
                            dve.wait_ge(flipped, r * 4 + (i - 3))
                            dve.wait_ge(rows_kept[i], r * 16)
                        nc.vector.tensor_scalar(byte[i][:].rearrange("p (b c e) -> p b e c", c=P, e=2),
                                                raw[i][:].rearrange("p (b e c) -> p b e c", c=P, e=2),
                                                BYTE, None, ALU.mult).then_inc(byte_ready, 1)
                    for i in range(4):
                        to_bytes(0, i, True)
                    with dve.Fori(1, rounds) as r:
                        for i in range(4):
                            to_bytes(r, i)
                            dve.wait_ge(acc_ready, r * 4 + (i - 3))
                            reduce(nc, g, r * 4 + (i - 4), acc[i]).then_inc(acc_read, 1)
                    for i in range(4):
                        dve.wait_ge(acc_ready, T - 3 + i)
                        reduce(nc, g, T - 4 + i, acc[i]).then_inc(acc_read, 1)

                def last_of_round(pe, r):
                    pe.wait_ge(img_ready, r * 4)
                    if not (isinstance(r, int) and r == 1):
                        pe.wait_ge(acc_read, r * 4 - 4)
                    g.carry(pe)
                    image_matmuls(nc, img[3], acc[3][:, 0:cols], parts, cols).then_inc(acc_ready, 1)

                @block.tensor
                def _(pe):
                    def flip(r, i, first=False):
                        pe.wait_ge(byte_ready, r * 4 + (i + 1))
                        if not (first and i < 2):
                            pe.wait_ge(img_ready, r * 4 + (i - 1))
                        flip_pairs(nc, g, byte[i][:], bank[i % 2][:]).then_inc(flipped, 1)

                    def product(r, i, first=False):
                        pe.wait_ge(img_ready, r * 4 + (i + 1))
                        if not first:
                            pe.wait_ge(acc_read, r * 4 + (i - 3))
                        g.carry(pe)
                        image_matmuls(nc, img[i], acc[i][:, 0:cols], parts, cols).then_inc(acc_ready, 1)

                    flip(0, 0, True)
                    for i in range(1, 4):
                        flip(0, i, True)
                        product(0, i - 1, True)

                    def round_(r):
                        flip(r, 0)
                        last_of_round(pe, r)
                        for i in range(1, 4):
                            flip(r, i)
                            product(r, i - 1)
                    round_(1)
                    with pe.Fori(2, rounds) as r:
                        round_(r)
                    last_of_round(pe, rounds)

                @block.scalar
                def _(act):
                    def to_image(r, i, first=False):
                        act.wait_ge(flipped, r * 4 + (i + 1))
                        if not first:
                            act.wait_ge(acc_ready, r * 4 + (i - 3))
                            act.wait_ge(imgs_kept[i], r * 16)
                        nc.scalar.copy(img[i][:].bitcast(U16), bank[i % 2][:].bitcast(U16)).then_inc(img_ready, 1)
                    for i in range(4):
                        to_image(0, i, True)
                    with act.Fori(1, rounds) as r:
                        for i in range(4):
                            to_image(r, i)

                @block.gpsimd
                def _(pool):
                    with pool.Fori(0, rounds) as r:
                        for i in range(4):
                            to = bass.ds(r * 4 + i, 1)
                            pool.wait_ge(byte_ready, r * 4 + (i + 1))
                            g.carry(pool)
                            nc.gpsimd.dma_start(g.rows[to, :, :].rearrange("t p j -> (t p) j"),
                                                byte[i][:]).then_inc(rows_kept[i], 16)
                            pool.wait_ge(img_ready, r * 4 + (i + 1))
                            g.carry(pool)
                            nc.gpsimd.dma_start(g.images[to, :, :].rearrange("t p j -> (t p) j"),
                                                img[i][:]).then_inc(imgs_kept[i], 16)
                    for i in range(4):
                        pool.wait_ge(rows_kept[i], rounds * 16)
                        pool.wait_ge(imgs_kept[i], rounds * 16)

        with nc.Block() as block:
            @block.vector
            def _(dve):
                v, step = nc.vector, Chain(dve, g)
                step(v.tensor_scalar(g.deg_floor[:], g.deg[:], 1.0, None, ALU.max))
                step(v.tensor_scalar(g.others[:], g.deg[:], -1.0, float(N), ALU.mult, ALU.add))
                step(v.reciprocal(inv[:], g.deg_floor[:]))
                step(v.tensor_copy(wide[:, :, 0:D], g.x[:]))
                step(v.tensor_scalar(g.prod[:], g.prod[:], INV, None, ALU.mult))
                step(v.tensor_tensor(wide[:, :, D:2 * D], g.prod[:], per_node(inv[:]), ALU.mult))
        linear(nc, g, "nb_out", wide, 2 * D, g.w0[:], D, None, relu=True, norm=True)


def attention_scores(nc, g, name, theta):
    with ExitStack() as ctx:
        q_hm, q_lh, f_hh, f_mm, f_hl = g.stacks
        weighted = sbuf(nc, ctx, f"{name}_weighted", [P, N], F32)
        score = [sbuf(nc, ctx, f"{name}_score{i}", [P, N], F32) for i in range(2)]
        row = [sbuf(nc, ctx, f"{name}_row{i}", [P, N], U8) for i in range(2)]
        share = [sbuf(nc, ctx, f"{name}_share{i}", [P, N - DVE_COLS], F32) for i in range(2)]
        top = sbuf(nc, ctx, f"{name}_top", [P, 2, 4], F32)
        total = sbuf(nc, ctx, f"{name}_total", [P, 2, 2], F32)
        loaded = [g.sem(f"{name}_loaded{i}") for i in range(2)]
        raw_ready, masked, shift_ready, exp_ready, weight_ready, weighted_step, share_ready, share_added = (
            g.sem(f"{name}_{s}") for s in ("raw_ready", "masked", "shift_ready", "exp_ready", "weight_ready",
                                           "weighted_step", "share_ready", "share_added"))
        with ExitStack() as inner:
            raw = [psum(nc, inner, f"{name}_raw{i}", [P, HALF], F32) for i in range(2)]
            rounds = T // 2
            with nc.Block() as block:
                @block.sync
                def _(sp):
                    def load(r, e):
                        nc.sync.dma_start(row[e][:], g.rows[bass.ds(r * 2 + e, 1), :, :]
                                          .rearrange("t p j -> (t p) j")).then_inc(loaded[e], 16)
                    load(0, 0)
                    load(0, 1)
                    with sp.Fori(1, rounds) as r:
                        for e in range(2):
                            sp.wait_ge(masked, r * 4 + (2 * e - 2))
                            load(r, e)

                @block.tensor
                def _(pe):
                    def products(r, e, first=False):
                        cols = bass.ds((r * 2 + e) * P, P)
                        for half in range(2):
                            if not (first and e == 0):
                                pe.wait_ge(masked, r * 4 + (2 * e + half - 1))
                            for lhs, rhs, kind in ((q_hm, f_hh, 0), (q_hm, f_mm, 1), (q_lh, f_hl, 2)):
                                for c in range(4):
                                    j = half * HALF + c * 512
                                    last = nc.tensor.matmul(raw[half][:, c * 512:(c + 1) * 512],
                                                            lhs[:, cols], rhs[:, j:j + 512],
                                                            start=(kind == 0), stop=(kind == 2))
                            last.then_inc(raw_ready, 1)
                    products(0, 0, True)
                    products(0, 1, True)
                    with pe.Fori(1, rounds) as r:
                        products(r, 0)
                        products(r, 1)

                @block.vector
                def _(dve):
                    v = nc.vector

                    def mask(r, e, half):
                        dve.wait_ge(raw_ready, r * 4 + (2 * e + half + 1))
                        if half == 0:
                            dve.wait_ge(loaded[e], (r + 1) * 16)
                            if not (isinstance(r, int) and r == 0):
                                dve.wait_ge(weighted_step, r * 2 + e)
                                dve.wait_ge(share_ready, r * 2 + (e - 1))
                        j = half * HALF
                        g.carry(dve)
                        v.tensor_tensor_reduce(score[e][:, j:j + HALF], raw[half][:], row[e][:, j:j + HALF],
                                               D ** -0.5 * INV / BYTE, -3.0e38, ALU.mult, ALU.max,
                                               top[:, e, half:half + 1]).then_inc(masked, 1)

                    def negate(r, e):
                        dve.wait_ge(masked, r * 4 + (2 * e + 2))
                        v.tensor_scalar(top[:, e, 3:4], top[:, e, 0:1], top[:, e, 1:2], -1.0,
                                        ALU.max, ALU.mult).then_inc(shift_ready, 1)

                    def invert(r, e, back=0):
                        par = (e - back) % 2
                        dve.wait_ge(exp_ready, r * 2 + (e + 1 - back))
                        v.reciprocal(total[:, par, 1:2], total[:, par, 0:1]).then_inc(weight_ready, 1)

                    def weigh(r, e, back=0):
                        par = (e - back) % 2
                        dve.wait_ge(weight_ready, r * 2 + (e + 1 - back))
                        dve.wait_ge(weighted_step, r * 2 + (e + 1 - back))
                        v.scalar_tensor_tensor(out=weighted[:, 0:DVE_COLS], in0=score[par][:, 0:DVE_COLS],
                                               scalar=total[:, par, 1:2], in1=weighted[:, 0:DVE_COLS],
                                               op0=ALU.mult, op1=ALU.add).then_inc(weighted_step, 1)

                    def tile(r, e):
                        mask(r, e, 0)
                        invert(r, e, 1)
                        mask(r, e, 1)
                        negate(r, e)
                        weigh(r, e, 1)

                    v.memset(weighted[:, 0:DVE_COLS], 0.0).then_inc(weighted_step, 1)
                    dve.wait_ge(weighted_step, 1)
                    mask(0, 0, 0)
                    mask(0, 0, 1)
                    negate(0, 0)
                    tile(0, 1)
                    with dve.Fori(1, rounds) as r:
                        tile(r, 0)
                        tile(r, 1)
                    invert(rounds - 1, 1)
                    weigh(rounds - 1, 1)

                @block.scalar
                def _(act):
                    def exps(r, e):
                        act.wait_ge(shift_ready, r * 2 + (e + 1))
                        nc.scalar.activation(score[e][:], score[e][:], ACT.Exp, bias=top[:, e, 3:4],
                                             accum_out=total[:, e, 0:1]).then_inc(exp_ready, 1)

                    def shares(r, e, back=0, first=False):
                        par = (e - back) % 2
                        act.wait_ge(weight_ready, r * 2 + (e + 1 - back))
                        if not first:
                            act.wait_ge(share_added, r * 2 + (e - back))
                        nc.scalar.activation(share[par][:], score[par][:, DVE_COLS:], ACT.Copy,
                                             scale=total[:, par, 1:2]).then_inc(share_ready, 1)
                    exps(0, 0)
                    shares(0, 1, 1, first=True)
                    exps(0, 1)
                    shares(1, 0, 1, first=True)
                    exps(1, 0)
                    shares(1, 1, 1)
                    exps(1, 1)
                    with act.Fori(2, rounds) as r:
                        for e in range(2):
                            shares(r, e, 1)
                            exps(r, e)
                    shares(rounds - 1, 1)

                @block.gpsimd
                def _(pool):
                    last_cols = weighted[:, DVE_COLS:]
                    nc.gpsimd.memset(last_cols, 0.0).then_inc(share_added, 1)
                    with pool.Fori(0, rounds) as r:
                        for e in range(2):
                            pool.wait_ge(share_ready, r * 2 + (e + 1))
                            pool.wait_ge(share_added, r * 2 + (e + 1))
                            nc.gpsimd.tensor_tensor(last_cols, share[e][:], last_cols, ALU.add).then_inc(share_added, 1)

        bank = psum(nc, ctx, f"{name}_colsum", [P, 512], F32)
        softmax = SoftmaxKeep(nc, g, ctx, f"{name}_comp", g.logit[:], theta, g.keep[:])
        summed = g.sem(f"{name}_summed")
        with nc.Block() as block:
            @block.tensor
            def _(pe):
                for t in range(T):
                    b, e = divmod(t, 2)
                    last = nc.tensor.matmul(bank[:, t:t + 1], weighted[:, 256 * b + e:256 * b + 256:2],
                                            g.ones[:, 0:1], start=True, stop=True)
                last.then_inc(summed, 1)
                softmax.tensor(pe)

            @block.scalar
            def _(act):
                softmax.scalar(act)

            @block.vector
            def _(dve):
                v, step = nc.vector, Chain(dve, g)
                dve.wait_ge(summed, 1)
                step(v.scalar_tensor_tensor(out=g.logit[:], in0=bank[:, 0:T], scalar=0.5 / N, in1=g.structural[:],
                                            op0=ALU.mult, op1=ALU.add))
                softmax.vector(dve, step)
                step(v.tensor_tensor(g.norm[:], g.norm[:], g.keep[:], ALU.mult))
                step(v.tensor_scalar(g.norm[:], g.norm[:], SAFE ** 0.5, None, ALU.max))
                step(v.tensor_tensor(g.unit[:], g.unit[:], per_node(g.keep[:], 2 * D), ALU.mult))
                for k, half in enumerate((0, 0, 1, 1)):
                    step(v.tensor_copy(g.units[:, :, k * D:(k + 1) * D], g.unit[:, :, half * D:(half + 1) * D]))
                step(v.tensor_scalar(g.never[:], g.keep[:], -1.0e30, 1.0e30, ALU.mult, ALU.add))


def prune_edges(nc, g, name, theta):
    with ExitStack() as ctx:
        u_hl = sbuf(nc, ctx, f"{name}_u_hl", [P, N], F16)
        u_hh = sbuf(nc, ctx, f"{name}_u_hh", [P, N], F16)
        u_ll = sbuf(nc, ctx, f"{name}_u_ll", [P, N], F16)
        build_stacks(nc, g, f"{name}_stacks", [
            (lambda t: g.unit[:, t, :], u_hl, False),
            (lambda t: g.units[:, t, 0:2 * D], u_hh, True),
            (lambda t: g.units[:, t, 2 * D:4 * D], u_ll, True)], F16, g.ident_h[:])

        row = [sbuf(nc, ctx, f"{name}_row{i}", [P, N], U8) for i in range(2)]
        away = [sbuf(nc, ctx, f"{name}_away{i}", [P, N], U8) for i in range(2)]
        e_cos = [sbuf(nc, ctx, f"{name}_e_cos{i}", [P, N], F32) for i in range(2)]
        kept = [sbuf(nc, ctx, f"{name}_kept{i}", [P, N], U8) for i in range(2)]
        img = [sbuf(nc, ctx, f"{name}_img{i}", [P, N], U8) for i in range(2)]
        weight = sbuf(nc, ctx, f"{name}_weight", [P, 2, 8], F32)
        cos = [psum(nc, ctx, f"{name}_cos{i}", [P, 1024], F32) for i in range(2)]
        bank = psum(nc, ctx, f"{name}_bank", [P, HALF], BF16)
        count = psum(nc, ctx, f"{name}_count", [P, 2, 512], F32)
        loaded, rows_kept, imgs_kept = ([g.sem(f"{name}_{s}{i}") for i in range(2)]
                                        for s in ("loaded", "rows_kept", "imgs_kept"))
        away_ready, cos_ready, exp_ready, thr_step, kept_ready, flipped, img_ready, count_ready, count_read = (
            g.sem(f"{name}_{s}") for s in ("away_ready", "cos_ready", "exp_ready", "thr_step", "kept_ready",
                                           "flipped", "img_ready", "count_ready", "count_read"))
        rounds = T // 2
        with nc.Block() as block:
            @block.sync
            def _(sp):
                def load(r, e):
                    nc.sync.dma_start(row[e][:], g.rows[bass.ds(r * 2 + e, 1), :, :]
                                      .rearrange("t p j -> (t p) j")).then_inc(loaded[e], 16)

                def keep_rows(t, e, n):
                    sp.wait_ge(kept_ready, n)
                    g.carry(sp)
                    nc.sync.dma_start(g.kept_rows[bass.ds(t, 1), :, :].rearrange("t p j -> (t p) j"),
                                      kept[e][:]).then_inc(rows_kept[e], 16)

                def keep_image(t, e, n):
                    sp.wait_ge(img_ready, n)
                    g.carry(sp)
                    nc.sync.dma_start(g.kept_images[bass.ds(t, 1), :, :].rearrange("t p j -> (t p) j"),
                                      img[e][:]).then_inc(imgs_kept[e], 16)
                load(0, 0)
                load(0, 1)
                def round_(r):
                    for e in range(2):
                        sp.wait_ge(away_ready, r * 2 + (e - 1))
                        g.carry(sp)
                        load(r, e)
                        keep_rows(r * 2 + (e - 2), e, r * 2 + (e - 1))
                        if e:
                            keep_image(r * 2 - 2, 0, r * 2 - 1)
                        elif not isinstance(r, int):
                            keep_image(r * 2 - 3, 1, r * 2 - 2)
                round_(1)
                with sp.Fori(2, rounds) as r:
                    round_(r)
                keep_rows(T - 2, 0, T - 1)
                keep_image(T - 3, 1, T - 2)
                keep_rows(T - 1, 1, T)
                keep_image(T - 2, 0, T - 1)
                keep_image(T - 1, 1, T)
                for e in range(2):
                    sp.wait_ge(rows_kept[e], rounds * 16)
                    sp.wait_ge(imgs_kept[e], rounds * 16)

            @block.gpsimd
            def _(pool):
                def turn(r, e, first=False):
                    pool.wait_ge(loaded[e], (r + 1) * 16)
                    if not first:
                        pool.wait_ge(cos_ready, r * 8 + (4 * e - 4))
                    g.carry(pool)
                    nc.gpsimd.tensor_scalar(away[e][:].bitcast(U16), row[e][:].bitcast(U16), -1.0,
                                            BYTE * 257.0, ALU.mult, ALU.add).then_inc(away_ready, 1)
                turn(0, 0, True)
                turn(0, 1, True)
                with pool.Fori(1, rounds) as r:
                    turn(r, 0)
                    turn(r, 1)

            @block.tensor
            def _(pe):
                def cosines(r, e, first=False):
                    cols = bass.ds((r * 2 + e) * P, P)
                    pe.wait_ge(away_ready, r * 2 + (e + 1))
                    for k in range(4):
                        if not (first and e == 0 and k < 2):
                            pe.wait_ge(exp_ready, r * 8 + (4 * e + k - 1))
                        g.carry(pe)
                        for lhs, rhs, kind in ((g.mask_off, None, 0), (u_hl, u_hh, 1), (u_hl, u_ll, 2)):
                            for c in range(2):
                                j = k * 1024 + c * 512
                                mov = rhs[:, j:j + 512] if kind else away[e][:, j:j + 512].bitcast(FP8)
                                last = nc.tensor.matmul(cos[k % 2][:, c * 512:(c + 1) * 512],
                                                        lhs[:, cols] if kind else lhs[:], mov,
                                                        start=(kind == 0), stop=(kind == 2))
                        last.then_inc(cos_ready, 1)

                def flip(par, n):
                    pe.wait_ge(kept_ready, n)
                    if not (isinstance(n, int) and n == 1):
                        pe.wait_ge(img_ready, n - 1)
                    flip_pairs(nc, g, kept[par][:], bank[:]).then_inc(flipped, 1)

                def degrees(par, n):
                    pe.wait_ge(img_ready, n)
                    if not (isinstance(n, int) and n <= 2):
                        pe.wait_ge(count_read, n - 2)
                    g.carry(pe)
                    image_matmuls(nc, img[par], count[:, par, 0:1], g.half, 1).then_inc(count_ready, 1)

                cosines(0, 0, True)
                cosines(0, 1, True)
                flip(0, 1)
                for e in range(2):
                    cosines(1, e)
                    degrees(e, 1 + e)
                    flip(1 - e, 2 + e)
                with pe.Fori(2, rounds) as r:
                    for e in range(2):
                        cosines(r, e)
                        degrees(e, r * 2 + (e - 1))
                        flip(1 - e, r * 2 + e)
                flip(1, T)
                degrees(0, T - 1)
                degrees(1, T)

            @block.scalar
            def _(act):
                def exps(r, e, first=False):
                    for k in range(4):
                        act.wait_ge(cos_ready, r * 8 + (4 * e + k + 1))
                        if k == 0 and not first:
                            act.wait_ge(kept_ready, r * 2 + (e - 1))
                        nc.scalar.activation(e_cos[e][:, k * 1024:(k + 1) * 1024], cos[k % 2][:], ACT.Exp,
                                             scale=COS_SCALE ** -2,
                                             accum_out=weight[:, e, k:k + 1]).then_inc(exp_ready, 1)
                exps(0, 0, True)
                exps(0, 1, True)
                with act.Fori(1, rounds) as r:
                    exps(r, 0)
                    exps(r, 1)

            @block.vector
            def _(dve):
                v = nc.vector

                def compare(r, e, first=False):
                    tile = bass.ds(r * 2 + e, 1)
                    dve.wait_ge(exp_ready, r * 8 + (4 * e + 4))
                    v.tensor_reduce(weight[:, e, 4:5], weight[:, e, 0:4], AX.X, ALU.add).then_inc(thr_step, 1)
                    dve.wait_ge(thr_step, r * 6 + (3 * e + 1))
                    v.tensor_tensor(weight[:, e, 5:6], weight[:, e, 4:5], g.others[:, tile], ALU.add).then_inc(thr_step, 1)
                    dve.wait_ge(thr_step, r * 6 + (3 * e + 2))
                    v.scalar_tensor_tensor(out=weight[:, e, 6:7], in0=weight[:, e, 5:6], scalar=theta,
                                           in1=g.never[:, tile], op0=ALU.mult, op1=ALU.add).then_inc(thr_step, 1)
                    dve.wait_ge(thr_step, r * 6 + (3 * e + 3))
                    if not first:
                        dve.wait_ge(flipped, r * 2 + (e - 1))
                        dve.wait_ge(rows_kept[e], r * 16)
                    v.tensor_scalar(kept[e][:], e_cos[e][:], weight[:, e, 6:7], BYTE,
                                    ALU.is_ge, ALU.mult).then_inc(kept_ready, 1)

                def image(par, n, first=False):
                    dve.wait_ge(flipped, n)
                    if not first:
                        dve.wait_ge(count_ready, n - 2)
                        dve.wait_ge(imgs_kept[par], (n - 1 - par) * 8)
                        v.tensor_copy(g.conn[:, bass.ds(n - 3, 1)], count[:, par, 0:1]).then_inc(count_read, 1)
                    v.tensor_copy(img[par][:].bitcast(U16), bank[:].bitcast(U16)).then_inc(img_ready, 1)

                compare(0, 0, True)
                compare(0, 1, True)
                image(0, 1, True)
                compare(1, 0)
                image(1, 2, True)
                compare(1, 1)
                image(0, 3)
                with dve.Fori(2, rounds) as r:
                    compare(r, 0)
                    image(1, r * 2)
                    compare(r, 1)
                    image(0, r * 2 + 1)
                image(1, T)
                for par in range(2):
                    dve.wait_ge(count_ready, T - 1 + par)
                    v.tensor_copy(g.conn[:, T - 2 + par:T - 1 + par], count[:, par, 0:1]).then_inc(count_read, 1)
                dve.wait_ge(count_read, T)


def pruned_layer(nc, g, name, src, theta):
    with ExitStack() as layer:
        g.xqv = sbuf(nc, layer, f"{name}_xqv_all", [P, T, 3 * D], F32)
        g.unit = sbuf(nc, layer, f"{name}_unit", [P, T, 2 * D], F16)
        g.units = sbuf(nc, layer, f"{name}_units", [P, T, 4 * D], F16)
        attention = layer.enter_context(ExitStack())
        g.stacks = [sbuf(nc, attention, f"{name}_stack_{n}", [P, N], BF16)
                    for n in ("q_hm", "q_lh", "f_hh", "f_mm", "f_hl")]
        with ExitStack() as ctx:
            g.qs = sbuf(nc, ctx, f"{name}_qs", [P, T, 3 * D], BF16)
            g.fs = sbuf(nc, ctx, f"{name}_fs", [P, T, 6 * D], BF16)
            maxima = sbuf(nc, ctx, f"{name}_maxima", [P, NPANEL, 2], F32)
            rest = sbuf(nc, ctx, f"{name}_rest", [P, PT, D], F32)
            sums = sbuf(nc, ctx, f"{name}_sums", [P, 2, T], F32)
            inv = sbuf(nc, ctx, f"{name}_inv", [P, T], F32)

            def maxima_and_q(step, tiles):
                step(nc.vector.tensor_reduce(maxima[:, tiles.start // PT, :], g.xqv[:, tiles, 0:2 * D]
                                             .rearrange("p t (s d) -> p s t d", s=2), AX.XY, ALU.max,
                                             apply_absolute_value=True))
                split3(nc.vector, step, g.qs[:, tiles, :], (1, 2, 0), g.xqv[:, tiles, 2 * D:3 * D], rest[:])
            linear(nc, g, f"{name}_xqv", src, D, g.w_prep[:], 3 * D, g.xqv, ones_row=True, post=maxima_and_q)

            big = [g.units[:, :, i * 2 * D:(i + 1) * 2 * D].bitcast(F32) for i in range(2)]
            scaling = ctx.enter_context(ExitStack())
            scales = Scales(nc, g, scaling, f"{name}_scales", maxima[:])
            squared, squares_ready, roots_ready = (
                g.sem(f"{name}_{s}") for s in ("squared", "squares_ready", "roots_ready"))
            squares_of = (g.xqv[:, :, 0:D], src[:])

            def squares(pool):
                for k, a in enumerate(squares_of):
                    nc.gpsimd.tensor_tensor(big[k], a, a, ALU.mult).then_inc(squared, 1)

            def prelude(dve, operand_ready):
                v, step, Q4 = nc.vector, Chain(dve, g), T // 4
                scales.vector(dve, step)
                for k in range(4):
                    t = slice(k * Q4, (k + 1) * Q4)
                    split2(v, step, g.operand[:, t, :], g.xqv[:, t, D:2 * D], g.prod[:, t, :],
                           g.scales[:, 1:2], operand_ready)
                for k in range(2):
                    dve.wait_ge(squared, k + 1)
                    step(v.tensor_reduce(sums[:, k, :], big[k], AX.X, ALU.add))
                    v.tensor_scalar(sums[:, k, :], sums[:, k, :], SAFE, None, ALU.max).then_inc(squares_ready, 1)
                dve.wait_ge(roots_ready, 2)
                step(v.tensor_scalar(g.structural[:], g.structural[:], 0.5, None, ALU.mult))
                step(v.tensor_scalar(inv[:], g.norm[:], 1e-8, None, ALU.max))
                step(v.reciprocal(inv[:], inv[:]))
                step(v.tensor_scalar(inv[:], inv[:], COS_SCALE, None, ALU.mult))
                step(v.tensor_tensor(big[0], src[:], per_node(inv[:]), ALU.mult))
                split2(v, step, g.unit, big[0])
                dve.wait_ge(operand_ready, 4)

            def roots(act):
                for k, to in enumerate((g.structural, g.norm)):
                    act.wait_ge(squares_ready, k + 1)
                    nc.scalar.activation(to[:], sums[:, k, :], ACT.Sqrt).then_inc(roots_ready, 1)

            def post(step, tiles):
                v, f = nc.vector, g.fs[:, tiles, :]
                step(v.tensor_scalar(g.prod[:, tiles, :], g.prod[:, tiles, :], g.scales[:, 3:4], None, ALU.mult))
                split3(v, step, f, (0, 2, 5), g.prod[:, tiles, :], rest[:])
                step(v.tensor_copy(f[:, :, D:2 * D], f[:, :, 0:D]))
                step(v.tensor_copy(f[:, :, 3 * D:4 * D], f[:, :, 2 * D:3 * D]))
                step(v.tensor_copy(f[:, :, 4 * D:5 * D], f[:, :, 0:D]))

            row_product(nc, g, f"{name}_ef", g.rows, g.operand, g.prod, prelude, post, 8,
                        opening=scales.tensor, squares=squares, roots=roots)
            scaling.close()
            q_hm, q_lh, f_hh, f_mm, f_hl = g.stacks
            build_stacks(nc, g, f"{name}_stacks", [
                (lambda t: g.qs[:, t, D:3 * D], q_hm, False),
                (lambda t: g.qs[:, t, 0:2 * D], q_lh, False),
                (lambda t: g.fs[:, t, 0:2 * D], f_hh, True),
                (lambda t: g.fs[:, t, 2 * D:4 * D], f_mm, True),
                (lambda t: g.fs[:, t, 4 * D:6 * D], f_hl, True)], BF16, g.ident_b[:])
        attention_scores(nc, g, f"{name}_att", theta)
        attention.close()
        g.end_stage()
        prune_edges(nc, g, f"{name}_prune", theta)

        with ExitStack() as ctx:
            floor = sbuf(nc, ctx, f"{name}_floor", [P, T], F32)
            root = sbuf(nc, ctx, f"{name}_root", [P, T], F32)
            floor_ready, root_ready = g.sem(f"{name}_floor_ready"), g.sem(f"{name}_root_ready")
            softmax = SoftmaxKeep(nc, g, ctx, f"{name}_node", g.logit[:], theta, g.node[:])
            with nc.Block() as block:
                @block.vector
                def _(dve):
                    v, step = nc.vector, Chain(dve, g)
                    step(v.tensor_tensor(g.logit[:], g.conn[:], g.norm[:], ALU.mult))
                    v.tensor_scalar(floor[:], g.conn[:], EDGE_EPS, None, ALU.max).then_inc(floor_ready, 1)
                    softmax.vector(dve, step)
                    step(v.tensor_scalar(g.logit[:], g.conn[:], 0.0, None, ALU.is_gt))
                    step(v.tensor_tensor(g.node[:], g.node[:], g.logit[:], ALU.mult))
                    step(v.tensor_tensor(g.node[:], g.node[:], g.keep[:], ALU.mult))
                    dve.wait_ge(root_ready, 1)
                    step(v.reciprocal(g.rsqrt[:], root[:]))
                    step(v.scalar_tensor_tensor(out=g.node[:], in0=g.node[:], scalar=g.scales[:, 0:1],
                                                in1=g.rsqrt[:], op0=ALU.mult, op1=ALU.mult))
                    step(v.tensor_scalar(g.rsqrt[:], g.rsqrt[:], INV, g.scales[:, 2:3], ALU.mult, ALU.mult))

                @block.tensor
                def _(pe):
                    softmax.tensor(pe)

                @block.scalar
                def _(act):
                    softmax.scalar(act)
                    act.wait_ge(floor_ready, 1)
                    nc.scalar.activation(root[:], floor[:], ACT.Sqrt).then_inc(root_ready, 1)

        with ExitStack() as ctx:
            g.ws = sbuf(nc, ctx, f"{name}_ws", [P, T, 2 * D], F16)
            Q4 = T // 4
            part = sbuf(nc, ctx, f"{name}_part", [P, Q4, D], F32)
            inv = sbuf(nc, ctx, f"{name}_inv2", [P, PT], F32)

            def prelude(dve, operand_ready):
                v, step = nc.vector, Chain(dve, g)
                for k in range(4):
                    t = slice(k * Q4, (k + 1) * Q4)
                    step(v.tensor_tensor(part[:], g.xqv[:, t, 0:D], per_node(g.node[:, t]), ALU.mult))
                    split2(v, step, g.operand[:, t, :], part[:], ready=operand_ready)
                    dve.wait_ge(operand_ready, k + 1)

            def post(step, tiles):
                v, a = nc.vector, g.prod[:, tiles, :]
                step(v.tensor_scalar(inv[:], g.logit[:, tiles], EDGE_EPS, None, ALU.max))
                step(v.reciprocal(inv[:], inv[:]))
                step(v.tensor_scalar(inv[:], inv[:], INV, None, ALU.mult))
                step(v.tensor_tensor(a, a, per_node(inv[:]), ALU.mult))
                split2(v, step, g.ws[:, tiles, :], a)

            row_product(nc, g, f"{name}_agg", g.kept_rows, g.operand, g.prod, prelude, post, 6, sums=g.logit)
            image_product(nc, g, f"{name}_msg", g.kept_images, g.prod, g.ws, g.rsqrt)
        linear(nc, g, f"{name}_theta", g.prod, D, g.theta[:], D, g.y, relu=True)


def split_features(nc, dve, g, xs, scaled, ready):
    Q4 = T // 4
    for k in range(4):
        t = slice(k * Q4, (k + 1) * Q4)
        split2(nc.vector, Chain(dve, g), xs[:, t, :], g.x[:, t, :], scaled[:, t, :], X_SCALE, ready)


def difference_layer(nc, g):
    with ExitStack() as ctx:
        xs = sbuf(nc, ctx, "df_xs", [P, T, 2 * D], F16)
        scaled = sbuf(nc, ctx, "df_scaled", [P, T, D], F32)
        inv = sbuf(nc, ctx, "df_inv", [P, T], F32)
        root = sbuf(nc, ctx, "df_root", [P, T], F32)
        root_ready = g.sem("df_root_ready")

        def prelude(dve, operand_ready):
            split_features(nc, dve, g, xs, scaled, operand_ready)
        image_product(nc, g, "df_sum", g.images, g.prod, xs, INV / X_SCALE, prelude=prelude)
        with nc.Block() as block:
            @block.scalar
            def _(act):
                nc.scalar.activation(root[:], g.deg_floor[:], ACT.Sqrt).then_inc(root_ready, 1)

            @block.vector
            def _(dve):
                v, step = nc.vector, Chain(dve, g)
                dve.wait_ge(root_ready, 1)
                step(v.reciprocal(inv[:], root[:]))
                step(v.tensor_tensor(g.prod[:], g.prod[:], per_node(inv[:]), ALU.mult))
                step(v.tensor_tensor(g.prod[:], g.x[:], g.prod[:], ALU.subtract))
        linear(nc, g, "df_out", g.prod, D, g.w2[:], D, None, relu=True, ones_row=True, norm=True)


def suffix_layer(nc, g):
    QUARTER = 8
    QT = 2 * QUARTER
    PAIRS = 2
    LOADS = NB // PAIRS
    BUF = 2
    R = LOADS // BUF
    S = 2 * PAIRS * BUF
    CLIP = BF16_STEP * (MAX_NEIGH - KEEP)
    with ExitStack() as ctx:
        xs = sbuf(nc, ctx, "sf_xs", [P, T, 2 * D], F16)
        scaled = sbuf(nc, ctx, "sf_scaled", [P, T, D], F32)
        clip = sbuf(nc, ctx, "sf_clip", [P, 1], F32)
        with nc.Block() as block:
            @block.vector
            def _(dve):
                Chain(dve, g)(nc.vector.memset(clip[:], CLIP))
                split_features(nc, dve, g, xs, scaled, g.sem("sf_operand_ready"))
        with ExitStack() as inner:
            blk = [sbuf(nc, inner, f"sf_blk{i}", [P, QT, PAIRS * 256], U8) for i in range(BUF)]
            w = [sbuf(nc, inner, f"sf_w{i}", [P, QT * P], I16) for i in range(2)]
            cnt = [psum(nc, inner, f"sf_cnt{i}", [P, 1024], F32) for i in range(2)]
            out = psum(nc, inner, "sf_out", [P, QT, 2 * D], F32)
            loaded = [g.sem(f"sf_loaded{i}") for i in range(BUF)]
            cnt_ready, w_act, w_dve, blk_used, w_used, out_read = (
                g.sem(f"sf_{s}") for s in ("cnt_ready", "w_act", "w_dve", "blk_used", "w_used", "out_read"))
            view = g.images.rearrange("t c (l m) -> l c t m", m=PAIRS * 256)
            passes = T // QT
            with nc.Block() as block:
                @block.sync
                def _(sp):
                    for q in range(passes):
                        def load(r, i):
                            nc.sync.dma_start(blk[i][:], view[bass.ds(r * (-BUF) + (LOADS - 1 - i), 1), :,
                                                              q * QT:(q + 1) * QT, :]
                                              .rearrange("l c t m -> (l c) t m")).then_inc(loaded[i], 16)
                        if q == 0:
                            for i in range(BUF):
                                load(0, i)
                        with sp.Fori(1 if q == 0 else 0, R) as r:
                            for i in range(BUF):
                                sp.wait_ge(blk_used, r * BUF + (q * LOADS + i + 1 - BUF))
                                load(r, i)

                @block.tensor
                def _(pe):
                    def add(i, pair, e, half, matrix, fresh=False):
                        for ch in range(2):
                            tt = half * QUARTER + ch * 4
                            cols = blk[i][:, tt:tt + 4, pair * 256 + e:pair * 256 + 256:2].bitcast(FP8)
                            last = nc.tensor.matmul(cnt[half][:, ch * 512:(ch + 1) * 512], g.count[:, matrix, :],
                                                    cols, start=fresh, stop=True, skip_group_check=True)
                        return last

                    def product(s, half, tile, opening=False):
                        rhs = xs[:, tile, :].rearrange("p t d -> p (t d)")
                        for i in range(half * QUARTER, (half + 1) * QUARTER):
                            last = nc.tensor.matmul(out[:, i, :], w[s % 2][:, i * P:(i + 1) * P].bitcast(BF16), rhs,
                                                    start=(opening and i % 4 == 0), stop=True,
                                                    skip_group_check=True)
                        return last

                    def where(s):
                        return s // (2 * PAIRS), PAIRS - 1 - s // 2 % PAIRS, 1 - s % 2

                    def finish(n0, s, tile, half, opening=False):
                        s %= S
                        i, pair, e = where(s)
                        pe.wait_ge(w_dve if half else w_act, n0)
                        g.carry(pe)
                        last = add(i, pair, e, half, 1)
                        if half and pair == 0 and e == 0:
                            last.then_inc(blk_used, 1)
                        last = product(s, half, tile, opening)
                        if half:
                            last.then_inc(w_used, 1)

                    def round_(q, r, first):
                        n0 = r * S + q * T
                        for s in range(S):
                            i, pair, e = where(s)
                            if s % (2 * PAIRS) == 0:
                                pe.wait_ge(loaded[i], (r + (q * R + 1)) * 16)
                                g.carry(pe)
                            if first and s == 1 and q:
                                pe.wait_ge(out_read, q)
                            for half in range(2):
                                if not (first and s == 0):
                                    finish_and_count(n0, s, i, pair, e, half, r, first)
                                else:
                                    add(i, pair, e, half, 0, fresh=True).then_inc(cnt_ready, 1)

                    def finish_and_count(n0, s, i, pair, e, half, r, first):
                        last_s = (s - 1) % S
                        pi, ppair, pe_ = where(last_s)
                        pe.wait_ge(w_dve if half else w_act, n0 + s)
                        g.carry(pe)
                        last = add(pi, ppair, pe_, half, 1)
                        if half and ppair == 0 and pe_ == 0:
                            last.then_inc(blk_used, 1)
                        add(i, pair, e, half, 0).then_inc(cnt_ready, 1)
                        last = product(last_s, half, bass.ds(r * (-S) + (T - s), 1), first and s == 1)
                        if half:
                            last.then_inc(w_used, 1)

                    for q in range(passes):
                        round_(q, 0, True)
                        with pe.Fori(1, R) as r:
                            round_(q, r, False)
                        for half in range(2):
                            finish((q + 1) * T, S - 1, slice(0, 1), half)

                @block.scalar
                def _(act):
                    def weights(r, first=False):
                        for s in range(S):
                            act.wait_ge(cnt_ready, r * (2 * S) + (2 * s + 1))
                            if not (first and s < 2):
                                act.wait_ge(w_used, r * S + (s - 1))
                            nc.scalar.activation(w[s % 2][:, 0:QUARTER * P], cnt[0][:], ACT.Relu,
                                                 bias=clip[:]).then_inc(w_act, 1)
                    weights(0, True)
                    with act.Fori(1, passes * R) as r:
                        weights(r)

                @block.vector
                def _(dve):
                    def weights(n0, s, wait_used=True):
                        dve.wait_ge(cnt_ready, n0 * 2 + (2 * s + 2))
                        if wait_used:
                            dve.wait_ge(w_used, n0 + (s - 1))
                        nc.vector.tensor_scalar(w[s % 2][:, QUARTER * P:], cnt[1][:], CLIP, 0.0,
                                                ALU.add, ALU.max).then_inc(w_dve, 1)

                    for q in range(passes):
                        for s in range(S):
                            weights(q * T, s, wait_used=(q > 0 or s >= 2))
                        with dve.Fori(1, R) as r:
                            for s in range(S):
                                weights(r * S + q * T, s)
                        dve.wait_ge(w_used, (q + 1) * T)
                        nc.vector.tensor_reduce(g.prod[:, q * QT:(q + 1) * QT, :],
                                                out[:].rearrange("p t (s d) -> p t d s", s=2),
                                                AX.X, ALU.add).then_inc(out_read, 1)
        with nc.Block() as block:
            @block.vector
            def _(dve):
                step = Chain(dve, g)
                step(nc.vector.tensor_scalar(g.prod[:], g.prod[:], W_UP / X_SCALE, None, ALU.mult))
        linear(nc, g, "sf_out_w", g.prod, D, g.w3[:], D, None, ones_row=True, norm=True)


class State:

    def __init__(self, nc, ctx):
        self.nc, self.held = nc, []
        self.carried = ctx.enter_context(nc.semaphore("carried"))
        self.vector_step, self.vector_steps = ctx.enter_context(nc.semaphore("vector_step")), 0

        def keep(name, shape, dt=F32):
            return sbuf(nc, ctx, name, shape, dt)
        self.x, self.prod, self.y = (keep(n, [P, T, D]) for n in ("x", "prod", "y"))
        self.operand = keep("operand", [P, T, 2 * D + 8], F16)
        self.scales = keep("scales", [P, 4])
        (self.deg, self.deg_floor, self.others, self.structural, self.norm, self.logit, self.keep, self.never,
         self.node, self.conn, self.rsqrt) = (
            keep(n, [P, T]) for n in ("deg", "deg_floor", "others", "structural", "norm", "logit", "keep",
                                      "never", "node", "conn", "rsqrt"))
        self.half = keep("half", [P, T, 1], BF16)
        self.ident_f = keep("ident_f", [P, P])
        self.ones = keep("ones", [P, P])
        self.ident_b = keep("ident_b", [P, P], BF16)
        self.ident_h = keep("ident_h", [P, P], F16)
        self.mask_off = keep("mask_off", [P, P], BF16)
        self.count = keep("count", [P, 2, P], BF16)
        self.w0_rows, self.w0 = keep("w0_rows", [D, 2 * D]), keep("w0", [2 * D, D])
        self.w_prep = keep("w_prep", [D + 1, 3 * D])
        self.theta = keep("theta", [D, D])
        self.w2, self.w3 = keep("w2", [D + 1, D]), keep("w3", [D + 1, D])
        self.rows, self.images, self.kept_rows, self.kept_images = (
            nc.dram_tensor(n, (T, P, N), U8, kind="Internal").ap()
            for n in ("rows", "images", "kept_rows", "kept_images"))


    def sem(self, name):
        self.held.append(self.nc.alloc_semaphore(name=name))
        return self.held[-1]

    def carry(self, eng):
        eng.sem_inc(self.carried, 1)

    def end_stage(self):
        with self.nc.Block() as block:
            @block.gpsimd
            def _(pool):
                self.nc.clear_and_free_semaphores(self.held)
        self.held = []


def store(nc, g, out):
    with ExitStack() as ctx:
        stored = g.sem("stored")
        with nc.Block() as block:
            @block.sync
            def _(sp):
                for h in (0, T // 2):
                    nc.sync.dma_start(out.rearrange("(t p) d -> p t d", p=P)[:, h:h + T // 2, :],
                                      g.x[:, h:h + T // 2, :]).then_inc(stored, 16)
                sp.wait_ge(stored, 32)


def program(nc, ins, out):
    with ExitStack() as ctx:
        g = State(nc, ctx)
        constants(nc, g, ins)
        neighbour_layer(nc, g, ins["adj"])
        g.end_stage()
        src = g.x
        for it in range(2):
            theta = THETA0 + (1.0 - float(np.exp(-LAM * it))) * (THETA_MAX - THETA0)
            pruned_layer(nc, g, f"l{it}", src, theta)
            src = g.y
            g.end_stage()
        layernorm(nc, g, "ln1")
        difference_layer(nc, g)
        g.end_stage()
        suffix_layer(nc, g)
        store(nc, g, out)


INPUTS = ["x", "adj", "L0_gnn_W", "L1_gnn_W", "L1_gnn_Theta", "L1_gnn_Wq", "L1_gnn_bq", "L1_gnn_Wv",
          "L1_gnn_bv", "L2_gnn_W", "L2_gnn_b", "L3_gnn_weight", "L3_gnn_bias"]


def kernel(**inputs):
    import concourse.bacc as bacc
    from concourse.bass_utils import run_bass_kernel_spmd

    nc = bacc.Bacc("TRN2", target_bir_lowering=False, num_devices=1)
    arrays, args = {}, {}
    for name in INPUTS:
        a = np.ascontiguousarray(inputs[name])
        arrays[f"in_{name}"] = a
        args[name] = nc.dram_tensor(f"in_{name}", a.shape, mybir.dt.from_np(a.dtype), kind="ExternalInput").ap()
    out = nc.dram_tensor("out", (N, D), F32, kind="ExternalOutput").ap()
    program(nc, args, out)
    return run_bass_kernel_spmd(nc, [arrays], core_ids=[0]).results[0]["out"]
```

```python
import numpy as np
from contextlib import ExitStack

import concourse.bass as bass
from concourse import mybir

DT = mybir.dt
F32, BF16, F16, U8, U16, I16, I32, FP8 = (DT.float32, DT.bfloat16, DT.float16, DT.uint8, DT.uint16,
                                          DT.int16, DT.int32, DT.float8e4)
ALU = mybir.AluOpType
ACT = mybir.ActivationFunctionType
AX = mybir.AxisListType

P = 128
N = 4096
D = 64
T = N // P
NB = T // 2
HALF = N // 2
BYTE = 64.0
FP8_ONE = 2.0
INV = 1.0 / FP8_ONE
SCALE_BITS = 14
SMALLEST_MAX = 1e-30
EXPONENT = 0x7F800000
PANEL = 512
PT = PANEL // P
NPANEL = N // PANEL
LN_EPS = 1e-5
SAFE = 1e-16
EDGE_EPS = 1e-6
COS_SCALE = 64.0
X_SCALE = 256.0
MASK_OFF = float(2 ** 19)
BF16_STEP = 128.0
W_UP = float(2 ** 27)
KEEP = 128.0
MAX_NEIGH = 100
LAST_SPLIT = 3456
DVE_COLS = 1280
THETA0, THETA_MAX, LAM = 0.000244, 0.0003, 0.1


def psum(nc, ctx, name, shape, dt):
    return ctx.enter_context(nc.psum_tensor(name, shape, dt))


def sbuf(nc, ctx, name, shape, dt):
    return ctx.enter_context(nc.sbuf_tensor(name, shape, dt))


class Chain:

    def __init__(self, eng, g):
        self.eng, self.g = eng, g

    def __call__(self, instruction):
        instruction.then_inc(self.g.vector_step, 1)
        self.g.vector_steps += 1
        self.eng.wait_ge(self.g.vector_step, self.g.vector_steps)


class LoopChain:

    def __init__(self, eng, sem, before):
        self.eng, self.sem, self.before, self.n = eng, sem, before, 0

    def __call__(self, instruction):
        self.unread(instruction)
        self.eng.wait_ge(self.sem, self.before + self.n)

    def unread(self, instruction):
        instruction.then_inc(self.sem, 1)
        self.n += 1


class Loads:

    def __init__(self, nc, g, ctx, name, shape, dt, count, source, next_stage=False):
        self.nc, self.count, self.source = nc, count, source
        self.buf = [sbuf(nc, ctx, f"{name}{i}", shape, dt) for i in range(count)]
        self.loaded = [g.sem(f"{name}_loaded{i}", next_stage) for i in range(count)]

    def load(self, r, i):
        self.nc.sync.dma_start(self.buf[i][:], self.source(r, i)).then_inc(self.loaded[i], 16)

    def first(self):
        for i in range(self.count):
            self.load(0, i)


def image_loads(nc, g, ctx, name, images):
    return Loads(nc, g, ctx, name, [P, N], U8, 4, lambda r, i: images[bass.ds(r * 4 + i, 1), :, :]
                 .rearrange("t p j -> (t p) j"))


def panel_loads(nc, g, ctx, name, rows):
    by_panel = rows.rearrange("t p (n j) -> n p t j", j=PANEL)
    return Loads(nc, g, ctx, name, [P, T // 2, PANEL], U8, 4,
                 lambda r, i: by_panel[bass.ds(r * 2 + i // 2, 1), :, (i % 2) * (T // 2):(i % 2 + 1) * (T // 2), :]
                 .rearrange("n p t j -> (n p) t j"))


def per_node(a, width=D):
    return a.unsqueeze(2).broadcast_to([P, a.shape[1], width])


def split3(v, step, dst, slots, src, rest, ready=None):
    hi, mid, lo = (dst[:, :, s * D:(s + 1) * D] for s in slots)
    step(v.tensor_copy(hi, src))
    step(v.tensor_tensor(rest, src, hi, ALU.subtract))
    step(v.tensor_copy(mid, rest))
    low = v.tensor_tensor(lo, rest, mid, ALU.subtract)
    low.then_inc(ready, 1) if ready is not None else step(low)


def split2(v, step, dst, src, scale=None, ready=None):
    hi, lo = dst[:, :, 0:D], dst[:, :, D:2 * D]
    if scale is None:
        step(v.tensor_copy(hi, src))
        low = v.tensor_tensor(lo, src, hi, ALU.subtract)
    else:
        step(v.tensor_scalar(hi, src, scale, None, ALU.mult))
        low = v.scalar_tensor_tensor(out=lo, in0=src, scalar=scale, in1=hi, op0=ALU.mult, op1=ALU.subtract)
    low.then_inc(ready, 1) if ready is not None else step(low)


class Layernorm:

    def __init__(self, nc, g, ctx, name, G):
        self.nc, self.g, self.G, self.NG = nc, g, G, T // G
        self.row, self.mean_of, self.var, self.std, self.inv = (
            sbuf(nc, ctx, f"{name}_{n}", [P, T], F32) for n in ("row", "mean", "var", "std", "inv"))
        self.square = sbuf(nc, ctx, f"{name}_square", [P, 2, G, D], F32)
        (self.mean_ready, self.centered, self.centered_last, self.squared, self.var_ready, self.std_ready,
         self.inv_ready) = (g.sem(f"{name}_{s}") for s in ("mean_ready", "centered", "centered_last", "squared",
                                                           "var_ready", "std_ready", "inv_ready"))

    def tiles(self, i):
        return slice(i * self.G, (i + 1) * self.G)

    def mean(self, step, i):
        v, x, row = self.nc.vector, self.g.x[:, self.tiles(i), :], self.row[:, self.tiles(i)]
        step(v.tensor_reduce(row, x, AX.X, ALU.add))
        if i < self.NG - 1:
            v.tensor_scalar(self.mean_of[:, self.tiles(i)], row, 1.0 / D, None, ALU.mult).then_inc(self.mean_ready, 1)
        else:
            v.scalar_tensor_tensor(out=x, in0=per_node(row), scalar=-1.0 / D, in1=x, op0=ALU.mult,
                                   op1=ALU.add).then_inc(self.centered_last, 1)

    def center(self, pool, i):
        x, mean = self.g.x[:, self.tiles(i), :], self.mean_of[:, self.tiles(i)]
        pool.wait_ge(self.mean_ready, i + 1)
        self.nc.gpsimd.tensor_tensor(x, x, per_node(mean), ALU.subtract).then_inc(self.centered, 1)

    def variance(self, dve, step, i):
        v, t = self.nc.vector, self.tiles(i)
        dve.wait_ge(self.squared, i + 1)
        step(v.tensor_reduce(self.row[:, t], self.square[:, i % 2], AX.X, ALU.add))
        v.tensor_scalar(self.var[:, t], self.row[:, t], 1.0 / D, LN_EPS, ALU.mult, ALU.add).then_inc(self.var_ready, 1)

    def invert(self, dve, i):
        t = self.tiles(i)
        dve.wait_ge(self.std_ready, i + 1)
        self.nc.vector.reciprocal(self.inv[:, t], self.std[:, t]).then_inc(self.inv_ready, 1)

    def scale(self, wait_engine, engine, i):
        t = self.tiles(i)
        wait_engine.wait_ge(self.inv_ready, i + 1)
        return engine.tensor_tensor(self.g.x[:, t, :], self.g.x[:, t, :], per_node(self.inv[:, t]), ALU.mult)

    def squares(self, act, i):
        if i < self.NG - 1:
            act.wait_ge(self.centered, i + 1)
        else:
            act.wait_ge(self.centered_last, 1)
        if i >= 2:
            act.wait_ge(self.var_ready, i - 1)
        self.nc.scalar.activation(self.square[:, i % 2], self.g.x[:, self.tiles(i), :],
                                  ACT.Square).then_inc(self.squared, 1)

    def roots(self, act, i):
        t = self.tiles(i)
        act.wait_ge(self.var_ready, i + 1)
        self.nc.scalar.activation(self.std[:, t], self.var[:, t], ACT.Sqrt).then_inc(self.std_ready, 1)


def linear(nc, g, name, src, k, weights, n, dst, relu=False, ones_row=False, post=None, norm=False,
           prefetch=None):
    kk = k + 1 if ones_row else k
    G = 4 if n > D else 8
    NG = T // G
    with ExitStack() as ctx:
        turned = sbuf(nc, ctx, f"{name}_turned", [kk, 2, G * P], F32)
        flipped = [psum(nc, ctx, f"{name}_flipped{i}", [P, G * P], F32) for i in range(2)]
        out = [psum(nc, ctx, f"{name}_out{i}", [P, G, 256 if n > D else D], F32) for i in range(2)]
        ln = Layernorm(nc, g, ctx, name, G) if norm else None
        flip_ready, turned_ready, out_ready, out_read, ones_ready, normed = (
            g.sem(f"{name}_{s}") for s in ("flip_ready", "turned_ready", "out_ready", "out_read", "ones_ready",
                                           "normed"))
        with nc.Block() as block:
            if prefetch:
                @block.sync
                def _(sp):
                    prefetch.first()

            @block.tensor
            def _(pe):
                def flips(i):
                    if i >= 2:
                        pe.wait_ge(turned_ready, i - 1)
                    for q in range(G):
                        last = nc.tensor.transpose(flipped[i % 2][0:k, q * P:(q + 1) * P],
                                                   src[:, i * G + q, 0:k], g.ident_f[:])
                    last.then_inc(flip_ready, 1)

                def products(i):
                    pe.wait_ge(turned_ready, i + 1)
                    if i == 0 and ones_row:
                        pe.wait_ge(ones_ready, 1)
                    if i >= 2:
                        pe.wait_ge(out_read, i - 1)
                    for q in range(G):
                        last = nc.tensor.matmul(out[i % 2][:, q, 0:n], turned[0:kk, i % 2, q * P:(q + 1) * P],
                                                weights, start=True, stop=True)
                    last.then_inc(out_ready, 1)

                flips(0)
                for i in range(NG):
                    if i + 1 < NG:
                        flips(i + 1)
                    products(i)

            @block.scalar
            def _(act):
                for i in range(NG + 4 if norm else NG):
                    if i < NG:
                        act.wait_ge(flip_ready, i + 1)
                        if i >= 2:
                            act.wait_ge(out_ready, i - 1)
                        nc.scalar.copy(turned[0:k, i % 2, :], flipped[i % 2][0:k, :]).then_inc(turned_ready, 1)
                    if norm and 0 <= i - 2 < NG:
                        ln.squares(act, i - 2)
                    if norm and 0 <= i - 3 < NG:
                        ln.roots(act, i - 3)

            if norm:
                @block.gpsimd
                def _(pool):
                    for i in range(NG - 1):
                        ln.center(pool, i)
                    pool.wait_ge(ln.centered, NG - 1)
                    for i in range(NG - 1):
                        ln.scale(pool, nc.gpsimd, i).then_inc(normed, 1)

            @block.vector
            def _(dve):
                v, step = nc.vector, Chain(dve, g)
                if ones_row:
                    v.memset(turned[k:kk, :, :], 1.0).then_inc(ones_ready, 1)
                for i in range(NG):
                    dve.wait_ge(out_ready, i + 1)
                    tiles, frm = slice(i * G, (i + 1) * G), out[i % 2][:, :, 0:n]
                    if norm:
                        x = g.x[:, tiles, :]
                        if relu:
                            last = v.scalar_tensor_tensor(out=x, in0=frm, scalar=0.0, in1=x, op0=ALU.max, op1=ALU.add)
                        else:
                            last = v.tensor_tensor(x, frm, x, ALU.add)
                    elif relu:
                        last = v.tensor_scalar(dst[:, tiles, 0:n], frm, 0.0, None, ALU.max)
                    else:
                        last = v.tensor_copy(dst[:, tiles, 0:n], frm)
                    last.then_inc(out_read, 1)
                    if norm or post:
                        dve.wait_ge(out_read, i + 1)
                    if norm:
                        ln.mean(step, i)
                        if i >= 2:
                            ln.invert(dve, i - 2)
                        if i >= 1:
                            ln.variance(dve, step, i - 1)
                    if post:
                        post(step, tiles)
                if norm:
                    ln.invert(dve, NG - 2)
                    ln.variance(dve, step, NG - 1)
                    ln.invert(dve, NG - 1)
                    ln.scale(dve, nc.vector, NG - 1).then_inc(normed, 1)
                    dve.wait_ge(normed, NG)


def build_stacks(nc, g, name, jobs, dt, ident, prefetch=None, dve_make=None, act_make=None,
                 pool_first=None):
    G = 8
    groups = [(src, dst, interleaved, t0) for t0 in range(0, T, G) for src, dst, interleaved in jobs]
    per_k = len(jobs)
    with ExitStack() as ctx:
        bank = [psum(nc, ctx, f"{name}_bank{i}", [P, G, P], dt) for i in range(8)]
        flipped, by_dve, by_act, made_dve, made_act = (
            g.sem(f"{name}_{s}") for s in ("flipped", "by_dve", "by_act", "made_dve", "made_act"))

        def place(i):
            _, dst, interleaved, t0 = groups[i]
            to = dst[:, t0 * P:(t0 + G) * P]
            if interleaved:
                return to.rearrange("k (b p e) -> k b e p", p=P, e=2), \
                    bank[i % 8][:].rearrange("k (b e) p -> k b e p", e=2)
            return to.rearrange("k (t p) -> k t p", p=P), bank[i % 8][:]

        with nc.Block() as block:
            if prefetch:
                @block.sync
                def _(sp):
                    prefetch.first()

            if pool_first:
                @block.gpsimd
                def _(pool):
                    pool_first(pool)

            @block.tensor
            def _(pe):
                for i, (src, _, _, t0) in enumerate(groups):
                    if i % per_k == 0 and dve_make:
                        pe.wait_ge(made_dve, i // per_k + 1)
                        pe.wait_ge(made_act, i // per_k + 1)
                    if i >= 8:
                        pe.wait_ge(by_act if i % 2 else by_dve, (i - 8) // 2 + 1)
                    for q in range(G):
                        last = nc.tensor.transpose(bank[i % 8][:, q, :], src(t0 + q), ident)
                    last.then_inc(flipped, 1)

            @block.vector
            def _(dve):
                if dve_make:
                    for k in range(T // G):
                        dve_make(dve, Chain(dve, g), k, made_dve)
                for i in range(0, len(groups), 2):
                    dve.wait_ge(flipped, i + 1)
                    nc.vector.tensor_copy(*place(i)).then_inc(by_dve, 1)

            @block.scalar
            def _(act):
                for i in range(1, len(groups), 2):
                    if act_make and i == 1:
                        act_make(act, 0, made_act)
                        act_make(act, 1, made_act)
                    elif act_make and i in (3, 5):
                        act_make(act, i // 2 + 1, made_act)
                    act.wait_ge(flipped, i + 1)
                    nc.scalar.copy(*place(i)).then_inc(by_act, 1)


class SoftmaxKeep:

    def __init__(self, nc, g, ctx, name, logits, theta, keep, bank=None):
        self.nc, self.g, self.logits, self.theta, self.keep = nc, g, logits, theta, keep
        self.one = sbuf(nc, ctx, f"{name}_one", [P, 4], F32)
        self.top = sbuf(nc, ctx, f"{name}_top", [1, 1], F32)
        self.e = sbuf(nc, ctx, f"{name}_e", [P, T], F32)
        self.bank = bank or [psum(nc, ctx, f"{name}_bank{i}", [P, 512], F32) for i in range(2)]
        (self.top_ready, self.turned, self.neg_ready, self.spread, self.shift_ready, self.sum_ready,
         self.total_ready) = (g.sem(f"{name}_{s}") for s in ("top_ready", "turned", "neg_ready", "spread",
                                                             "shift_ready", "sum_ready", "total_ready"))

    def vector(self, dve, step):
        v, one = self.nc.vector, self.one
        v.tensor_reduce(one[:, 0:1], self.logits, AX.X, ALU.max).then_inc(self.top_ready, 1)
        dve.wait_ge(self.turned, 1)
        step(v.tensor_reduce(self.top[:], self.bank[0][0:1, 0:P], AX.X, ALU.max))
        v.tensor_scalar(self.top[:], self.top[:], -1.0, None, ALU.mult).then_inc(self.neg_ready, 1)
        dve.wait_ge(self.spread, 1)
        v.tensor_copy(one[:, 1:2], self.bank[1][:, 0:1]).then_inc(self.shift_ready, 1)
        dve.wait_ge(self.total_ready, 1)
        step(v.reciprocal(one[:, 3:4], self.bank[0][:, 0:1]))
        step(v.tensor_scalar(self.keep, self.e[:], one[:, 3:4], self.theta, ALU.mult, ALU.is_ge))

    def tensor(self, pe):
        t, g, one = self.nc.tensor, self.g, self.one
        pe.wait_ge(self.top_ready, 1)
        t.transpose(self.bank[0][0:1, 0:P], one[:, 0:1], g.ident_f[:]).then_inc(self.turned, 1)
        pe.wait_ge(self.neg_ready, 1)
        t.matmul(self.bank[1][:, 0:1], g.ones[0:1, :], self.top[:], start=True, stop=True).then_inc(self.spread, 1)
        pe.wait_ge(self.sum_ready, 1)
        t.matmul(self.bank[0][:, 0:1], g.ones[:], one[:, 2:3], start=True, stop=True).then_inc(self.total_ready, 1)

    def scalar(self, act):
        act.wait_ge(self.shift_ready, 1)
        self.nc.scalar.activation(self.e[:], self.logits, ACT.Exp, bias=self.one[:, 1:2],
                                  accum_out=self.one[:, 2:3]).then_inc(self.sum_ready, 1)


class Scales:

    def __init__(self, nc, g, ctx, name, maxima):
        self.nc, self.g, self.maxima = nc, g, maxima
        self.own = sbuf(nc, ctx, f"{name}_own", [P, 2], F32)
        self.top = sbuf(nc, ctx, f"{name}_top", [1, 2], F32)
        self.all = sbuf(nc, ctx, f"{name}_all", [P, 2], F32)
        self.bank = [psum(nc, ctx, f"{name}_bank{i}", [P, 512], F32) for i in range(2)]
        self.own_ready, self.turned, self.top_ready, self.spread = (
            g.sem(f"{name}_{s}") for s in ("own_ready", "turned", "top_ready", "spread"))

    def vector(self, dve, step):
        v, scales = self.nc.vector, self.g.scales
        v.tensor_reduce(self.own[:], self.maxima.rearrange("p g s -> p s g"), AX.X, ALU.max).then_inc(self.own_ready, 1)
        dve.wait_ge(self.turned, 1)
        step(v.tensor_reduce(self.top[:], self.bank[0][0:1, 0:2 * P].rearrange("o (s p) -> o s p", s=2),
                             AX.X, ALU.max))
        v.tensor_scalar(self.top[:], self.top[:], SMALLEST_MAX, None, ALU.max).then_inc(self.top_ready, 1)
        dve.wait_ge(self.spread, 1)
        step(v.tensor_copy(self.all[:], self.bank[1][:, 0:2]))
        bits = self.all[:].bitcast(I32)
        step(v.tensor_scalar(bits, bits, EXPONENT, None, ALU.bitwise_and))
        step(v.tensor_scalar(scales[:, 0:2].bitcast(I32), bits, -1.0, float((254 + SCALE_BITS) << 23),
                             ALU.mult, ALU.add))
        step(v.tensor_scalar(scales[:, 2:4].bitcast(I32), bits, float(-(SCALE_BITS << 23)), None, ALU.add))

    def turn(self, pe):
        t, g = self.nc.tensor, self.g
        pe.wait_ge(self.own_ready, 1)
        for k in range(2):
            last = t.transpose(self.bank[0][0:1, k * P:(k + 1) * P], self.own[:, k:k + 1], g.ident_f[:])
        last.then_inc(self.turned, 1)

    def spread_out(self, pe):
        t, g = self.nc.tensor, self.g
        pe.wait_ge(self.top_ready, 1)
        t.matmul(self.bank[1][:, 0:2], g.ones[0:1, :], self.top[:], start=True, stop=True).then_inc(self.spread, 1)


def row_product(nc, g, name, panels, operand, out, prelude, post, post_steps, sums=None, opening=None,
                before_second=None, squares=None, roots=None, prefetch=None):
    cols = 2 * D + (1 if sums is not None else 0)
    HT = T // 2
    with ExitStack() as ctx:
        panel, loaded = panels.buf, panels.loaded
        acc = [psum(nc, ctx, f"{name}_acc{i}", [P, PT, 256], F32) for i in range(2)]
        half_used, acc_read, summed, operand_ready = (
            g.sem(f"{name}_{s}") for s in ("half_used", "acc_read", "summed", "operand_ready"))
        rounds = NPANEL // 2
        banks = [acc[1][:, 2 * i:2 * i + 2, :].rearrange("p q c -> p (q c)") for i in range(2)]
        with nc.Block() as block:
            @block.sync
            def _(sp):
                with sp.Fori(1, rounds) as r:
                    for i in range(4):
                        sp.wait_ge(half_used, r * 4 + (i - 3))
                        g.carry(sp)
                        panels.load(r, i)
                if prefetch:
                    prefetch.first()

            @block.tensor
            def _(pe):
                def round_(r, first):
                    for i in range(4):
                        a, half = acc[i // 2], i % 2
                        pe.wait_ge(loaded[i], (r + 1) * 16)
                        if half == 0 and not first:
                            pe.wait_ge(acc_read, r * 2 + (i // 2 - 1))
                        if first and i == 2 and before_second:
                            before_second(pe)
                        g.carry(pe)
                        for t in range(HT):
                            tt = half * HT + t
                            if first and i < 2 and tt % (T // 4) == 0:
                                pe.wait_ge(operand_ready, tt // (T // 4) + 1)
                            for q in range(PT):
                                b, e = divmod(q, 2)
                                lhs = panel[i][:, t, 256 * b + e:256 * b + 256:2].bitcast(FP8)
                                last = nc.tensor.matmul(a[:, q, 0:cols], lhs, operand[:, tt, 0:cols],
                                                        start=(tt == 0 and e == 0), stop=(tt == T - 1),
                                                        skip_group_check=True)
                        last.then_inc(half_used, 1)
                if opening:
                    opening(pe, banks)
                round_(0, True)
                with pe.Fori(1, rounds) as r:
                    round_(r, False)

            @block.vector
            def _(dve):
                prelude(dve, operand_ready)
                with dve.Fori(0, rounds) as r:
                    for k in range(2):
                        per_panel = post_steps + (1 if sums is not None else 0)
                        step = LoopChain(dve, summed, r * (2 * per_panel) + k * per_panel)
                        dve.wait_ge(half_used, r * 4 + (2 * k + 2))
                        tiles = bass.ds((r * 2 + k) * PT, PT)
                        if sums is not None:
                            step(nc.vector.tensor_scalar(sums[:, tiles], acc[k][:, :, 2 * D], INV, None, ALU.mult))
                        nc.vector.tensor_reduce(out[:, tiles, :], acc[k][:, :, 0:2 * D]
                                                .rearrange("p q (s d) -> p q d s", s=2),
                                                AX.X, ALU.add).then_inc(acc_read, 1)
                        dve.wait_ge(acc_read, r * 2 + (k + 1))
                        post(step, tiles)
                        assert step.n == per_panel

            if roots:
                @block.scalar
                def _(act):
                    roots(act, banks)

            if squares:
                @block.gpsimd
                def _(pool):
                    squares(pool)


def image_product(nc, g, name, images, out, operand, scale, plus=None, prelude=None,
                  highs=None):
    cols = 2 * D
    with ExitStack() as ctx:
        img, loaded = images.buf, images.loaded
        acc = [psum(nc, ctx, f"{name}_acc{i}", [P, 512], F32) for i in range(4)]
        raw = sbuf(nc, ctx, f"{name}_raw", [P, 4, D], F32)
        acc_ready, acc_read, scaled, operand_ready = (
            g.sem(f"{name}_{s}") for s in ("acc_ready", "acc_read", "scaled", "operand_ready"))
        rounds = T // 4
        with nc.Block() as block:
            @block.sync
            def _(sp):
                with sp.Fori(1, rounds) as r:
                    for i in range(4):
                        sp.wait_ge(acc_ready, r * 4 + (i - 3))
                        g.carry(sp)
                        images.load(r, i)

            @block.tensor
            def _(pe):
                def round_(r, first):
                    for i in range(4):
                        pe.wait_ge(loaded[i], (r + 1) * 16)
                        if not first:
                            pe.wait_ge(acc_read, r * 4 + (i - 3))
                        g.carry(pe)
                        if first and i == 0 and prelude:
                            last = image_matmuls(nc, img[i], acc[i][:, 0:cols], operand, cols,
                                                 lambda quarter: pe.wait_ge(operand_ready, quarter + 1))
                        else:
                            last = image_matmuls(nc, img[i], acc[i][:, 0:cols], operand, cols)
                        last.then_inc(acc_ready, 1)
                round_(0, True)
                with pe.Fori(1, rounds) as r:
                    round_(r, False)

            if highs:
                @block.scalar
                def _(act):
                    highs(act)

            @block.vector
            def _(dve):
                if prelude:
                    prelude(dve, operand_ready)

                def round_(r, first=False):
                    for i in range(4):
                        dve.wait_ge(acc_ready, r * 4 + (i + 1))
                        if not first:
                            dve.wait_ge(scaled, r * 4 + (i - 3))
                        nc.vector.tensor_reduce(raw[:, i, :], acc[i][:, 0:cols].rearrange("p (s d) -> p d s", s=2),
                                                AX.X, ALU.add).then_inc(acc_read, 1)
                        dve.wait_ge(acc_read, r * 4 + (i + 1))
                        tile = bass.ds(r * 4 + i, 1)
                        to = out[:, tile, :].rearrange("p t d -> p (t d)")
                        if plus is None:
                            last = nc.vector.tensor_scalar(to, raw[:, i, :], scale[:, tile], None, ALU.mult)
                        else:
                            last = nc.vector.scalar_tensor_tensor(
                                out=to, in0=raw[:, i, :], scalar=scale[:, tile],
                                in1=plus[:, tile, :].rearrange("p t d -> p (t d)"), op0=ALU.mult, op1=ALU.add)
                        last.then_inc(scaled, 1)
                round_(0, True)
                with dve.Fori(1, rounds) as r:
                    round_(r)


def image_matmuls(nc, img, acc, operand, cols, await_quarter=None):
    view = img[:].rearrange("c (b i e) -> c b i e", i=P, e=2)
    for t in range(T):
        if await_quarter and t % (T // 4) == 0:
            await_quarter(t // (T // 4))
        last = nc.tensor.matmul(acc, view[:, t // 2, :, t % 2].bitcast(FP8), operand[:, t, 0:cols],
                                start=(t == 0), stop=(t == T - 1))
    return last


def flip_pairs(nc, g, rows, bank):
    pairs = rows.bitcast(BF16)
    for b in range(NB):
        last = nc.tensor.transpose(bank[:, b * P:(b + 1) * P], pairs[:, b * P:(b + 1) * P], g.ident_b[:])
    return last


def constants(nc, g, ins, prefetch):
    with ExitStack() as ctx:
        work = sbuf(nc, ctx, "const_work", [P, 3, P], F32)
        loaded, zeroed, shaped = (g.sem(f"const_{s}") for s in ("loaded", "zeroed", "shaped"))
        w0 = ins["L0_gnn_W"]
        x_tiles = ins["x"].rearrange("(t p) d -> p t d", p=P)
        loads = [(g.x[:, h:h + T // 2, :], x_tiles[:, h:h + T // 2, :]) for h in (0, T // 2)]
        loads += [
            (g.w0_rows[:], w0),
            (g.w_prep[0:D, 0:D], ins["L1_gnn_W"]), (g.w_prep[0:D, D:2 * D], ins["L1_gnn_Wv"]),
            (g.w_prep[0:D, 2 * D:3 * D], ins["L1_gnn_Wq"]),
            (g.w_prep[D:D + 1, D:2 * D], ins["L1_gnn_bv"].unsqueeze(0)),
            (g.w_prep[D:D + 1, 2 * D:3 * D], ins["L1_gnn_bq"].unsqueeze(0)),
            (g.theta[:], ins["L1_gnn_Theta"]),
            (g.w2[0:D, :], ins["L2_gnn_W"]), (g.w2[D:D + 1, :], ins["L2_gnn_b"].unsqueeze(0)),
            (g.w3[0:D, :], ins["L3_gnn_weight"]), (g.w3[D:D + 1, :], ins["L3_gnn_bias"].unsqueeze(0)),
        ]
        flipped = psum(nc, ctx, "const_flipped", [P, D], F32)
        w0_flipped = g.sem("const_w0_flipped")
        ident_ready = g.sem("const_ident_ready")
        with nc.Block() as block:
            @block.sync
            def _(sp):
                for to, frm in loads:
                    nc.sync.dma_start(to, frm).then_inc(loaded, 16)
                prefetch.first()

            @block.gpsimd
            def _(pool):
                nc.gpsimd.memset(work[:], 0.0).then_inc(zeroed, 1)
                pool.wait_ge(zeroed, 1)
                nc.gpsimd.affine_select(out=work[:, 0, :], in_=work[:, 0, :], compare_op=ALU.not_equal, fill=1.0,
                                        base=0, pattern=[[-1, P]], channel_multiplier=1).then_inc(shaped, 1)
                nc.gpsimd.affine_select(out=work[:, 1, :], in_=work[:, 1, :], compare_op=ALU.is_ge, fill=1.0,
                                        base=0, pattern=[[1, P]], channel_multiplier=-1).then_inc(shaped, 1)

            @block.tensor
            def _(pe):
                pe.wait_ge(loaded, 16 * len(loads))
                pe.wait_ge(ident_ready, 1)
                nc.tensor.transpose(flipped[:], g.w0_rows[:], g.ident_f[0:D, 0:D]).then_inc(w0_flipped, 1)

            @block.vector
            def _(dve):
                v, step = nc.vector, Chain(dve, g)
                step(v.memset(g.w_prep[D:D + 1, 0:D], 0.0))
                dve.wait_ge(shaped, 2)
                eye, low = work[:, 0, :], work[:, 1, :]
                v.tensor_copy(g.ident_f[:], eye).then_inc(ident_ready, 1)
                step(v.tensor_copy(g.ident_b[:], eye))
                step(v.tensor_copy(g.ident_h[:], eye))
                step(v.tensor_scalar(g.mask_off[:], eye, -MASK_OFF, None, ALU.mult))
                step(v.memset(g.byte_one[:], BYTE))
                step(v.memset(g.ones[:], 1.0))
                step(v.memset(g.operand[:, :, 2 * D:2 * D + 1], 1.0))
                count, unit = g.count, -BF16_STEP * INV
                step(v.tensor_scalar(work[:, 2, :], eye, -KEEP, None, ALU.mult))
                step(v.tensor_tensor(work[:, 2, :], low, work[:, 2, :], ALU.add))
                step(v.tensor_scalar(count[:, 0, :], work[:, 2, :], unit, None, ALU.mult))
                step(v.tensor_scalar(count[:, 1, :], work[:, 2, :], -unit, unit, ALU.mult, ALU.add))
                dve.wait_ge(w0_flipped, 1)
                step(v.tensor_copy(g.w0[:], flipped[:]))
                dve.wait_ge(loaded, 16 * len(loads))
                step(v.tensor_scalar(g.w3[0:D, :], g.w3[0:D, :], W_UP / X_SCALE, None, ALU.mult))


def neighbour_layer(nc, g, tiles):
    cols = 3 * D + 1
    with ExitStack() as ctx:
        parts = sbuf(nc, ctx, "nb_parts", [P, T, cols + 7], BF16)
        wide = sbuf(nc, ctx, "nb_wide", [P, T, 2 * D], F32)
        rest = sbuf(nc, ctx, "nb_rest", [P, T, D], F32)
        inv, deg_floor = (sbuf(nc, ctx, f"nb_{n}", [P, T], F32) for n in ("inv", "deg_floor"))
        with nc.Block() as block:
            @block.vector
            def _(dve):
                step = Chain(dve, g)
                split3(nc.vector, step, parts, (1, 2, 0), g.x[:], rest[:])
                step(nc.vector.memset(parts[:, :, 3 * D:cols], 1.0))
                step(nc.vector.tensor_copy(wide[:, :, 0:D], g.x[:]))

        with ExitStack() as inner:
            raw, loaded = tiles.buf, tiles.loaded
            byte = [sbuf(nc, inner, f"nb_byte{i}", [P, N], U8) for i in range(4)]
            img = [sbuf(nc, inner, f"nb_img{i}", [P, N], U8) for i in range(4)]
            bank = [psum(nc, inner, f"nb_bank{i}", [P, HALF], BF16) for i in range(2)]
            acc = [psum(nc, inner, f"nb_acc{i}", [P, 512], F32) for i in range(4)]
            rows_kept = [g.sem(f"nb_rows_kept{i}") for i in range(4)]
            imgs_kept = [g.sem(f"nb_imgs_kept{i}") for i in range(4)]
            byte_ready, flipped, img_ready, acc_ready, acc_read = (
                g.sem(f"nb_{s}") for s in ("byte_ready", "flipped", "img_ready", "acc_ready", "acc_read"))
            rounds = T // 4
            with nc.Block() as block:
                @block.sync
                def _(sp):
                    with sp.Fori(1, rounds) as r:
                        for i in range(4):
                            sp.wait_ge(byte_ready, r * 4 + (i - 3))
                            tiles.load(r, i)

                def reduce(nc, g, t, a):
                    tile = bass.ds(t, 1)
                    nc.vector.tensor_scalar(g.deg[:, tile], a[:, 3 * D:cols], INV, None, ALU.mult)
                    return nc.vector.tensor_reduce(g.prod[:, tile, :].rearrange("p t d -> p (t d)"),
                                                   a[:, 0:3 * D].rearrange("p (s d) -> p d s", s=3), AX.X, ALU.add)

                @block.vector
                def _(dve):
                    def to_bytes(r, i, first=False):
                        dve.wait_ge(loaded[i], (r + 1) * 16)
                        if not first:
                            dve.wait_ge(flipped, r * 4 + (i - 3))
                            dve.wait_ge(rows_kept[i], r * 16)
                        nc.vector.tensor_scalar(byte[i][:].rearrange("p (b c e) -> p b e c", c=P, e=2),
                                                raw[i][:].rearrange("p (b e c) -> p b e c", c=P, e=2),
                                                BYTE, None, ALU.mult).then_inc(byte_ready, 1)
                    for i in range(4):
                        to_bytes(0, i, True)
                    with dve.Fori(1, rounds) as r:
                        for i in range(4):
                            to_bytes(r, i)
                            dve.wait_ge(acc_ready, r * 4 + (i - 3))
                            reduce(nc, g, r * 4 + (i - 4), acc[i]).then_inc(acc_read, 1)
                    for i in range(4):
                        dve.wait_ge(acc_ready, T - 3 + i)
                        reduce(nc, g, T - 4 + i, acc[i]).then_inc(acc_read, 1)

                def last_of_round(pe, r):
                    pe.wait_ge(img_ready, r * 4)
                    if not (isinstance(r, int) and r == 1):
                        pe.wait_ge(acc_read, r * 4 - 4)
                    g.carry(pe)
                    image_matmuls(nc, img[3], acc[3][:, 0:cols], parts, cols).then_inc(acc_ready, 1)

                @block.tensor
                def _(pe):
                    def flip(r, i, first=False):
                        pe.wait_ge(byte_ready, r * 4 + (i + 1))
                        if not (first and i < 2):
                            pe.wait_ge(img_ready, r * 4 + (i - 1))
                        flip_pairs(nc, g, byte[i][:], bank[i % 2][:]).then_inc(flipped, 1)

                    def product(r, i, first=False):
                        pe.wait_ge(img_ready, r * 4 + (i + 1))
                        if not first:
                            pe.wait_ge(acc_read, r * 4 + (i - 3))
                        g.carry(pe)
                        image_matmuls(nc, img[i], acc[i][:, 0:cols], parts, cols).then_inc(acc_ready, 1)

                    flip(0, 0, True)
                    for i in range(1, 4):
                        flip(0, i, True)
                        product(0, i - 1, True)

                    def round_(r):
                        flip(r, 0)
                        last_of_round(pe, r)
                        for i in range(1, 4):
                            flip(r, i)
                            product(r, i - 1)
                    round_(1)
                    with pe.Fori(2, rounds) as r:
                        round_(r)
                    last_of_round(pe, rounds)

                @block.scalar
                def _(act):
                    def to_image(r, i, first=False):
                        act.wait_ge(flipped, r * 4 + (i + 1))
                        if not first:
                            act.wait_ge(acc_ready, r * 4 + (i - 3))
                            act.wait_ge(imgs_kept[i], r * 16)
                        nc.scalar.copy(img[i][:].bitcast(U16), bank[i % 2][:].bitcast(U16)).then_inc(img_ready, 1)
                    for i in range(4):
                        to_image(0, i, True)
                    with act.Fori(1, rounds) as r:
                        for i in range(4):
                            to_image(r, i)

                @block.gpsimd
                def _(pool):
                    with pool.Fori(0, rounds) as r:
                        for i in range(4):
                            to = bass.ds(r * 4 + i, 1)
                            pool.wait_ge(byte_ready, r * 4 + (i + 1))
                            g.carry(pool)
                            nc.gpsimd.dma_start(g.rows[to, :, :].rearrange("t p j -> (t p) j"),
                                                byte[i][:]).then_inc(rows_kept[i], 16)
                            pool.wait_ge(img_ready, r * 4 + (i + 1))
                            g.carry(pool)
                            nc.gpsimd.dma_start(g.images[to, :, :].rearrange("t p j -> (t p) j"),
                                                img[i][:]).then_inc(imgs_kept[i], 16)
                    for i in range(4):
                        pool.wait_ge(rows_kept[i], rounds * 16)
                        pool.wait_ge(imgs_kept[i], rounds * 16)

        floor_ready, root_ready = g.sem("nb_floor_ready"), g.sem("nb_root_ready")
        with nc.Block() as block:
            @block.vector
            def _(dve):
                v, step = nc.vector, Chain(dve, g)
                v.tensor_scalar(deg_floor[:], g.deg[:], 1.0, None, ALU.max).then_inc(floor_ready, 1)
                step(v.tensor_scalar(g.others[:], g.deg[:], -1.0, float(N), ALU.mult, ALU.add))
                dve.wait_ge(floor_ready, 1)
                step(v.reciprocal(inv[:], deg_floor[:]))
                step(v.tensor_scalar(inv[:], inv[:], INV, None, ALU.mult))
                step(v.tensor_tensor(wide[:, :, D:2 * D], g.prod[:], per_node(inv[:]), ALU.mult))
                dve.wait_ge(root_ready, 1)
                step(v.reciprocal(g.sum_scale[:], g.sum_scale[:]))
                step(v.tensor_scalar(g.sum_scale[:], g.sum_scale[:], -INV / X_SCALE, None, ALU.mult))

            @block.scalar
            def _(act):
                act.wait_ge(floor_ready, 1)
                nc.scalar.activation(g.sum_scale[:], deg_floor[:], ACT.Sqrt).then_inc(root_ready, 1)
        linear(nc, g, "nb_out", wide, 2 * D, g.w0[:], D, None, relu=True, norm=True)


def attention_scores(nc, g, name, theta):
    with ExitStack() as ctx:
        q_hm, q_lh, f_hh, f_mm, f_hl = g.stacks
        weighted = sbuf(nc, ctx, f"{name}_weighted", [P, N], F32)
        score = [sbuf(nc, ctx, f"{name}_score{i}", [P, N], F32) for i in range(2)]
        row = [sbuf(nc, ctx, f"{name}_row{i}", [P, N], U8) for i in range(2)]
        share = [sbuf(nc, ctx, f"{name}_share{i}", [P, N - DVE_COLS], F32) for i in range(2)]
        top = sbuf(nc, ctx, f"{name}_top", [P, 2, 4], F32)
        total = sbuf(nc, ctx, f"{name}_total", [P, 2, 2], F32)
        loaded = [g.sem(f"{name}_loaded{i}") for i in range(2)]
        raw_ready, masked, shift_ready, exp_ready, weight_ready, weighted_step, share_ready, share_added = (
            g.sem(f"{name}_{s}") for s in ("raw_ready", "masked", "shift_ready", "exp_ready", "weight_ready",
                                           "weighted_step", "share_ready", "share_added"))
        with ExitStack() as inner:
            raw = [psum(nc, inner, f"{name}_raw{i}", [P, HALF], F32) for i in range(2)]
            softmax = SoftmaxKeep(nc, g, ctx, f"{name}_comp", g.logit[:], theta, g.keep[:],
                                  bank=[raw[0][:, 512:1024], raw[1][:, 0:512]])
            sums_turned = g.sem(f"{name}_sums_turned")

            def turned(i):
                return raw[i // 4][:, i % 4 * 512:(i % 4 + 1) * 512]
            rounds = T // 2
            with nc.Block() as block:
                @block.sync
                def _(sp):
                    def load(r, e):
                        nc.sync.dma_start(row[e][:], g.rows[bass.ds(r * 2 + e, 1), :, :]
                                          .rearrange("t p j -> (t p) j")).then_inc(loaded[e], 16)
                    load(0, 0)
                    load(0, 1)
                    with sp.Fori(1, rounds) as r:
                        for e in range(2):
                            sp.wait_ge(masked, r * 4 + (2 * e - 2))
                            load(r, e)

                @block.tensor
                def _(pe):
                    def products(r, e, first=False):
                        cols = bass.ds((r * 2 + e) * P, P)
                        for half in range(2):
                            if not (first and e == 0):
                                pe.wait_ge(masked, r * 4 + (2 * e + half - 1))
                            for lhs, rhs, kind in ((q_hm, f_hh, 0), (q_hm, f_mm, 1), (q_lh, f_hl, 2)):
                                for c in range(4):
                                    j = half * HALF + c * 512
                                    last = nc.tensor.matmul(raw[half][:, c * 512:(c + 1) * 512],
                                                            lhs[:, cols], rhs[:, j:j + 512],
                                                            start=(kind == 0), stop=(kind == 2))
                            last.then_inc(raw_ready, 1)
                    products(0, 0, True)
                    products(0, 1, True)
                    with pe.Fori(1, rounds) as r:
                        products(r, 0)
                        products(r, 1)
                    pe.wait_ge(masked, 2 * T)
                    pe.wait_ge(weighted_step, T + 1)
                    for t in range(T):
                        b, e = divmod(t, 2)
                        if t == DVE_COLS // P:
                            pe.wait_ge(share_added, T + 1)
                            pe.wait_ge(weighted_step, T + 2)
                        last = nc.tensor.transpose(turned(t // 4)[:, t % 4 * P:(t % 4 + 1) * P],
                                                   weighted[:, 256 * b + e:256 * b + 256:2], g.ident_f[:])
                        if t % 4 == 3:
                            last.then_inc(sums_turned, 1)
                    softmax.tensor(pe)

                @block.vector
                def _(dve):
                    v = nc.vector

                    def mask(r, e, half):
                        dve.wait_ge(raw_ready, r * 4 + (2 * e + half + 1))
                        if half == 0:
                            dve.wait_ge(loaded[e], (r + 1) * 16)
                            if not (isinstance(r, int) and r == 0):
                                dve.wait_ge(weighted_step, r * 2 + e)
                                dve.wait_ge(share_ready, r * 2 + (e - 1))
                        j = half * HALF
                        g.carry(dve)
                        v.tensor_tensor_reduce(score[e][:, j:j + HALF], raw[half][:], row[e][:, j:j + HALF],
                                               D ** -0.5 * INV / BYTE, -3.0e38, ALU.mult, ALU.max,
                                               top[:, e, half:half + 1]).then_inc(masked, 1)

                    def negate(r, e):
                        dve.wait_ge(masked, r * 4 + (2 * e + 2))
                        v.tensor_scalar(top[:, e, 3:4], top[:, e, 0:1], top[:, e, 1:2], -1.0,
                                        ALU.max, ALU.mult).then_inc(shift_ready, 1)

                    def invert(r, e, back=0):
                        par = (e - back) % 2
                        dve.wait_ge(exp_ready, r * 2 + (e + 1 - back))
                        v.reciprocal(total[:, par, 1:2], total[:, par, 0:1]).then_inc(weight_ready, 1)

                    def weigh(r, e, back=0):
                        par = (e - back) % 2
                        dve.wait_ge(weight_ready, r * 2 + (e + 1 - back))
                        dve.wait_ge(weighted_step, r * 2 + (e + 1 - back))
                        v.scalar_tensor_tensor(out=weighted[:, 0:DVE_COLS], in0=score[par][:, 0:DVE_COLS],
                                               scalar=total[:, par, 1:2], in1=weighted[:, 0:DVE_COLS],
                                               op0=ALU.mult, op1=ALU.add).then_inc(weighted_step, 1)

                    def tile(r, e):
                        mask(r, e, 0)
                        invert(r, e, 1)
                        mask(r, e, 1)
                        negate(r, e)
                        weigh(r, e, 1)

                    v.memset(weighted[:, 0:DVE_COLS], 0.0).then_inc(weighted_step, 1)
                    dve.wait_ge(weighted_step, 1)
                    mask(0, 0, 0)
                    mask(0, 0, 1)
                    negate(0, 0)
                    tile(0, 1)
                    with dve.Fori(1, rounds) as r:
                        tile(r, 0)
                        tile(r, 1)
                    invert(rounds - 1, 1)
                    weigh(rounds - 1, 1)
                    dve.wait_ge(share_ready, T)
                    dve.wait_ge(share_added, T)
                    own = slice(DVE_COLS, LAST_SPLIT)
                    v.tensor_tensor(weighted[:, own], share[1][:, 0:LAST_SPLIT - DVE_COLS], weighted[:, own],
                                    ALU.add).then_inc(weighted_step, 1)
                    step = Chain(dve, g)
                    for i in range(T // 4):
                        dve.wait_ge(sums_turned, i + 1)
                        step(v.tensor_reduce(g.logit[:, 4 * i:4 * i + 4],
                                             turned(i).rearrange("p (t n) -> p t n", n=P), AX.X, ALU.add))
                    step(v.scalar_tensor_tensor(out=g.logit[:], in0=g.logit[:], scalar=0.5 / N,
                                                in1=g.structural[:], op0=ALU.mult, op1=ALU.add))
                    softmax.vector(dve, step)
                    step(v.tensor_tensor(g.norm[:], g.norm[:], g.keep[:], ALU.mult))
                    step(v.tensor_scalar(g.norm[:], g.norm[:], SAFE ** 0.5, None, ALU.max))
                    step(v.tensor_scalar(g.never[:], g.keep[:], -1.0e30, 1.0e30, ALU.mult, ALU.add))

                @block.scalar
                def _(act):
                    def exps(r, e):
                        act.wait_ge(shift_ready, r * 2 + (e + 1))
                        nc.scalar.activation(score[e][:], score[e][:], ACT.Exp, bias=top[:, e, 3:4],
                                             accum_out=total[:, e, 0:1]).then_inc(exp_ready, 1)

                    def shares(r, e, back=0, first=False):
                        par = (e - back) % 2
                        act.wait_ge(weight_ready, r * 2 + (e + 1 - back))
                        if not first:
                            act.wait_ge(share_added, r * 2 + (e - back))
                        nc.scalar.activation(share[par][:], score[par][:, DVE_COLS:], ACT.Copy,
                                             scale=total[:, par, 1:2]).then_inc(share_ready, 1)
                    exps(0, 0)
                    shares(0, 1, 1, first=True)
                    exps(0, 1)
                    shares(1, 0, 1, first=True)
                    exps(1, 0)
                    shares(1, 1, 1)
                    exps(1, 1)
                    with act.Fori(2, rounds) as r:
                        for e in range(2):
                            shares(r, e, 1)
                            exps(r, e)
                    shares(rounds - 1, 1)
                    softmax.scalar(act)

                @block.gpsimd
                def _(pool):
                    last_cols = weighted[:, DVE_COLS:]
                    nc.gpsimd.memset(last_cols, 0.0).then_inc(share_added, 1)

                    def add(r, e, skip=0):
                        pool.wait_ge(share_ready, r * 2 + (e + 1))
                        pool.wait_ge(share_added, r * 2 + (e + 1))
                        nc.gpsimd.tensor_tensor(last_cols[:, skip:], share[e][:, skip:], last_cols[:, skip:],
                                                ALU.add).then_inc(share_added, 1)
                    with pool.Fori(0, rounds - 1) as r:
                        add(r, 0)
                        add(r, 1)
                    add(rounds - 1, 0)
                    add(rounds - 1, 1, LAST_SPLIT - DVE_COLS)


def prune_edges(nc, g, name, theta):
    with ExitStack() as ctx:
        u_hl = sbuf(nc, ctx, f"{name}_u_hl", [P, N], F16)
        u_hh = sbuf(nc, ctx, f"{name}_u_hh", [P, N], F16)
        u_ll = sbuf(nc, ctx, f"{name}_u_ll", [P, N], F16)
        rows_in = Loads(nc, g, ctx, f"{name}_row", [P, N], U8, 2,
                        lambda r, e: g.rows[bass.ds(r * 2 + e, 1), :, :].rearrange("t p j -> (t p) j"))
        row, loaded = rows_in.buf, rows_in.loaded
        masked = g.sem(f"{name}_masked")

        def mask_and_double(dve, step, k, made):
            v, t = nc.vector, slice(k * 8, (k + 1) * 8)
            v.tensor_tensor(g.unit[:, t, :], g.unit[:, t, :], per_node(g.keep[:, t], 2 * D),
                            ALU.mult).then_inc(masked, 1)
            dve.wait_ge(masked, k + 1)
            step(v.tensor_copy(g.units[:, t, 0:D], g.unit[:, t, 0:D]))
            v.tensor_copy(g.units[:, t, D:2 * D], g.unit[:, t, 0:D]).then_inc(made, 1)

        def double(act, k, made):
            t = slice(k * 8, (k + 1) * 8)
            act.wait_ge(masked, k + 1)
            nc.scalar.copy(g.units[:, t, 2 * D:3 * D], g.unit[:, t, D:2 * D]).then_inc(doubled, 1)
            nc.scalar.copy(g.units[:, t, 3 * D:4 * D], g.unit[:, t, D:2 * D]).then_inc(doubled, 1)
            act.wait_ge(doubled, 2 * k + 2)
            act.sem_inc(made, 1)
        doubled = g.sem(f"{name}_doubled")
        away = [sbuf(nc, ctx, f"{name}_away{i}", [P, N], U8) for i in range(2)]
        away_ready = g.sem(f"{name}_away_ready")

        def turn(pool, e):
            nc.gpsimd.tensor_scalar(away[e][:].bitcast(U16), row[e][:].bitcast(U16), -1.0, BYTE * 257.0,
                                    ALU.mult, ALU.add).then_inc(away_ready, 1)

        def first_turns(pool):
            for e in range(2):
                pool.wait_ge(loaded[e], 16)
                turn(pool, e)
        build_stacks(nc, g, f"{name}_stacks", [
            (lambda t: g.unit[:, t, :], u_hl, False),
            (lambda t: g.units[:, t, 0:2 * D], u_hh, True),
            (lambda t: g.units[:, t, 2 * D:4 * D], u_ll, True)], F16, g.ident_h[:], prefetch=rows_in,
            dve_make=mask_and_double, act_make=double, pool_first=first_turns)

        e_cos = [sbuf(nc, ctx, f"{name}_e_cos{i}", [P, N], F32) for i in range(2)]
        kept = [sbuf(nc, ctx, f"{name}_kept{i}", [P, N], U8) for i in range(2)]
        img = [sbuf(nc, ctx, f"{name}_img{i}", [P, N], U8) for i in range(2)]
        weight = sbuf(nc, ctx, f"{name}_weight", [P, 2, 8], F32)
        cos = [psum(nc, ctx, f"{name}_cos{i}", [P, 1024], F32) for i in range(2)]
        bank = [psum(nc, ctx, f"{name}_bank{i}", [P, HALF], BF16) for i in range(2)]
        rows_kept, imgs_kept = ([g.sem(f"{name}_{s}{i}") for i in range(2)] for s in ("rows_kept", "imgs_kept"))
        g.rows_kept, g.imgs_kept = rows_kept, imgs_kept
        cos_ready, exp_ready, thr_step, kept_ready, flipped, img_dve, img_act = (
            g.sem(f"{name}_{s}") for s in ("cos_ready", "exp_ready", "thr_step", "kept_ready",
                                           "flipped", "img_dve", "img_act"))
        rounds = T // 2
        with nc.Block() as block:
            @block.sync
            def _(sp):
                def keep_rows(t, e, n):
                    sp.wait_ge(kept_ready, n)
                    g.carry(sp)
                    nc.sync.dma_start(g.kept_rows[bass.ds(t, 1), :, :].rearrange("t p j -> (t p) j"),
                                      kept[e][:]).then_inc(rows_kept[e], 16)

                def keep_image(t, e, n):
                    sp.wait_ge(img_dve, n)
                    sp.wait_ge(img_act, n)
                    g.carry(sp)
                    nc.sync.dma_start(g.kept_images[bass.ds(t, 1), :, :].rearrange("t p j -> (t p) j"),
                                      img[e][:]).then_inc(imgs_kept[e], 16)
                def next_row(r, e):
                    sp.wait_ge(away_ready, r * 2 + e)
                    g.carry(sp)
                    rows_in.load(r + e, 1 - e)

                def keep(r, e, image=True):
                    keep_rows(r * 2 + (e - 2), e, r * 2 + (e - 1))
                    if image:
                        keep_image(r * 2 + (e - 3), 1 - e, r * 2 + (e - 2))
                next_row(0, 1)
                next_row(1, 0)
                keep(1, 0, image=False)
                next_row(1, 1)
                keep(1, 1)
                with sp.Fori(2, rounds - 1) as r:
                    for e in range(2):
                        next_row(r, e)
                        keep(r, e)
                next_row(rounds - 1, 0)
                keep(rounds - 1, 0)
                keep(rounds - 1, 1)
                keep_rows(T - 2, 0, T - 1)
                keep_image(T - 3, 1, T - 2)
                keep_rows(T - 1, 1, T)
                keep_image(T - 2, 0, T - 1)
                keep_image(T - 1, 1, T)

            @block.gpsimd
            def _(pool):
                with pool.Fori(1, rounds) as r:
                    for e in range(2):
                        pool.wait_ge(loaded[e], (r + 1) * 16)
                        pool.wait_ge(cos_ready, r * 8 + (4 * e - 4))
                        g.carry(pool)
                        turn(pool, e)

            @block.tensor
            def _(pe):
                def cosines(r, e, first=False):
                    cols = bass.ds((r * 2 + e) * P, P)
                    pe.wait_ge(away_ready, r * 2 + (e + 1))
                    for k in range(4):
                        if not (first and e == 0 and k < 2):
                            pe.wait_ge(exp_ready, r * 8 + (4 * e + k - 1))
                        g.carry(pe)
                        for lhs, rhs, kind in ((g.mask_off, None, 0), (u_hl, u_hh, 1), (u_hl, u_ll, 2)):
                            for c in range(2):
                                j = k * 1024 + c * 512
                                mov = rhs[:, j:j + 512] if kind else away[e][:, j:j + 512].bitcast(FP8)
                                last = nc.tensor.matmul(cos[k % 2][:, c * 512:(c + 1) * 512],
                                                        lhs[:, cols] if kind else lhs[:], mov,
                                                        start=(kind == 0), stop=(kind == 2))
                        last.then_inc(cos_ready, 1)

                def flip(par, n):
                    pe.wait_ge(kept_ready, n)
                    if not (isinstance(n, int) and n <= 2):
                        pe.wait_ge(img_dve, n - 2)
                        pe.wait_ge(img_act, n - 2)
                    g.carry(pe)
                    flip_pairs(nc, g, kept[par][:], bank[par][:]).then_inc(flipped, 1)

                cosines(0, 0, True)
                cosines(0, 1, True)
                for e in range(2):
                    cosines(1, e)
                    flip(e, 1 + e)
                with pe.Fori(2, rounds) as r:
                    for e in range(2):
                        cosines(r, e)
                        flip(e, r * 2 + (e - 1))
                flip(0, T - 1)
                flip(1, T)

            @block.scalar
            def _(act):
                def exps(r, e, first=False):
                    for k in range(4):
                        act.wait_ge(cos_ready, r * 8 + (4 * e + k + 1))
                        if k == 0 and not first:
                            act.wait_ge(kept_ready, r * 2 + (e - 1))
                        nc.scalar.activation(e_cos[e][:, k * 1024:(k + 1) * 1024], cos[k % 2][:], ACT.Exp,
                                             scale=COS_SCALE ** -2,
                                             accum_out=weight[:, e, k:k + 1]).then_inc(exp_ready, 1)

                def image(par, n, first=False):
                    act.wait_ge(flipped, n)
                    if not first:
                        act.wait_ge(imgs_kept[par], (n - 1 - par) * 8)
                    nc.scalar.copy(img[par][:, N // 2:].bitcast(U16),
                                   bank[par][:, HALF // 2:].bitcast(U16)).then_inc(img_act, 1)
                exps(0, 0, True)
                exps(0, 1, True)
                for e in range(2):
                    exps(1, e)
                    image(e, 1 + e, True)
                with act.Fori(2, rounds) as r:
                    for e in range(2):
                        exps(r, e)
                        image(e, r * 2 + (e - 1))
                image(0, T - 1)
                image(1, T)

            @block.vector
            def _(dve):
                v = nc.vector

                def compare(r, e, first=False):
                    tile = bass.ds(r * 2 + e, 1)
                    w = weight[:, e, :]
                    v.tensor_copy(w[:, 4:5], g.others[:, tile]).then_inc(thr_step, 1)
                    dve.wait_ge(thr_step, r * 6 + (3 * e + 1))
                    dve.wait_ge(exp_ready, r * 8 + (4 * e + 4))
                    v.tensor_reduce(w[:, 5:6], w[:, 0:5], AX.X, ALU.add).then_inc(thr_step, 1)
                    dve.wait_ge(thr_step, r * 6 + (3 * e + 2))
                    v.scalar_tensor_tensor(out=w[:, 6:7], in0=w[:, 5:6], scalar=theta, in1=g.never[:, tile],
                                           op0=ALU.mult, op1=ALU.add).then_inc(thr_step, 1)
                    dve.wait_ge(thr_step, r * 6 + (3 * e + 3))
                    if not first:
                        dve.wait_ge(flipped, r * 2 + (e - 1))
                        dve.wait_ge(rows_kept[e], r * 16)
                    v.scalar_tensor_tensor(out=kept[e][:], in0=e_cos[e][:], scalar=w[:, 6:7],
                                           in1=g.byte_one[:].broadcast_to([P, N]), op0=ALU.is_ge, op1=ALU.mult,
                                           accum_out=g.conn[:, tile]).then_inc(kept_ready, 1)

                def image(par, n, first=False):
                    dve.wait_ge(flipped, n)
                    if not first:
                        dve.wait_ge(imgs_kept[par], (n - 1 - par) * 8)
                    v.tensor_copy(img[par][:, 0:N // 2].bitcast(U16),
                                  bank[par][:, 0:HALF // 2].bitcast(U16)).then_inc(img_dve, 1)

                compare(0, 0, True)
                compare(0, 1, True)
                for e in range(2):
                    image(e, 1 + e, True)
                    compare(1, e)
                with dve.Fori(2, rounds) as r:
                    for e in range(2):
                        image(e, r * 2 + (e - 1))
                        compare(r, e)
                image(0, T - 1)
                image(1, T)


def pruned_layer(nc, g, name, src, theta):
    with ExitStack() as layer:
        g.xqv = sbuf(nc, layer, f"{name}_xqv_all", [P, T, 3 * D], F32)
        g.unit = sbuf(nc, layer, f"{name}_unit", [P, T, 2 * D], F16)
        g.units = sbuf(nc, layer, f"{name}_units", [P, T, 4 * D], F16)
        attention = layer.enter_context(ExitStack())
        g.stacks = [sbuf(nc, attention, f"{name}_stack_{n}", [P, N], BF16)
                    for n in ("q_hm", "q_lh", "f_hh", "f_mm", "f_hl")]
        with ExitStack() as ctx:
            g.qs = sbuf(nc, ctx, f"{name}_qs", [P, T, 3 * D], BF16)
            g.fs = sbuf(nc, ctx, f"{name}_fs", [P, T, 6 * D], BF16)
            maxima = sbuf(nc, ctx, f"{name}_maxima", [P, NPANEL, 2], F32)
            rest = sbuf(nc, ctx, f"{name}_rest", [P, PT, D], F32)
            sums = sbuf(nc, ctx, f"{name}_sums", [P, 2, T], F32)
            inv = sbuf(nc, ctx, f"{name}_inv", [P, T], F32)

            def maxima_and_q(step, tiles):
                step(nc.vector.tensor_reduce(maxima[:, tiles.start // PT, :], g.xqv[:, tiles, 0:2 * D]
                                             .rearrange("p t (s d) -> p s t d", s=2), AX.XY, ALU.max,
                                             apply_absolute_value=True))
                split3(nc.vector, step, g.qs[:, tiles, :], (1, 2, 0), g.xqv[:, tiles, 2 * D:3 * D], rest[:])
            panels = panel_loads(nc, g, ctx, f"{name}_panel", g.rows)
            linear(nc, g, f"{name}_xqv", src, D, g.w_prep[:], 3 * D, g.xqv, ones_row=True, post=maxima_and_q,
                   prefetch=panels)

            big = [g.units[:, :, i * 2 * D:(i + 1) * 2 * D].bitcast(F32) for i in range(2)]
            scaling = ctx.enter_context(ExitStack())
            scales = Scales(nc, g, scaling, f"{name}_scales", maxima[:])
            squared, squares_ready, roots_ready = (
                g.sem(f"{name}_{s}") for s in ("squared", "squares_ready", "roots_ready"))
            squares_of = (g.xqv[:, :, 0:D], src[:])

            def squares(pool):
                for k, a in enumerate(squares_of):
                    nc.gpsimd.tensor_tensor(big[k], a, a, ALU.mult).then_inc(squared, 1)

            def prelude(dve, operand_ready):
                v, step, Q4 = nc.vector, Chain(dve, g), T // 4
                scales.vector(dve, step)
                for k in range(4):
                    t = slice(k * Q4, (k + 1) * Q4)
                    split2(v, step, g.operand[:, t, :], g.xqv[:, t, D:2 * D], g.scales[:, 1:2],
                           operand_ready)
                for k in range(2):
                    dve.wait_ge(squared, k + 1)
                    step(v.tensor_reduce(sums[:, k, :], big[k], AX.X, ALU.add))
                    v.tensor_scalar(sums[:, k, :], sums[:, k, :], SAFE, None, ALU.max).then_inc(squares_ready, 1)
                dve.wait_ge(roots_ready, 2)
                step(v.tensor_scalar(g.structural[:], g.structural[:], 0.5, None, ALU.mult))
                step(v.tensor_scalar(inv[:], g.norm[:], 1e-8, None, ALU.max))
                step(v.reciprocal(inv[:], inv[:]))
                step(v.tensor_scalar(inv[:], inv[:], COS_SCALE, None, ALU.mult))
                step(v.tensor_tensor(big[0], src[:], per_node(inv[:]), ALU.mult))
                split2(v, step, g.unit, big[0])

            q_hm, q_lh, f_hh, f_mm, f_hl = g.stacks
            q_bank = [psum(nc, scaling, f"{name}_q_bank{i}", [P, 512], F32) for i in range(2)]
            q_flipped, q_copied = g.sem(f"{name}_q_flipped"), g.sem(f"{name}_q_copied")

            def q_group(i, banks):
                stack, first_slot, t0 = (q_hm, q_lh)[i // 4], (1, 0)[i // 4], i % 4 * 8
                to = (q_bank[0][:], q_bank[1][:], *banks)[i % 4].bitcast(BF16)
                return first_slot * D, t0, stack[:, t0 * P:(t0 + 8) * P], to

            def opening(pe, banks):
                scales.turn(pe)
                for i in range(8):
                    if i == 2:
                        scales.spread_out(pe)
                    col, t0, _, bank = q_group(i, banks)
                    if i >= 4:
                        pe.wait_ge(q_copied, i - 3)
                    for q in range(8):
                        last = nc.tensor.transpose(bank[:, q * P:(q + 1) * P], g.qs[:, t0 + q, col:col + 2 * D],
                                                   g.ident_b[:])
                    last.then_inc(q_flipped, 1)

            def roots(act, banks):
                for i in range(8):
                    _, _, to, bank = q_group(i, banks)
                    act.wait_ge(q_flipped, i + 1)
                    nc.scalar.copy(to, bank).then_inc(q_copied, 1)
                for k, to in enumerate((g.structural, g.norm)):
                    act.wait_ge(squares_ready, k + 1)
                    nc.scalar.activation(to[:], sums[:, k, :], ACT.Sqrt).then_inc(roots_ready, 1)

            def post(step, tiles):
                v, f = nc.vector, g.fs[:, tiles, :]
                step(v.tensor_scalar(g.prod[:, tiles, :], g.prod[:, tiles, :], g.scales[:, 3:4], None, ALU.mult))
                hi, mid, lo = (f[:, :, k * D:(k + 1) * D] for k in (0, 2, 5))
                step(v.tensor_copy(hi, g.prod[:, tiles, :]))
                step.unread(v.tensor_tensor(rest[:], g.prod[:, tiles, :], hi, ALU.subtract))
                step(v.tensor_copy(f[:, :, D:2 * D], hi))
                step.unread(v.tensor_copy(mid, rest[:]))
                step(v.tensor_copy(f[:, :, 4 * D:5 * D], hi))
                step.unread(v.tensor_copy(f[:, :, 3 * D:4 * D], mid))
                step(v.tensor_tensor(lo, rest[:], mid, ALU.subtract))

            row_product(nc, g, f"{name}_ef", panels, g.operand, g.prod, prelude, post, 8,
                        opening=opening, before_second=lambda pe: pe.wait_ge(q_copied, 8),
                        squares=squares, roots=roots)
            scaling.close()
            build_stacks(nc, g, f"{name}_stacks", [
                (lambda t: g.fs[:, t, 0:2 * D], f_hh, True),
                (lambda t: g.fs[:, t, 2 * D:4 * D], f_mm, True),
                (lambda t: g.fs[:, t, 4 * D:6 * D], f_hl, True)], BF16, g.ident_b[:])
        attention_scores(nc, g, f"{name}_att", theta)
        attention.close()
        g.end_stage()
        prune_edges(nc, g, f"{name}_prune", theta)

        kept_panels = panel_loads(nc, g, layer, f"{name}_kept_panel", g.kept_rows)
        kept_images = image_loads(nc, g, layer, f"{name}_kept_image", g.kept_images)
        with ExitStack() as ctx:
            floor = sbuf(nc, ctx, f"{name}_floor", [P, T], F32)
            root = sbuf(nc, ctx, f"{name}_root", [P, T], F32)
            floor_ready, root_ready = g.sem(f"{name}_floor_ready"), g.sem(f"{name}_root_ready")
            softmax = SoftmaxKeep(nc, g, ctx, f"{name}_node", g.logit[:], theta, g.node[:])
            with nc.Block() as block:
                @block.sync
                def _(sp):
                    for e in range(2):
                        sp.wait_ge(g.rows_kept[e], T // 2 * 16)
                    kept_panels.first()
                    for e in range(2):
                        sp.wait_ge(g.imgs_kept[e], T // 2 * 16)

                @block.vector
                def _(dve):
                    v, step = nc.vector, Chain(dve, g)
                    step(v.tensor_scalar(g.conn[:], g.conn[:], 1.0 / BYTE, None, ALU.mult))
                    step(v.tensor_tensor(g.logit[:], g.conn[:], g.norm[:], ALU.mult))
                    v.tensor_scalar(floor[:], g.conn[:], EDGE_EPS, None, ALU.max).then_inc(floor_ready, 1)
                    softmax.vector(dve, step)
                    step(v.tensor_scalar(g.logit[:], g.conn[:], 0.0, None, ALU.is_gt))
                    step(v.tensor_tensor(g.node[:], g.node[:], g.logit[:], ALU.mult))
                    step(v.tensor_tensor(g.node[:], g.node[:], g.keep[:], ALU.mult))
                    dve.wait_ge(root_ready, 1)
                    step(v.reciprocal(g.rsqrt[:], root[:]))
                    step(v.scalar_tensor_tensor(out=g.node[:], in0=g.node[:], scalar=g.scales[:, 0:1],
                                                in1=g.rsqrt[:], op0=ALU.mult, op1=ALU.mult))
                    step(v.tensor_scalar(g.rsqrt[:], g.rsqrt[:], INV, g.scales[:, 2:3], ALU.mult, ALU.mult))

                @block.tensor
                def _(pe):
                    softmax.tensor(pe)

                @block.scalar
                def _(act):
                    act.wait_ge(floor_ready, 1)
                    nc.scalar.activation(root[:], floor[:], ACT.Sqrt).then_inc(root_ready, 1)
                    softmax.scalar(act)

        with ExitStack() as ctx:
            g.ws = sbuf(nc, ctx, f"{name}_ws", [P, T, 2 * D], F16)
            Q4 = T // 4
            part = sbuf(nc, ctx, f"{name}_part", [P, Q4, D], F32)
            inv = sbuf(nc, ctx, f"{name}_inv2", [P, PT], F32)

            def prelude(dve, operand_ready):
                v, step = nc.vector, Chain(dve, g)
                for k in range(4):
                    t = slice(k * Q4, (k + 1) * Q4)
                    step(v.tensor_tensor(part[:], g.xqv[:, t, 0:D], per_node(g.node[:, t]), ALU.mult))
                    split2(v, step, g.operand[:, t, :], part[:], ready=operand_ready)
                    dve.wait_ge(operand_ready, k + 1)

            def post(step, tiles):
                v, a = nc.vector, g.prod[:, tiles, :]
                step(v.tensor_scalar(inv[:], g.logit[:, tiles], EDGE_EPS, None, ALU.max))
                step(v.reciprocal(inv[:], inv[:]))
                step(v.tensor_scalar(inv[:], inv[:], INV, None, ALU.mult))
                step(v.tensor_tensor(a, a, per_node(inv[:]), ALU.mult))
                split2(v, step, g.ws[:, tiles, :], a)

            row_product(nc, g, f"{name}_agg", kept_panels, g.operand, g.prod, prelude, post, 6, sums=g.logit,
                        prefetch=kept_images)
            image_product(nc, g, f"{name}_msg", kept_images, g.prod, g.ws, g.rsqrt)


def difference_layer(nc, g, images, prefetch):
    with ExitStack() as ctx:
        xs = sbuf(nc, ctx, "df_xs", [P, T, 2 * D], F16)
        highs_ready = g.sem("df_highs_ready")
        quarters = [slice(k * T // 4, (k + 1) * T // 4) for k in range(4)]

        def highs(act):
            for t in quarters:
                nc.scalar.activation(xs[:, t, 0:D], g.x[:, t, :], ACT.Copy, scale=X_SCALE).then_inc(highs_ready, 1)

        def prelude(dve, operand_ready):
            for k, t in enumerate(quarters):
                dve.wait_ge(highs_ready, k + 1)
                nc.vector.scalar_tensor_tensor(out=xs[:, t, D:2 * D], in0=g.x[:, t, :], scalar=X_SCALE,
                                               in1=xs[:, t, 0:D], op0=ALU.mult,
                                               op1=ALU.subtract).then_inc(operand_ready, 1)
        image_product(nc, g, "df_sum", images, g.prod, xs, g.sum_scale, plus=g.x, prelude=prelude,
                      highs=highs)
        linear(nc, g, "df_out", g.prod, D, g.w2[:], D, None, relu=True, ones_row=True, norm=True,
               prefetch=prefetch)


SUFFIX_TILES = T // 2
SUFFIX_PAIRS = 2
SUFFIX_LOADS = NB // SUFFIX_PAIRS


def suffix_loads(nc, g, ctx):
    view = g.images.rearrange("t c (l m) -> l c t m", m=SUFFIX_PAIRS * 256)

    def source(r, i, q=0):
        return view[bass.ds(r * -2 + (SUFFIX_LOADS - 1 - i), 1), :, q * SUFFIX_TILES:(q + 1) * SUFFIX_TILES, :] \
            .rearrange("l c t m -> (l c) t m")
    return Loads(nc, g, ctx, "sf_blk", [P, SUFFIX_TILES, SUFFIX_PAIRS * 256], U8, 2, source, next_stage=True)


def suffix_layer(nc, g, columns):
    QT, PAIRS, LOADS = SUFFIX_TILES, SUFFIX_PAIRS, SUFFIX_LOADS
    QUARTER = QT // 2
    BUF = 2
    R = LOADS // BUF
    S = 2 * PAIRS * BUF
    CLIP = BF16_STEP * (MAX_NEIGH - KEEP)
    with ExitStack() as ctx:
        xs = sbuf(nc, ctx, "sf_xs", [P, T, 2 * D], F16)
        scaled = sbuf(nc, ctx, "sf_scaled", [P, S, D], F32)
        clip = sbuf(nc, ctx, "sf_clip", [P, 1], F32)
        with ExitStack() as inner:
            blk, loaded = columns.buf, columns.loaded
            w = [sbuf(nc, inner, f"sf_w{i}", [P, QT * P], I16) for i in range(2)]
            cnt = [psum(nc, inner, f"sf_cnt{i}", [P, 1024], F32) for i in range(2)]
            out = psum(nc, inner, "sf_out", [P, QT, 2 * D], F32)
            cnt_ready, w_act, w_dve, blk_used, w_used, out_read, clip_ready, split_step, operand_ready = (
                g.sem(f"sf_{s}") for s in ("cnt_ready", "w_act", "w_dve", "blk_used", "w_used", "out_read",
                                           "clip_ready", "split_step", "operand_ready"))
            passes = T // QT
            with nc.Block() as block:
                @block.sync
                def _(sp):
                    for q in range(passes):
                        with sp.Fori(1 if q == 0 else 0, R) as r:
                            for i in range(BUF):
                                sp.wait_ge(blk_used, r * BUF + (q * LOADS + i + 1 - BUF))
                                nc.sync.dma_start(blk[i][:], columns.source(r, i, q)).then_inc(loaded[i], 16)

                @block.tensor
                def _(pe):
                    def add(i, pair, e, half, matrix, fresh=False):
                        for ch in range(2):
                            tt = half * QUARTER + ch * 4
                            cols = blk[i][:, tt:tt + 4, pair * 256 + e:pair * 256 + 256:2].bitcast(FP8)
                            last = nc.tensor.matmul(cnt[half][:, ch * 512:(ch + 1) * 512], g.count[:, matrix, :],
                                                    cols, start=fresh, stop=True, skip_group_check=True)
                        return last

                    def product(s, half, tile, opening=False):
                        rhs = xs[:, tile, :].rearrange("p t d -> p (t d)")
                        for i in range(half * QUARTER, (half + 1) * QUARTER):
                            last = nc.tensor.matmul(out[:, i, :], w[s % 2][:, i * P:(i + 1) * P].bitcast(BF16), rhs,
                                                    start=(opening and i % 4 == 0), stop=True,
                                                    skip_group_check=True)
                        return last

                    def where(s):
                        return s // (2 * PAIRS), PAIRS - 1 - s // 2 % PAIRS, 1 - s % 2

                    def finish(n0, s, tile, half, opening=False):
                        s %= S
                        i, pair, e = where(s)
                        pe.wait_ge(w_dve if half else w_act, n0)
                        g.carry(pe)
                        last = add(i, pair, e, half, 1)
                        if half and pair == 0 and e == 0:
                            last.then_inc(blk_used, 1)
                        last = product(s, half, tile, opening)
                        if half:
                            last.then_inc(w_used, 1)

                    def round_(q, r, first):
                        n0 = r * S + q * T
                        for s in range(S):
                            i, pair, e = where(s)
                            if s % (2 * PAIRS) == 0:
                                pe.wait_ge(loaded[i], (r + (q * R + 1)) * 16)
                                g.carry(pe)
                            if first and s == 1 and q:
                                pe.wait_ge(out_read, q)
                            if s == 1 and q == 0:
                                pe.wait_ge(operand_ready, r + 1)
                            for half in range(2):
                                if not (first and s == 0):
                                    finish_and_count(n0, s, i, pair, e, half, r, first)
                                else:
                                    add(i, pair, e, half, 0, fresh=True).then_inc(cnt_ready, 1)

                    def finish_and_count(n0, s, i, pair, e, half, r, first):
                        last_s = (s - 1) % S
                        pi, ppair, pe_ = where(last_s)
                        pe.wait_ge(w_dve if half else w_act, n0 + s)
                        g.carry(pe)
                        last = add(pi, ppair, pe_, half, 1)
                        if half and ppair == 0 and pe_ == 0:
                            last.then_inc(blk_used, 1)
                        add(i, pair, e, half, 0).then_inc(cnt_ready, 1)
                        last = product(last_s, half, bass.ds(r * (-S) + (T - s), 1), first and s == 1)
                        if half:
                            last.then_inc(w_used, 1)

                    for q in range(passes):
                        round_(q, 0, True)
                        with pe.Fori(1, R) as r:
                            round_(q, r, False)
                        for half in range(2):
                            finish((q + 1) * T, S - 1, slice(0, 1), half)

                @block.gpsimd
                def _(pool):
                    step = LoopChain(pool, split_step, 0)
                    for k in reversed(range(R)):
                        t = slice(k * S, (k + 1) * S)
                        step(nc.gpsimd.tensor_scalar(scaled[:], g.x[:, t, :], X_SCALE, None, ALU.mult))
                        step(nc.gpsimd.tensor_copy(xs[:, t, 0:D], scaled[:]))
                        nc.gpsimd.tensor_tensor(xs[:, t, D:2 * D], scaled[:], xs[:, t, 0:D],
                                                ALU.subtract).then_inc(operand_ready, 1)
                        pool.wait_ge(operand_ready, R - k)

                @block.scalar
                def _(act):
                    def weights(r, first=False):
                        for s in range(S):
                            act.wait_ge(cnt_ready, r * (2 * S) + (2 * s + 1))
                            if not (first and s < 2):
                                act.wait_ge(w_used, r * S + (s - 1))
                            nc.scalar.activation(w[s % 2][:, 0:QUARTER * P], cnt[0][:], ACT.Relu,
                                                 bias=clip[:]).then_inc(w_act, 1)
                    act.wait_ge(clip_ready, 1)
                    weights(0, True)
                    with act.Fori(1, passes * R) as r:
                        weights(r)

                @block.vector
                def _(dve):
                    def weights(n0, s, wait_used=True):
                        dve.wait_ge(cnt_ready, n0 * 2 + (2 * s + 2))
                        if wait_used:
                            dve.wait_ge(w_used, n0 + (s - 1))
                        nc.vector.tensor_scalar(w[s % 2][:, QUARTER * P:], cnt[1][:], CLIP, 0.0,
                                                ALU.add, ALU.max).then_inc(w_dve, 1)

                    nc.vector.memset(clip[:], CLIP).then_inc(clip_ready, 1)
                    for q in range(passes):
                        for s in range(S):
                            weights(q * T, s, wait_used=(q > 0 or s >= 2))
                        with dve.Fori(1, R) as r:
                            for s in range(S):
                                weights(r * S + q * T, s)
                        dve.wait_ge(w_used, (q + 1) * T)
                        nc.vector.tensor_reduce(g.prod[:, q * QT:(q + 1) * QT, :],
                                                out[:].rearrange("p t (s d) -> p t d s", s=2),
                                                AX.X, ALU.add).then_inc(out_read, 1)
        linear(nc, g, "sf_out_w", g.prod, D, g.w3[:], D, None, ones_row=True, norm=True)


class State:

    def __init__(self, nc, ctx):
        self.nc, self.held, self.held_on = nc, [], []
        self.carried = ctx.enter_context(nc.semaphore("carried"))
        self.vector_step, self.vector_steps = ctx.enter_context(nc.semaphore("vector_step")), 0

        def keep(name, shape, dt=F32):
            return sbuf(nc, ctx, name, shape, dt)
        self.x, self.prod, self.y = (keep(n, [P, T, D]) for n in ("x", "prod", "y"))
        self.operand = keep("operand", [P, T, 2 * D + 8], F16)
        self.scales = keep("scales", [P, 4])
        (self.deg, self.sum_scale, self.others, self.structural, self.norm, self.logit, self.keep, self.never,
         self.node, self.conn, self.rsqrt) = (
            keep(n, [P, T]) for n in ("deg", "sum_scale", "others", "structural", "norm", "logit", "keep",
                                      "never", "node", "conn", "rsqrt"))
        self.byte_one = keep("byte_one", [P, 1])
        self.ident_f = keep("ident_f", [P, P])
        self.ones = keep("ones", [P, P])
        self.ident_b = keep("ident_b", [P, P], BF16)
        self.ident_h = keep("ident_h", [P, P], F16)
        self.mask_off = keep("mask_off", [P, P], BF16)
        self.count = keep("count", [P, 2, P], BF16)
        self.w0_rows, self.w0 = keep("w0_rows", [D, 2 * D]), keep("w0", [2 * D, D])
        self.w_prep = keep("w_prep", [D + 1, 3 * D])
        self.theta = keep("theta", [D, D])
        self.w2, self.w3 = keep("w2", [D + 1, D]), keep("w3", [D + 1, D])
        self.rows, self.images, self.kept_rows, self.kept_images = (
            nc.dram_tensor(n, (T, P, N), U8, kind="Internal").ap()
            for n in ("rows", "images", "kept_rows", "kept_images"))

    def sem(self, name, next_stage=False):
        sem = self.nc.alloc_semaphore(name=name)
        (self.held_on if next_stage else self.held).append(sem)
        return sem

    def carry(self, eng):
        eng.sem_inc(self.carried, 1)

    def end_stage(self):
        with self.nc.Block() as block:
            @block.gpsimd
            def _(pool):
                self.nc.clear_and_free_semaphores(self.held)
        self.held, self.held_on = self.held_on, []


def store(nc, g, out):
    with ExitStack() as ctx:
        stored = g.sem("stored")
        with nc.Block() as block:
            @block.sync
            def _(sp):
                for h in (0, T // 2):
                    nc.sync.dma_start(out.rearrange("(t p) d -> p t d", p=P)[:, h:h + T // 2, :],
                                      g.x[:, h:h + T // 2, :]).then_inc(stored, 16)
                sp.wait_ge(stored, 32)


def program(nc, ins, out):
    with ExitStack() as ctx:
        g = State(nc, ctx)
        with ExitStack() as layer:
            adj = ins["adj"].rearrange("(t p) j -> t p j", p=P)
            tiles = Loads(nc, g, layer, "nb_raw", [P, N], F32, 4,
                          lambda r, i: adj[bass.ds(r * 4 + i, 1), :, :].rearrange("t p j -> (t p) j"))
            constants(nc, g, ins, prefetch=tiles)
            neighbour_layer(nc, g, tiles)
        g.end_stage()
        pruned_layer(nc, g, "l0", g.x, THETA0)
        linear(nc, g, "l0_theta", g.prod, D, g.theta[:], D, g.y, relu=True)
        g.end_stage()
        pruned_layer(nc, g, "l1", g.y, THETA0 + (1.0 - float(np.exp(-LAM))) * (THETA_MAX - THETA0))
        with ExitStack() as layer:
            columns = suffix_loads(nc, g, layer)
            images = image_loads(nc, g, layer, "df_image", g.images)
            linear(nc, g, "l1_theta", g.prod, D, g.theta[:], D, None, relu=True, norm=True, prefetch=images)
            difference_layer(nc, g, images, prefetch=columns)
            g.end_stage()
            suffix_layer(nc, g, columns)
        store(nc, g, out)


INPUTS = ["x", "adj", "L0_gnn_W", "L1_gnn_W", "L1_gnn_Theta", "L1_gnn_Wq", "L1_gnn_bq", "L1_gnn_Wv",
          "L1_gnn_bv", "L2_gnn_W", "L2_gnn_b", "L3_gnn_weight", "L3_gnn_bias"]


def kernel(**inputs):
    import concourse.bacc as bacc
    from concourse.bass_utils import run_bass_kernel_spmd

    nc = bacc.Bacc("TRN2", target_bir_lowering=False, num_devices=1)
    arrays, args = {}, {}
    for name in INPUTS:
        a = np.ascontiguousarray(inputs[name])
        arrays[f"in_{name}"] = a
        args[name] = nc.dram_tensor(f"in_{name}", a.shape, mybir.dt.from_np(a.dtype), kind="ExternalInput").ap()
    out = nc.dram_tensor("out", (N, D), F32, kind="ExternalOutput").ap()
    program(nc, args, out)
    return run_bass_kernel_spmd(nc, [arrays], core_ids=[0]).results[0]["out"]
```
